# Optimizing a Trainium2 kernel written in Bass

```python
import numpy as np
import jax
import jax.numpy as jnp

def _softmax(x, axis=-1):
    return jax.nn.softmax(x, axis=axis)

def _gelu(x):
    return jax.nn.gelu(x, approximate=True)

def _silu(x):
    return jax.nn.silu(x)

def _sigmoid(x):
    return jax.nn.sigmoid(x)

def _layernorm(x, axis=-1, eps=1e-05):
    m = jnp.mean(x, axis=axis, keepdims=True)
    v = jnp.var(x, axis=axis, keepdims=True)
    return (x - m) / jnp.sqrt(v + eps)

def _scatter_add(tgt, idx, src, axis=0):
    return tgt.at[idx].add(src)

def _segment_sum(src, seg, n):
    return jax.ops.segment_sum(src, seg, n)
kernel_name = 'mk_prb_d2_jaxref_r8_7ead97'

def setup_inputs(seed: int=0):
    np.random.seed(seed)
    _w = jnp.asarray

    def _L0_attn_setup():
        import jax, jax.numpy as jnp
        import numpy as np
        DIM = 128
        HEADS = 16
        HEAD_DIM = DIM // HEADS

        def _feature_map(z, W, b):
            p = jnp.einsum('bhtd,ed->bhte', z, W) + b
            return jnp.concatenate([jax.nn.softmax(p, axis=-1), jax.nn.softmax(-p, axis=-1)], axis=-1)
        key = jax.random.key(seed)
        ks = jax.random.split(key, 7)
        s = 0.02
        x = jax.random.normal(ks[0], (1, 128, DIM), dtype=jnp.float32)
        w_qkv = jax.random.normal(ks[1], (3 * DIM, DIM), dtype=jnp.float32) * s
        wq_map = jnp.eye(HEAD_DIM, dtype=jnp.float32) + jax.random.normal(ks[2], (HEAD_DIM, HEAD_DIM), dtype=jnp.float32) * s
        bq_map = jax.random.normal(ks[3], (HEAD_DIM,), dtype=jnp.float32) * s
        wk_map = jnp.eye(HEAD_DIM, dtype=jnp.float32) + jax.random.normal(ks[4], (HEAD_DIM, HEAD_DIM), dtype=jnp.float32) * s
        bk_map = jax.random.normal(ks[5], (HEAD_DIM,), dtype=jnp.float32) * s
        w_out = jax.random.normal(ks[6], (DIM, DIM), dtype=jnp.float32) * s
        return {'x': x, 'w_qkv': w_qkv, 'wq_map': wq_map, 'bq_map': bq_map, 'wk_map': wk_map, 'bk_map': bk_map, 'w_out': w_out}
    _L0_attn_in = _L0_attn_setup()

    def _L0_ffn_setup():
        import jax, jax.numpy as jnp
        import numpy as np
        D = 128
        H = 128
        E = 8
        K = 2
        I = 2 * 128
        ROUTE_SCALE = 1.0
        key = jax.random.key(seed)
        ks = jax.random.split(key, 12)
        s = lambda *sh: 1.0 / np.sqrt(sh[-1])
        return {'x': jax.random.normal(ks[0], (1, 256, D), jnp.float32), 'gate_w': jax.random.normal(ks[1], (E, D), jnp.float32) * s(E, D), 'w1': jax.random.normal(ks[2], (E, H, D), jnp.float32) * s(H, D), 'b1': jax.random.normal(ks[3], (E, H), jnp.float32) * 0.01, 'w2': jax.random.normal(ks[4], (E, D, H), jnp.float32) * s(D, H), 'b2': jax.random.normal(ks[5], (E, D), jnp.float32) * 0.01, 'w3': jax.random.normal(ks[6], (E, H, D), jnp.float32) * s(H, D), 'b3': jax.random.normal(ks[7], (E, H), jnp.float32) * 0.01, 'sw1': jax.random.normal(ks[8], (I, D), jnp.float32) * s(I, D), 'sw2': jax.random.normal(ks[9], (I, D), jnp.float32) * s(I, D), 'sw3': jax.random.normal(ks[10], (D, I), jnp.float32) * s(D, I)}
    _L0_ffn_in = _L0_ffn_setup()

    def _L1_attn_setup():
        import jax, jax.numpy as jnp
        import numpy as np
        DIMS = 128
        HEAD = 16
        HD = DIMS // HEAD
        CTX = 256
        B = 1

        def _ln(x, w, b, eps=1e-05):
            m = jnp.mean(x, axis=-1, keepdims=True)
            v = jnp.var(x, axis=-1, keepdims=True)
            return (x - m) * jax.lax.rsqrt(v + eps) * w + b

        def _rotary(x, xa, rh_w, rh_b):
            c = x.shape[2]
            d2 = x.shape[-1] // 2
            mel_max = 2595.0 * np.log10(1.0 + 4000.0 / 200.0)
            scale = jnp.power(10.0, jnp.linspace(0.0, mel_max, d2, dtype=jnp.float32) / 2595.0) - 1.0
            fb = 200.0 * scale / 1000.0
            freqs = jnp.arange(c, dtype=jnp.float32)[:, None] * fb[None, :]
            per_step = (xa @ rh_w + rh_b)[..., 0]
            radius = jnp.clip(per_step / 100.0, 0.5, 2.0)
            fr = radius[:, :, None] * jnp.cos(freqs)[None]
            fi = radius[:, :, None] * jnp.sin(freqs)[None]
            xr = x[..., 0::2]
            xi = x[..., 1::2]
            out_r = xr * fr[:, None] - xi * fi[:, None]
            out_i = xr * fi[:, None] + xi * fr[:, None]
            return jnp.stack([out_r, out_i], axis=-1).reshape(x.shape)
        key = jax.random.key(seed)
        ks = jax.random.split(key, 8)
        s = 0.02
        return {'x': jax.random.normal(ks[0], (B, CTX, DIMS), dtype=jnp.float32), 'qn_w': jnp.ones((DIMS,), jnp.float32), 'qn_b': jnp.zeros((DIMS,), jnp.float32), 'q_w': jax.random.normal(ks[1], (DIMS, DIMS), jnp.float32) * s, 'q_b': jnp.zeros((DIMS,), jnp.float32), 'kvn_w': jnp.ones((DIMS,), jnp.float32), 'kvn_b': jnp.zeros((DIMS,), jnp.float32), 'kv_w': jax.random.normal(ks[2], (DIMS, 2 * DIMS), jnp.float32) * s, 'kv_b': jnp.zeros((2 * DIMS,), jnp.float32), 'out_w': jax.random.normal(ks[3], (DIMS, DIMS), jnp.float32) * s, 'out_b': jnp.zeros((DIMS,), jnp.float32), 'ln_w': jnp.ones((HD,), jnp.float32), 'ln_b': jnp.zeros((HD,), jnp.float32), 'rh_w': jax.random.normal(ks[4], (DIMS, 1), jnp.float32) * s, 'rh_b': jnp.zeros((1,), jnp.float32)}
    _L1_attn_in = _L1_attn_setup()

    def _L1_ffn_setup():
        import jax, jax.numpy as jnp
        import numpy as np
        from math import ceil
        CAPACITY_FACTOR = 2.0
        MIN_CAPACITY = 4
        key = jax.random.key(seed)
        ks = jax.random.split(key, 4)
        B, S, D, Di, E = (4, 256, 128, 512, 8)
        x = jax.random.normal(ks[0], (B, S, D), dtype=jnp.float32)
        Wr = jax.random.normal(ks[1], (D, E), dtype=jnp.float32) * D ** (-0.5)
        W1 = jax.random.normal(ks[2], (E, D, Di), dtype=jnp.float32) * D ** (-0.5)
        b1 = jnp.zeros((E, Di), dtype=jnp.float32)
        W2 = jax.random.normal(ks[3], (E, Di, D), dtype=jnp.float32) * Di ** (-0.5)
        b2 = jnp.zeros((E, D), dtype=jnp.float32)
        return {'x': x, 'Wr': Wr, 'W1': W1, 'b1': b1, 'W2': W2, 'b2': b2}
    _L1_ffn_in = _L1_ffn_setup()
    _d = {'L0_attn_x': _L0_attn_in['x'], 'L0_attn_w_qkv': _L0_attn_in['w_qkv'], 'L0_attn_wq_map': _L0_attn_in['wq_map'], 'L0_attn_bq_map': _L0_attn_in['bq_map'], 'L0_attn_wk_map': _L0_attn_in['wk_map'], 'L0_attn_bk_map': _L0_attn_in['bk_map'], 'L0_attn_w_out': _L0_attn_in['w_out'], 'L0_ffn_gate_w': _L0_ffn_in['gate_w'], 'L0_ffn_w1': _L0_ffn_in['w1'], 'L0_ffn_b1': _L0_ffn_in['b1'], 'L0_ffn_w2': _L0_ffn_in['w2'], 'L0_ffn_b2': _L0_ffn_in['b2'], 'L0_ffn_w3': _L0_ffn_in['w3'], 'L0_ffn_b3': _L0_ffn_in['b3'], 'L0_ffn_sw1': _L0_ffn_in['sw1'], 'L0_ffn_sw2': _L0_ffn_in['sw2'], 'L0_ffn_sw3': _L0_ffn_in['sw3'], 'L1_attn_qn_w': _L1_attn_in['qn_w'], 'L1_attn_qn_b': _L1_attn_in['qn_b'], 'L1_attn_q_w': _L1_attn_in['q_w'], 'L1_attn_q_b': _L1_attn_in['q_b'], 'L1_attn_kvn_w': _L1_attn_in['kvn_w'], 'L1_attn_kvn_b': _L1_attn_in['kvn_b'], 'L1_attn_kv_w': _L1_attn_in['kv_w'], 'L1_attn_kv_b': _L1_attn_in['kv_b'], 'L1_attn_out_w': _L1_attn_in['out_w'], 'L1_attn_out_b': _L1_attn_in['out_b'], 'L1_attn_ln_w': _L1_attn_in['ln_w'], 'L1_attn_ln_b': _L1_attn_in['ln_b'], 'L1_attn_rh_w': _L1_attn_in['rh_w'], 'L1_attn_rh_b': _L1_attn_in['rh_b'], 'L1_ffn_Wr': _L1_ffn_in['Wr'], 'L1_ffn_W1': _L1_ffn_in['W1'], 'L1_ffn_b1': _L1_ffn_in['b1'], 'L1_ffn_W2': _L1_ffn_in['W2'], 'L1_ffn_b2': _L1_ffn_in['b2']}
    _x0 = _d['L0_attn_x']
    _d['L0_attn_x'] = jax.random.normal(jax.random.fold_in(jax.random.key(seed), 1), (4, 1024, 128), dtype=_x0.dtype)
    del _x0
    return _d

def reference(L0_attn_x, L0_attn_w_qkv, L0_attn_wq_map, L0_attn_bq_map, L0_attn_wk_map, L0_attn_bk_map, L0_attn_w_out, L0_ffn_gate_w, L0_ffn_w1, L0_ffn_b1, L0_ffn_w2, L0_ffn_b2, L0_ffn_w3, L0_ffn_b3, L0_ffn_sw1, L0_ffn_sw2, L0_ffn_sw3, L1_attn_qn_w, L1_attn_qn_b, L1_attn_q_w, L1_attn_q_b, L1_attn_kvn_w, L1_attn_kvn_b, L1_attn_kv_w, L1_attn_kv_b, L1_attn_out_w, L1_attn_out_b, L1_attn_ln_w, L1_attn_ln_b, L1_attn_rh_w, L1_attn_rh_b, L1_ffn_Wr, L1_ffn_W1, L1_ffn_b1, L1_ffn_W2, L1_ffn_b2):

    def _L0_attn_ref(x, w_qkv, wq_map, bq_map, wk_map, bk_map, w_out):
        import jax, jax.numpy as jnp
        import numpy as np
        DIM = 128
        HEADS = 16
        HEAD_DIM = DIM // HEADS

        def _feature_map(z, W, b):
            p = jnp.einsum('bhtd,ed->bhte', z, W) + b
            return jnp.concatenate([jax.nn.softmax(p, axis=-1), jax.nn.softmax(-p, axis=-1)], axis=-1)
        b, t, dim = x.shape
        h, hd = (HEADS, HEAD_DIM)
        qkv = (x @ w_qkv.T).reshape(b, t, 3, h, hd)
        q, k, v = [jnp.transpose(qkv[:, :, i], (0, 2, 1, 3)) for i in range(3)]
        q = _feature_map(q, wq_map, bq_map)
        k = _feature_map(k, wk_map, bk_map)
        k_prefix = jnp.cumsum(k, axis=2)
        kv_prefix = jnp.cumsum(jnp.einsum('bhtf,bhtd->bhtfd', k, v), axis=2)
        numer = jnp.einsum('bhtf,bhtfd->bhtd', q, kv_prefix)
        denom = jnp.maximum(jnp.einsum('bhtf,bhtf->bht', q, k_prefix)[..., None], 1e-06)
        y = jnp.transpose(numer / denom, (0, 2, 1, 3)).reshape(b, t, dim)
        return y @ w_out.T

    def _L0_ffn_ref(x, gate_w, w1, b1, w2, b2, w3, b3, sw1, sw2, sw3):
        import jax, jax.numpy as jnp
        import numpy as np
        D = 128
        H = 128
        E = 8
        K = 2
        I = 2 * 128
        ROUTE_SCALE = 1.0
        B, S, _ = x.shape
        xt = x.reshape(-1, D)
        logits = xt @ gate_w.T
        scores = jax.nn.softmax(logits.astype(jnp.float32), axis=-1)
        top_vals, idx = jax.lax.top_k(scores, K)
        weights = jnp.take_along_axis(scores, idx, axis=1).astype(x.dtype) * ROUTE_SCALE
        xs = xt[:, None, :] * weights[:, :, None]
        y = jnp.zeros_like(xt)
        for e in range(E):
            mask = (idx == e).astype(x.dtype)
            h = jax.nn.silu(jnp.einsum('tkd,hd->tkh', xs, w1[e]) + b1[e])
            x2 = jnp.einsum('tkh,dh->tkd', h, w2[e]) + b2[e]
            x3 = jnp.einsum('tkd,hd->tkh', xs, w3[e]) + b3[e]
            y = y + jnp.sum(x2 * x3 * mask[:, :, None], axis=1)
        z = jax.nn.silu(xt @ sw1.T) * (xt @ sw2.T) @ sw3.T
        return (y + z).reshape(B, S, D)

    def _L1_attn_ref(x, qn_w, qn_b, q_w, q_b, kvn_w, kvn_b, kv_w, kv_b, out_w, out_b, ln_w, ln_b, rh_w, rh_b):
        import jax, jax.numpy as jnp
        import numpy as np
        DIMS = 128
        HEAD = 16
        HD = DIMS // HEAD
        CTX = 256
        B = 1

        def _ln(x, w, b, eps=1e-05):
            m = jnp.mean(x, axis=-1, keepdims=True)
            v = jnp.var(x, axis=-1, keepdims=True)
            return (x - m) * jax.lax.rsqrt(v + eps) * w + b

        def _rotary(x, xa, rh_w, rh_b):
            c = x.shape[2]
            d2 = x.shape[-1] // 2
            mel_max = 2595.0 * np.log10(1.0 + 4000.0 / 200.0)
            scale = jnp.power(10.0, jnp.linspace(0.0, mel_max, d2, dtype=jnp.float32) / 2595.0) - 1.0
            fb = 200.0 * scale / 1000.0
            freqs = jnp.arange(c, dtype=jnp.float32)[:, None] * fb[None, :]
            per_step = (xa @ rh_w + rh_b)[..., 0]
            radius = jnp.clip(per_step / 100.0, 0.5, 2.0)
            fr = radius[:, :, None] * jnp.cos(freqs)[None]
            fi = radius[:, :, None] * jnp.sin(freqs)[None]
            xr = x[..., 0::2]
            xi = x[..., 1::2]
            out_r = xr * fr[:, None] - xi * fi[:, None]
            out_i = xr * fi[:, None] + xi * fr[:, None]
            return jnp.stack([out_r, out_i], axis=-1).reshape(x.shape)
        b, c, dims = x.shape
        kv = _ln(x, kvn_w, kvn_b) @ kv_w + kv_b
        kv = kv.reshape(b, c, 2, HEAD, HD).transpose(2, 0, 3, 1, 4)
        k, v = (kv[0], kv[1])
        q = (_ln(x, qn_w, qn_b) @ q_w + q_b).reshape(b, c, HEAD, HD).transpose(0, 2, 1, 3)
        q = _rotary(q, x, rh_w, rh_b)
        k = _rotary(k, x, rh_w, rh_b)
        qn = _ln(q, ln_w, ln_b)
        kn = _ln(k, ln_w, ln_b)
        scores = jnp.einsum('bhqd,bhkd->bhqk', qn, kn) / np.sqrt(HD).astype(np.float32)
        attn = jax.nn.softmax(scores, axis=-1)
        a = jnp.einsum('bhqk,bhkd->bhqd', attn, v)
        a = a.transpose(0, 2, 1, 3).reshape(b, c, dims)
        return a @ out_w + out_b

    def _L1_ffn_ref(x, Wr, W1, b1, W2, b2):
        import jax, jax.numpy as jnp
        import numpy as np
        from math import ceil
        CAPACITY_FACTOR = 2.0
        MIN_CAPACITY = 4
        B, S, D = x.shape
        E = Wr.shape[1]
        N = B * S
        k = max(MIN_CAPACITY, ceil(N * CAPACITY_FACTOR / E))
        xt = x.reshape(N, D)
        scores = jax.nn.softmax(xt @ Wr, axis=-1)
        G, idx = jax.lax.top_k(scores.T, k)
        X_in = xt[idx]
        h = jax.nn.gelu(jnp.einsum('ekd,edh->ekh', X_in, W1) + b1[:, None, :], approximate=False)
        X_e = jnp.einsum('ekh,ehd->ekd', h, W2) + b2[:, None, :]
        contrib = (G[..., None] * X_e).reshape(E * k, D)
        out = jnp.zeros((N, D), dtype=x.dtype).at[idx.reshape(-1)].add(contrib)
        return out.reshape(B, S, D)
    x = L0_attn_x
    xn = _layernorm(x, axis=-1)
    x = x + _L0_attn_ref(xn, L0_attn_w_qkv, L0_attn_wq_map, L0_attn_bq_map, L0_attn_wk_map, L0_attn_bk_map, L0_attn_w_out) + _L0_ffn_ref(xn, L0_ffn_gate_w, L0_ffn_w1, L0_ffn_b1, L0_ffn_w2, L0_ffn_b2, L0_ffn_w3, L0_ffn_b3, L0_ffn_sw1, L0_ffn_sw2, L0_ffn_sw3)
    xn = _layernorm(x, axis=-1)
    x = x + _L1_attn_ref(xn, L1_attn_qn_w, L1_attn_qn_b, L1_attn_q_w, L1_attn_q_b, L1_attn_kvn_w, L1_attn_kvn_b, L1_attn_kv_w, L1_attn_kv_b, L1_attn_out_w, L1_attn_out_b, L1_attn_ln_w, L1_attn_ln_b, L1_attn_rh_w, L1_attn_rh_b) + _L1_ffn_ref(xn, L1_ffn_Wr, L1_ffn_W1, L1_ffn_b1, L1_ffn_W2, L1_ffn_b2)
    return x

_drawn_inputs = setup_inputs


def setup_inputs(seed=0):
    import zlib

    import numpy as np

    out = dict(_drawn_inputs(seed))
    spreads = {'L1_attn_qn_w': (1.0, 0.6),
     'L1_attn_qn_b': (0.0, 0.8),
     'L1_attn_q_b': (0.0, 0.8),
     'L1_attn_kvn_w': (1.0, 0.6),
     'L1_attn_kvn_b': (0.0, 0.8),
     'L1_attn_kv_b': (0.0, 0.423),
     'L1_attn_out_b': (0.0, 0.1),
     'L1_attn_ln_w': (1.0, 0.6),
     'L1_attn_ln_b': (0.0, 0.8),
     'L1_ffn_b1': (0.0, 0.308),
     'L1_ffn_b2': (0.0, 0.316)}
    factors = {'L0_attn_w_qkv': 8.0,
     'L0_attn_wq_map': 8.0,
     'L0_attn_bq_map': 26.502,
     'L0_attn_wk_map': 8.0,
     'L0_attn_bk_map': 41.245,
     'L0_attn_w_out': 8.0,
     'L0_ffn_b1': 30.758,
     'L0_ffn_b2': 7.664,
     'L0_ffn_b3': 28.005,
     'L1_attn_q_w': 8.0,
     'L1_attn_kv_w': 8.0,
     'L1_attn_out_w': 3.18}
    for name, (base, spread) in spreads.items():
        noise = np.random.default_rng([zlib.crc32(name.encode()), seed]).standard_normal(out[name].shape)
        drawn = base * np.exp(spread * noise) if base else spread * noise
        out[name] = jnp.asarray(drawn.astype(out[name].dtype))
    for name, factor in factors.items():
        out[name] = (out[name] * factor).astype(out[name].dtype)
    return out
```

```python
from contextlib import ExitStack

import numpy as np

import concourse.bass as bass
from concourse import mybir

ALU = mybir.AluOpType
ACT = mybir.ActivationFunctionType
F32 = mybir.dt.float32
BF16 = mybir.dt.bfloat16
I32 = mybir.dt.int32
AX = mybir.AxisListType.X

P = 128
D = 128
BATCH, SEQ = 4, 1024
TOK = BATCH * SEQ
NT = TOK // P
U = 4
BLK = U * P
NB = TOK // BLK
TB = SEQ // P
H, HD = 16, 8
E = 8
HID0 = 128
ISH = 256
HID1 = 512
CH1 = HID1 // P
CAP = TOK * 2 // E
EPS = 1e-5
G = 4
NG = H // G
PARTS = 3
SR = PARTS * PARTS * HD
HALF_MAX = 512

CONST = {}
_w = 0
for _name, _n in (("ident", P), ("causal", P), ("blk8", P), ("rep8", P), ("same_e", P), ("before_e", P),
                  ("kvmask", 72), ("parity", 2), ("tri", E * E), ("keep", NT), ("cos", TB * 4), ("sin", TB * 4)):
    CONST[_name] = (_w, _w + _n)
    _w += _n
NCONST = _w


def constants():
    c = np.zeros((P, NCONST), np.float32)
    p = np.arange(P)

    def put(name, a):
        lo, hi = CONST[name]
        c[: a.shape[0], lo:hi] = a

    put("ident", np.eye(P))
    put("causal", p[:, None] <= p[None, :])
    put("blk8", p[:, None] // HD == p[None, :] // HD)
    put("rep8", np.arange(HD)[:, None] == p[None, :] % HD)
    put("same_e", p[:, None] % E == p[None, :] % E)
    put("before_e", (p[:, None] % E == p[None, :] % E) & (p[:, None] // E < p[None, :] // E))
    put("kvmask", p[:, None] // 16 == np.arange(72)[None, :] // 9)
    put("parity", (p[:, None] // 16) % 2 == np.arange(2)[None, :])
    e = np.arange(E)
    put("tri", np.broadcast_to((e[None, :] < e[:, None]).reshape(1, -1), (P, E * E)))
    put("keep", np.broadcast_to((np.arange(1, NT + 1) % TB != 0)[None, :], (P, NT)))
    d2 = HD // 2
    mel_max = 2595.0 * np.log10(1.0 + 4000.0 / 200.0)
    lin = np.linspace(0.0, mel_max, d2, dtype=np.float32)
    scale = np.power(np.float32(10.0), lin / np.float32(2595.0)).astype(np.float32) - np.float32(1.0)
    fb = (np.float32(200.0) * scale / np.float32(1000.0)).astype(np.float32)
    fr = np.arange(SEQ, dtype=np.float32)[:, None] * fb[None, :]
    lay = lambda a: a.reshape(TB, P, d2).transpose(1, 0, 2).reshape(P, TB * d2)
    put("cos", lay(np.cos(fr)))
    put("sin", lay(np.sin(fr)))
    return c


class Steps:

    def __init__(self, eng, sem):
        self.eng, self.sem, self.base, self.n = eng, sem, 0, 0

    def __call__(self, ins):
        self.mark(ins)
        self.eng.wait_ge(self.sem, self.base + self.n)

    def mark(self, ins):
        self.n += 1
        ins.then_inc(self.sem, 1)

    def loop(self, it, per):
        self.start, self.per = self.base + self.n, per
        self.base, self.n = it * per + self.start, 0

    def end(self, count):
        assert self.n == self.per, (self.n, self.per)
        self.base, self.n = self.start + count * self.per, 0


def tiles_of(big, it, n=U):
    return big[:, bass.ds(it * n, n)]


class Kernel:

    def __init__(self, nc, ctx, io):
        self.nc, self.ctx, self.io = nc, ctx, io
        self.x = self.sb(ctx, "x_res", [P, NT, D])
        self.xnT = self.sb(ctx, "xnT", [P, TOK])
        self.cst = self.sb(ctx, "cst", [P, NCONST])
        self.eps = self.sb(ctx, "eps", [P, 1])

    def sb(self, ctx, name, shape, dt=F32):
        return ctx.enter_context(self.nc.sbuf_tensor(name, shape, dt))

    def ps(self, ctx, name, shape, dt=F32):
        return ctx.enter_context(self.nc.psum_tensor(name, shape, dt))

    def sem(self, name):
        return self.ctx.enter_context(self.nc.semaphore(name))

    def const(self, name, rows=P):
        lo, hi = CONST[name]
        return self.cst[0:rows, lo:hi]


def rows_of(vec, n):
    return vec.partition_broadcast(n)


def phase_weights0(k, w):
    nc, io = k.nc, k.io
    with ExitStack() as ctx:
        wqkv = k.sb(ctx, "wqkv_nat", [P, 3, D])
        maps = k.sb(ctx, "maps_nat", [HD, 2, HD])
        wexp = k.sb(ctx, "wexp_nat", [P, 3 * E, D])
        wsh = k.sb(ctx, "wsh_nat", [P, 6, D])
        wo = k.sb(ctx, "wo_nat", [P, D])
        small = k.sb(ctx, "small_nat", [32, D])
        bd = k.sb(ctx, "bd", [P, 2, D])
        pst = k.ps(ctx, "ps_w0", [P, 8, 512])
        loaded, tr_done, copied, bd_done = (k.sem(n) for n in ("w0_loaded", "w0_tr", "w0_copied", "w0_bd"))
        xl = k.x_loaded
        block = ctx.enter_context(nc.Block("weights0"))

        groups = [([wexp[:, 4 * j + i, :] for i in range(4)], w.expT[:, 4 * j:4 * j + 4, :]) for j in range(6)]
        groups.append(([wsh[:, i, :] for i in range(4)], w.shT[:, 0:4, :]))
        groups.append(([wsh[:, 4, :], wsh[:, 5, :], wo[:], wqkv[:, 2, :]], None))

        @block.sync
        def _(sp):
            sp.dma_start(k.cst[:], io["consts"]).then_inc(loaded, 16)
            sp.dma_start(wqkv[:], io["L0_attn_w_qkv"].rearrange("(t p) d -> p t d", p=P)).then_inc(loaded, 16)
            for i, n in enumerate(("L0_attn_wq_map", "L0_attn_wk_map")):
                with nc.allow_non_contiguous_dma("eight by eight"):
                    sp.dma_start(maps[:, i, :], io[n].rearrange("e d -> d e")).then_inc(loaded, 16)
            for i, n in enumerate(("L0_attn_bq_map", "L0_attn_bk_map")):
                sp.dma_start(w.map_bias[:, i, :], rows_of(io[n], P)).then_inc(loaded, 16)
            for i, n in enumerate(("L0_ffn_w1", "L0_ffn_w2", "L0_ffn_w3")):
                sp.dma_start(wexp[:, i * E:(i + 1) * E, :], io[n].rearrange("e h d -> h e d")).then_inc(loaded, 16)
            for i, n in enumerate(("L0_ffn_sw1", "L0_ffn_sw2")):
                sp.dma_start(wsh[:, 2 * i:2 * i + 2, :], io[n].rearrange("(c p) d -> p c d", p=P)).then_inc(loaded, 16)
            sp.dma_start(wsh[:, 4:6, :], io["L0_ffn_sw3"].rearrange("d (c p) -> d c p", p=P)).then_inc(loaded, 16)
            sp.dma_start(wo[:], io["L0_attn_w_out"]).then_inc(loaded, 16)
            for i, n in enumerate(("L0_ffn_b1", "L0_ffn_b2", "L0_ffn_b3", "L0_ffn_gate_w")):
                sp.dma_start(small[i * E:(i + 1) * E, :], io[n]).then_inc(loaded, 16)

        @block.scalar
        def _(act):
            xd = io["L0_attn_x"].rearrange("b (t p) d -> p (b t) d", p=P)
            for b in range(NB):
                act.dma_start(k.x[:, U * b:U * b + U, :], xd[:, U * b:U * b + U, :]).then_inc(xl[b], 16)

        n_loads = 17

        @block.tensor
        def _(pe):
            pe.wait_ge(loaded, 16 * n_loads)
            ident = k.const("ident")
            for g, (srcs, _) in enumerate(groups):
                for i, s in enumerate(srcs):
                    last = nc.tensor.transpose(pst[:, g, i * P:(i + 1) * P], s, ident)
                last.then_inc(tr_done, 1)
            pe.wait_ge(copied, 1)
            nc.tensor.transpose(pst[:, 0, 0:32], small[:], ident[0:32, 0:32])
            for i in range(2):
                last = nc.tensor.matmul(pst[:, 0, 64 + 8 * i:72 + 8 * i], k.const("rep8", HD), maps[:, i, :],
                                        start=True, stop=True)
            last.then_inc(tr_done, 1)
            pe.wait_ge(bd_done, 1)
            for i in range(2):
                last = nc.tensor.matmul(pst[:, 1, i * P:(i + 1) * P], wqkv[:, i, :], bd[:, i, :], start=True, stop=True)
            last.then_inc(tr_done, 1)

        @block.vector
        def _(dve):
            nc.vector.memset(k.eps[:], EPS)
            nc.vector.memset(w.v1[:, :, :, HD:HD + 1], 1.0)
            for g, (_, dst) in enumerate(groups):
                dve.wait_ge(tr_done, g + 1)
                if dst is not None:
                    nc.vector.tensor_copy(dst.rearrange("p a b -> p (a b)"), pst[:, g, :]).then_inc(copied, 1)
                else:
                    nc.vector.tensor_copy(w.shT[:, 4:6, :].rearrange("p a b -> p (a b)"), pst[:, g, 0:256])
                    nc.vector.tensor_copy(w.outT[:], pst[:, g, 256:384])
                    nc.vector.tensor_copy(w.proj[:, 256:384], pst[:, g, 384:512])
            dve.wait_ge(tr_done, len(groups) + 1)
            nc.vector.tensor_copy(w.bias[:], pst[:, 0, 0:24])
            nc.vector.tensor_copy(w.proj[:, 384:392], pst[:, 0, 24:32])
            for i in range(2):
                blk = k.const("blk8").rearrange("p (h e) -> p h e", e=HD)
                rep = pst[:, 0, 64 + 8 * i:72 + 8 * i].unsqueeze(1).broadcast_to([P, H, HD])
                ins = nc.vector.tensor_tensor(bd[:, i, :].rearrange("p (h e) -> p h e", e=HD), rep, blk, ALU.mult)
            ins.then_inc(bd_done, 1)
            dve.wait_ge(tr_done, len(groups) + 2)
            nc.vector.tensor_copy(w.proj[:, 0:256], pst[:, 1, 0:256])


def phase_project0(k, w):
    nc = k.nc
    with ExitStack() as ctx:
        st = k.sb(ctx, "p0_st", [P, U, 6])
        mv = k.sb(ctx, "p0_mv", [P, U, 2])
        pause = k.sb(ctx, "p0_pause", [P, 2])
        sd = k.sb(ctx, "p0_sd", [P, U])
        rs = k.sb(ctx, "p0_rs", [P, U])
        xn = k.sb(ctx, "p0_xn", [P, U, D])
        xt = k.sb(ctx, "p0_xt", [P, BLK])
        ps_t = k.ps(ctx, "ps_p0t", [P, 512])
        ps_q = k.ps(ctx, "ps_p0q", [P, U, 512])
        chain = k.sem("p0_chain")
        stats, std, normed, turned, xt_ready, xt_kept, proj, qk_kept, v_kept = (
            k.sem("p0_" + n) for n in ("stats", "std", "normed", "turned", "xt_ready", "xt_kept", "proj", "qk", "v"))
        block = ctx.enter_context(nc.Block("project0"))

        @block.vector
        def _(dve):
            step = Steps(dve, chain)
            for b in range(NB):
                dve.wait_ge(k.x_loaded[b], 16)
            with dve.Fori(0, NB) as it:
                step.loop(it, 2)
                for u in range(U):
                    nc.vector.bn_stats(st[:, u, :], k.x[:, bass.ds(it * U + u, 1), :].rearrange("p a d -> p (a d)"))
                step(nc.vector.memset(pause[:, 0:1], 0.0))
                nc.vector.memset(pause[:, 1:2], 0.0)
                for u in range(U):
                    last = nc.vector.bn_aggr(mv[:, u, :], st[:, u, :])
                last.then_inc(stats, 1)
                dve.wait_ge(std, it + 1)
                step(nc.vector.reciprocal(rs[:], sd[:]))
                dve.wait_ge(turned, it * 1 + 1)
                for u in range(U):
                    last = nc.vector.tensor_scalar(xn[:, u, :], k.x[:, bass.ds(it * U + u, 1), :].rearrange("p a d -> p (a d)"),
                                                   mv[:, u, 0:1], rs[:, u:u + 1], ALU.subtract, ALU.mult)
                last.then_inc(normed, 1)
                dve.wait_ge(proj, it + 1)
                for u in range(U):
                    for i in range(2):
                        last = nc.vector.tensor_tensor(
                            w.qk[:, bass.ds(it * U + u, 1), i * P:(i + 1) * P].rearrange("p a (h e) -> p (a h) e", e=HD),
                            ps_q[:, u, i * P:(i + 1) * P].rearrange("p (h e) -> p h e", e=HD),
                            w.map_bias[:, i, :].unsqueeze(1).broadcast_to([P, H, HD]), ALU.add)
                last.then_inc(qk_kept, 1)
                nc.vector.tensor_copy(k.xnT[:, bass.ds(it * BLK, BLK)], xt[:]).then_inc(xt_kept, 1)

        @block.scalar
        def _(act):
            with act.Fori(0, NB) as it:
                act.wait_ge(stats, it + 1)
                nc.scalar.activation(sd[:], mv[:, :, 1], ACT.Sqrt, bias=k.eps[:]).then_inc(std, 1)
                act.wait_ge(turned, it + 2)
                act.wait_ge(xt_kept, it + 1)
                nc.scalar.activation(xt[:], ps_t[:], ACT.Copy).then_inc(xt_ready, 1)
                act.wait_ge(qk_kept, it + 1)
                nc.scalar.activation(w.v1[:, bass.ds(it * U, U), :, 0:HD].rearrange("p a h e -> p a h e"),
                                     ps_q[:, :, 256:384].rearrange("p a (h e) -> p a h e", e=HD), ACT.Copy)
                nc.scalar.activation(w.logits[:, bass.ds(it * U, U), :], ps_q[:, :, 384:392], ACT.Copy).then_inc(v_kept, 1)

        @block.tensor
        def _(pe):
            pe.sem_inc(turned, 1)
            with pe.Fori(0, NB) as it:
                pe.wait_ge(normed, it + 1)
                pe.wait_ge(xt_ready, it + 1)
                for u in range(U):
                    last = nc.tensor.transpose(ps_t[:, u * P:(u + 1) * P], xn[:, u, :], k.const("ident"))
                last.then_inc(turned, 1)
                pe.wait_ge(xt_ready, it + 2)
                pe.wait_ge(v_kept, it + 1)
                for u in range(U):
                    last = nc.tensor.matmul(ps_q[:, u, 0:392], xt[:, u * P:(u + 1) * P], w.proj[:], start=True, stop=True)
                last.then_inc(proj, 1)

        @block.gpsimd
        def _(pool):
            pool.sem_inc(xt_ready, 1)
            pool.sem_inc(xt_kept, 1)
            pool.sem_inc(v_kept, 1)


def phase_linear_attention(k, w):
    nc = k.nc
    with ExitStack() as ctx:
        S2 = range(2)
        mm = [k.sb(ctx, f"la_mm{s}", [P, 2, 32]) for s in S2]
        dd = [k.sb(ctx, f"la_dd{s}", [P, 32, 2, HD]) for s in S2]
        ee = [k.sb(ctx, f"la_ee{s}", [P, 64, HD]) for s in S2]
        sm = [k.sb(ctx, f"la_sm{s}", [P, 2, 64]) for s in S2]
        ff = [k.sb(ctx, f"la_ff{s}", [P, 64, HD]) for s in S2]
        vs = [k.sb(ctx, f"la_vs{s}", [P, H, HD + 1]) for s in S2]
        qT = [k.sb(ctx, f"la_qT{s}", [P, 256]) for s in S2]
        kT = [k.sb(ctx, f"la_kT{s}", [P, 2, 256]) for s in S2]
        am = [k.sb(ctx, f"la_am{s}", [P, 4, 4, P]) for s in S2]
        run = [k.sb(ctx, f"la_run{s}", [P, NG, G, 32]) for s in S2]
        add = k.sb(ctx, "la_add", [P, 2, 72])
        oT = [k.sb(ctx, f"la_oT{s}", [P, 512]) for s in S2]
        den = [k.sb(ctx, f"la_den{s}", [P, 2, H]) for s in S2]
        y = [k.sb(ctx, f"la_y{s}", [P, D]) for s in S2]
        yT = [k.sb(ctx, f"la_yT{s}", [P, D]) for s in S2]
        p_ft = k.ps(ctx, "ps_ft", [P, 512])
        p_a = k.ps(ctx, "ps_a", [P, 4, 512])
        p_o = k.ps(ctx, "ps_o", [P, 512])
        p_ds = k.ps(ctx, "ps_ds", [P, 512])
        p_y = k.ps(ctx, "ps_y", [P, 512])
        names = ("mm", "dd", "ee", "ff", "vs", "ft", "ds", "kt", "a", "am", "o", "ot", "otT", "run", "y", "yt", "yts", "pr", "x", "chain")
        s = {n: k.sem("la_" + n) for n in names}
        block = ctx.enter_context(nc.Block("linear_attention"))

        def loops(eng, body, ahead=None):
            if ahead:
                ahead(0, 0)
            with eng.Fori(0, NT // 2 - 1) as it:
                for u in S2:
                    body(it * 2 + u, u, it, True)
            for u in S2:
                body(NT - 2 + u, u, NT // 2 - 1, u == 0)

        @block.vector
        def _(dve):
            step = Steps(dve, s["chain"])
            for u in S2:
                step(nc.vector.memset(run[u][:], 0.0))
            dve.sem_inc(s["run"], 1)

            def maxima(t, u):
                src = w.qk[:, bass.ds(t, 1), :].rearrange("p a (g e) -> p (a g) e", e=HD)
                dve.wait_ge(s["dd"], t + 1)
                nc.vector.tensor_reduce(mm[u][:, 0, :], src, axis=AX, op=ALU.max)
                nc.vector.tensor_reduce(mm[u][:, 1, :], src, axis=AX, op=ALU.min).then_inc(s["mm"], 1)

            def body(t, u, it, more):
                dve.wait_ge(s["ee"], t + 1)
                stp(nc.vector.tensor_reduce(sm[u][:, 0, :], ee[u][:], axis=AX, op=ALU.add), t, 0)
                stp(nc.vector.reciprocal(sm[u][:, 1, :], sm[u][:, 0, :]), t, 1)
                nc.vector.tensor_tensor(ff[u][:], ee[u][:], sm[u][:, 1, :].unsqueeze(2).broadcast_to([P, 64, HD]),
                                        ALU.mult).then_inc(s["ff"], 1)
                if more:
                    maxima(t + 1, 1 - u)
                for b in range(4):
                    dve.wait_ge(s["a"], t * 4 + b + 1)
                    nc.vector.tensor_tensor(am[u][:, b], p_a[:, b, :].rearrange("p (a t) -> p a t", a=4),
                                            k.const("causal").unsqueeze(1).broadcast_to([P, 4, P]),
                                            ALU.mult).then_inc(s["am"], 1)
                dve.wait_ge(s["ds"], t + 1)
                keep = w_keep(t)
                stp(nc.vector.scalar_tensor_tensor(out=add[:], in0=p_ds[:, 0:144].rearrange("p (a c) -> p a c", a=2),
                                                   scalar=keep, in1=k.const("kvmask").unsqueeze(1).broadcast_to([P, 2, 72]),
                                                   op0=ALU.mult, op1=ALU.mult), t, 2)
                addv = add[:].rearrange("p a (j c) -> p (a j) c", c=HD + 1)
                nc.vector.scalar_tensor_tensor(
                    out=run[1 - u][:].rearrange("p g j c -> p (g j) c")[:, :, 0:HD + 1],
                    in0=run[u][:].rearrange("p g j c -> p (g j) c")[:, :, 0:HD + 1], scalar=keep,
                    in1=addv, op0=ALU.mult, op1=ALU.add).then_inc(s["run"], 1)
                dve.wait_ge(s["otT"], t + 1)
                o = p_y[:].rearrange("p (h c) -> p h c", c=32)
                stp(nc.vector.tensor_scalar(den[u][:, 0, :], o[:, :, HD], 1e-6, None, ALU.max), t, 3)
                stp(nc.vector.reciprocal(den[u][:, 1, :], den[u][:, 0, :]), t, 4)
                nc.vector.tensor_tensor(y[u][:].rearrange("p (h c) -> p h c", c=HD), o[:, :, 0:HD],
                                        den[u][:, 1, :].unsqueeze(2).broadcast_to([P, H, HD]), ALU.mult).then_inc(s["y"], 1)
                dve.wait_ge(s["pr"], t + 1)
                xt = k.x[:, bass.ds(t, 1), :].rearrange("p a d -> p (a d)")
                nc.vector.tensor_tensor(xt, xt, p_ds[:, 256:384], ALU.add).then_inc(s["x"], 1)

            def w_keep(t):
                lo = CONST["keep"][0]
                return k.cst[:, bass.ds(t + lo, 1)]

            def stp(ins, t, n):
                ins.then_inc(s["chain"], 1)
                dve.wait_ge(s["chain"], t * 5 + (2 + n + 1))

            loops(dve, body, maxima)

        @block.gpsimd
        def _(pool):
            pool.sem_inc(s["dd"], 2)

            def body(t, u, it, more):
                src = w.qk[:, bass.ds(t, 1), :].rearrange("p a (g e) -> p (a g) e", e=HD)
                pool.wait_ge(s["mm"], t + 1)
                nc.gpsimd.tensor_tensor(dd[u][:, :, 0, :], src, mm[u][:, 0, :].unsqueeze(2).broadcast_to([P, 32, HD]), ALU.subtract)
                nc.gpsimd.tensor_tensor(dd[u][:, :, 1, :], mm[u][:, 1, :].unsqueeze(2).broadcast_to([P, 32, HD]), src,
                                        ALU.subtract).then_inc(s["dd"], 1)
                pool.wait_ge(s["o"], t + 1)
                nc.gpsimd.tensor_copy(vs[u][:], w.v1[:, bass.ds(t, 1)].rearrange("p a h c -> p (a h) c")).then_inc(s["vs"], 1)

            loops(pool, body)

        @block.scalar
        def _(act):
            def body(t, u, it, more):
                act.wait_ge(s["dd"], t + 3)
                act.wait_ge(s["ff"], t + 1)
                nc.scalar.activation(ee[u][:], dd[u][:].rearrange("p g a e -> p (g a) e"), ACT.Exp).then_inc(s["ee"], 1)
                act.wait_ge(s["ft"], t + 1)
                nc.scalar.activation(qT[u][:], p_ft[:, 0:256], ACT.Copy)
                par = k.const("parity")
                for i in range(2):
                    last = nc.scalar.activation(kT[u][:, i, :], p_ft[:, 256:512], ACT.Copy, scale=par[:, i:i + 1])
                last.then_inc(s["kt"], 1)
                act.wait_ge(s["o"], t + 3)
                nc.scalar.activation(oT[u][:], p_o[:], ACT.Copy).then_inc(s["ot"], 1)
                act.wait_ge(s["yt"], t + 1)
                nc.scalar.activation(yT[u][:], p_ds[:, 384:512], ACT.Copy).then_inc(s["yts"], 1)

            loops(act, body)

        @block.tensor
        def _(pe):
            pe.sem_inc(s["o"], 2)
            ident = k.const("ident")

            def body(t, u, it, more):
                pe.wait_ge(s["ff"], t + 3)
                pe.wait_ge(s["kt"], t + 1)
                for i in range(4):
                    last = nc.tensor.transpose(p_ft[:, i * P:(i + 1) * P],
                                               ff[u][:, 16 * i:16 * i + 16, :].rearrange("p g e -> p (g e)"), ident)
                last.then_inc(s["ft"], 1)
                pe.wait_ge(s["vs"], t + 1)
                pe.wait_ge(s["x"], t + 1)
                for i in range(2):
                    last = nc.tensor.matmul(p_ds[:, 72 * i:72 * i + 72],
                                            ff[u][:, 32 + 16 * i:48 + 16 * i, :].rearrange("p g e -> p (g e)"),
                                            vs[u][:, 8 * i:8 * i + 8, :].rearrange("p h c -> p (h c)"), start=True, stop=True)
                last.then_inc(s["ds"], 1)
                pe.wait_ge(s["kt"], t + 2)
                for b in range(4):
                    pe.wait_ge(s["am"], t * 4 + b + 1)
                    for half in range(2):
                        for par in range(2):
                            i = half * 2 + par
                            last = nc.tensor.matmul(p_a[:, b, i * P:(i + 1) * P],
                                                    kT[u][32 * b:32 * b + 32, par, half * P:half * P + P],
                                                    qT[u][32 * b:32 * b + 32, half * P:half * P + P],
                                                    start=True, stop=True, tile_position=(32 * b, 0))
                    last.then_inc(s["a"], 1)
                pe.wait_ge(s["run"], t + 1)
                pe.wait_ge(s["ot"], t + 1)
                for g in range(NG):
                    nc.tensor.matmul(p_o[:, g * P:(g + 1) * P], run[u][:, g].rearrange("p j c -> p (j c)"),
                                     qT[u][:, (g // 2) * P:(g // 2) * P + P], start=(g == 0), stop=False, skip_group_check=True)
                pe.wait_ge(s["am"], t * 4 + 8)
                for g in range(NG):
                    for j in range(G):
                        h = g * G + j
                        last = nc.tensor.matmul(p_o[32 * j:32 * j + HD + 1, g * P:(g + 1) * P], vs[u][:, h, :],
                                                am[u][:, (h % 8) // 2, (h // 8) * 2 + h % 2, :], start=False,
                                                stop=(g == NG - 1), skip_group_check=True, tile_position=(0, 32 * j))
                last.then_inc(s["o"], 1)
                pe.wait_ge(s["ot"], t + 2)
                pe.wait_ge(s["y"], t + 1)
                for g in range(NG):
                    last = nc.tensor.transpose(p_y[:, g * P:(g + 1) * P], oT[u][:, g * P:(g + 1) * P], ident)
                last.then_inc(s["otT"], 1)
                pe.wait_ge(s["y"], t + 2)
                nc.tensor.transpose(p_ds[:, 384:512], y[u][:], ident).then_inc(s["yt"], 1)
                pe.wait_ge(s["yts"], t + 1)
                nc.tensor.matmul(p_ds[:, 256:384], yT[u][:], w.outT[:], start=True, stop=True).then_inc(s["pr"], 1)

            loops(pe, body)

        @block.sync
        def _(sp):
            for n, c in (("ff", 2), ("kt", 1), ("x", 1), ("am", 4), ("ot", 1), ("y", 1)):
                sp.sem_inc(s[n], c)


def phase_ffn0(k, w):
    nc, io = k.nc, k.io
    with ExitStack() as ctx:
        sc = k.sb(ctx, "f0_sc", [P, NT, E])
        r1 = k.sb(ctx, "f0_r1", [P, NT])
        gt = k.sb(ctx, "f0_gt", [P, NT, E, E])
        eq = k.sb(ctx, "f0_eq", [P, NT, E, E])
        rank = k.sb(ctx, "f0_rank", [P, NT, E])
        gT = k.sb(ctx, "f0_gT", [P, 2, P])
        p_g = k.ps(ctx, "ps_f0g", [P, 512])
        s = {n: k.sem("f0_" + n) for n in ("chain", "lg", "ex", "g", "gt", "gts", "gd")}
        with nc.Block("route0") as block:
            @block.vector
            def _(dve):
                step = Steps(dve, s["chain"])
                lg = w.logits
                wide = lambda a: a[:].unsqueeze(2).broadcast_to([P, NT, E])
                step(nc.vector.tensor_reduce(r1[:], lg[:], axis=AX, op=ALU.max))
                nc.vector.tensor_tensor(lg[:], lg[:], wide(r1), ALU.subtract).then_inc(s["lg"], 1)
                dve.wait_ge(s["ex"], 1)
                step(nc.vector.tensor_reduce(r1[:], sc[:], axis=AX, op=ALU.add))
                step(nc.vector.reciprocal(r1[:], r1[:]))
                step(nc.vector.tensor_tensor(sc[:], sc[:], wide(r1), ALU.mult))
                of_j = sc[:].unsqueeze(2).broadcast_to([P, NT, E, E])
                of_e = sc[:].unsqueeze(3).broadcast_to([P, NT, E, E])
                nc.vector.tensor_tensor(gt[:], of_j, of_e, ALU.is_gt)
                step(nc.vector.tensor_tensor(eq[:], of_j, of_e, ALU.is_equal))
                flat = lambda a: a[:].rearrange("p t e j -> p t (e j)")
                step(nc.vector.tensor_tensor(flat(eq), flat(eq), k.const("tri").unsqueeze(1).broadcast_to([P, NT, E * E]), ALU.mult))
                step(nc.vector.tensor_tensor(flat(gt), flat(gt), flat(eq), ALU.add))
                step(nc.vector.tensor_reduce(rank[:], gt[:], axis=AX, op=ALU.add))
                step(nc.vector.tensor_scalar(rank[:], rank[:], 2.0, None, ALU.is_lt))
                step(nc.vector.tensor_tensor(sc[:], sc[:], rank[:], ALU.mult))
                step(nc.vector.tensor_scalar(rank[:], rank[:], -1.0, None, ALU.add))
                nc.vector.tensor_tensor(sc[:], sc[:], rank[:], ALU.add).then_inc(s["g"], 1)

            @block.scalar
            def _(act):
                act.wait_ge(s["lg"], 1)
                nc.scalar.activation(sc[:], w.logits[:], ACT.Exp).then_inc(s["ex"], 1)
                act.wait_ge(s["gt"], 1)
                nc.scalar.activation(gT[:].rearrange("p a t -> p (a t)"), p_g[:, 0:256], ACT.Copy).then_inc(s["gts"], 1)

            @block.tensor
            def _(pe):
                pe.wait_ge(s["g"], 1)
                for i in range(2):
                    last = nc.tensor.transpose(p_g[:, i * P:(i + 1) * P],
                                               sc[:, 16 * i:16 * i + 16, :].rearrange("p t e -> p (t e)"), k.const("ident"))
                last.then_inc(s["gt"], 1)

            @block.sync
            def _(sp):
                sp.wait_ge(s["gts"], 1)
                for i in range(2):
                    for j in range(16):
                        sp.dma_start(k.gates[:, (16 * i + j) * P:(16 * i + j + 1) * P], gT[8 * j:8 * j + 8, i, :]).then_inc(s["gd"], 16)
                sp.wait_ge(s["gd"], 16 * 32)

    with ExitStack() as ctx:
        R = range(2)
        NGB = 4
        gb = [k.sb(ctx, f"f0_gb{i}", [P, BLK]) for i in range(NGB)]
        xs = [k.sb(ctx, f"f0_xs{i}", [P, BLK]) for i in R]
        hh = [k.sb(ctx, f"f0_hh{i}", [P, BLK]) for i in R]
        x3 = [k.sb(ctx, f"f0_x3{i}", [P, BLK]) for i in R]
        xm = [k.sb(ctx, f"f0_xm{i}", [P, BLK]) for i in R]
        pr = [k.sb(ctx, f"f0_pr{i}", [P, BLK]) for i in R]
        acc = k.sb(ctx, "f0_acc", [P, BLK])
        p_h = [k.ps(ctx, f"ps_f0h{i}", [P, 512]) for i in R]
        p_3 = [k.ps(ctx, f"ps_f03{i}", [P, 512]) for i in R]
        p_2 = [k.ps(ctx, f"ps_f02{i}", [P, 512]) for i in R]
        p_z = k.ps(ctx, "ps_f0z", [P, 512])
        p_t = k.ps(ctx, "ps_f0t", [P, 512])
        names = ("gb", "xs", "h", "hs", "x3", "x3s", "sm", "x2", "pr", "acc", "z", "zc", "tr", "x", "chain")
        s = {n: k.sem("f0b_" + n) for n in names}
        gbs = [k.sem(f"f0b_gate{i}") for i in range(NGB)]
        N = E + 2
        with nc.Block("experts0") as block:

            @block.sync
            def _(sp):
                for n, c in (("sm", 1), ("x3s", 2), ("hs", 2), ("pr", 2), ("acc", 2), ("x", 1), ("x2", 2), ("tr", 1)):
                    sp.sem_inc(s[n], c)
                sp.sem_inc(s["gb"], NGB)
                with sp.Fori(0, NB) as it:
                    for e in range(E):
                        sp.wait_ge(s["gb"], it * E + e + 1)
                        sp.dma_start(gb[e % NGB][:], k.gates[e:e + 1, bass.ds(it * BLK, BLK)].broadcast_to([P, BLK])).then_inc(gbs[e % NGB], 16)

            @block.vector
            def _(dve):
                def scale(it, e):
                    dve.wait_ge(gbs[e % NGB], it * (16 * (E // NGB)) + 16 * (e // NGB + 1))
                    dve.wait_ge(s["x3"], it * N + e + 1)
                    nc.vector.scalar_tensor_tensor(out=xs[e % 2][:], in0=gb[e % NGB][:], scalar=0.0,
                                                   in1=k.xnT[:, bass.ds(it * BLK, BLK)], op0=ALU.max, op1=ALU.mult).then_inc(s["xs"], 1)

                with dve.Fori(0, NB) as it:
                    scale(it, 0)
                    for e in range(E):
                        if e + 1 < E:
                            scale(it, e + 1)
                        dve.wait_ge(s["x3s"], it * E + e + 3)
                        dve.wait_ge(s["pr"], it * E + e + 1)
                        nc.vector.scalar_tensor_tensor(out=xm[e % 2][:], in0=gb[e % NGB][:], scalar=0.0, in1=x3[e % 2][:],
                                                       op0=ALU.is_ge, op1=ALU.mult).then_inc(s["gb"], 1)
                        dve.wait_ge(s["gb"], it * E + e + NGB + 1)
                        dve.wait_ge(s["x2"], it * E + e + 3)
                        dve.wait_ge(s["acc"], it * (E + 1) + max(e + 1, 2))
                        nc.vector.scalar_tensor_tensor(out=pr[e % 2][:], in0=p_2[e % 2][:], scalar=w.bias[:, E + e:E + e + 1],
                                                       in1=xm[e % 2][:], op0=ALU.add, op1=ALU.mult).then_inc(s["pr"], 1)
                    for c in range(2):
                        dve.wait_ge(s["hs"], it * N + E + c + 3)
                        dve.wait_ge(s["x3"], it * N + E + c + 3)
                        dve.wait_ge(s["pr"], it * E + E + c + 1)
                        nc.vector.tensor_tensor(xm[c][:], hh[c][:], p_3[c][:], ALU.mult).then_inc(s["sm"], 1)
                    dve.wait_ge(s["tr"], it + 2)
                    xv = k.x[:, bass.ds(it * U, U), :].rearrange("p a d -> p (a d)")
                    nc.vector.tensor_tensor(xv, xv, p_t[:], ALU.add).then_inc(s["x"], 1)

            @block.gpsimd
            def _(pool):
                with pool.Fori(0, NB) as it:
                    pool.wait_ge(s["tr"], it + 1)
                    pool.wait_ge(s["pr"], it * E + 4)
                    nc.gpsimd.tensor_tensor(acc[:], pr[0][:], pr[1][:], ALU.add).then_inc(s["acc"], 2)
                    for e in range(2, E):
                        pool.wait_ge(s["pr"], it * E + e + 3)
                        pool.wait_ge(s["acc"], it * (E + 1) + e + 2)
                        nc.gpsimd.tensor_tensor(acc[:], acc[:], pr[e % 2][:], ALU.add).then_inc(s["acc"], 1)
                    pool.wait_ge(s["zc"], it + 1)
                    pool.wait_ge(s["acc"], it * (E + 1) + E + 2)
                    nc.gpsimd.tensor_tensor(acc[:], acc[:], pr[0][:], ALU.add).then_inc(s["acc"], 1)

            @block.scalar
            def _(act):
                with act.Fori(0, NB) as it:
                    for n in range(N):
                        sl = n % 2
                        act.wait_ge(s["h"], it * N + n + 1)
                        if n >= 2:
                            act.wait_ge(s["x2"], it * E + n + 1)
                        else:
                            act.wait_ge(s["sm"], it * 2 + 1)
                        if n < E:
                            nc.scalar.activation(hh[sl][:], p_h[sl][:], ACT.Silu, bias=w.bias[:, n:n + 1]).then_inc(s["hs"], 1)
                            act.wait_ge(s["x3"], it * N + n + 3)
                            act.wait_ge(s["gb"], it * E + n + 3)
                            nc.scalar.activation(x3[sl][:], p_3[sl][:], ACT.Identity, bias=w.bias[:, 2 * E + n:2 * E + n + 1]).then_inc(s["x3s"], 1)
                        else:
                            nc.scalar.activation(hh[sl][:], p_h[sl][:], ACT.Silu).then_inc(s["hs"], 1)
                    act.wait_ge(s["z"], it + 1)
                    act.wait_ge(s["acc"], it * (E + 1) + E + 1)
                    nc.scalar.activation(pr[0][:], p_z[:], ACT.Copy).then_inc(s["zc"], 1)

            @block.tensor
            def _(pe):
                pe.sem_inc(s["x3"], 2)
                with pe.Fori(0, NB) as it:
                    def up(n):
                        sl = n % 2
                        pe.wait_ge(s["hs"], it * N + n + 1)
                        if n < E:
                            pe.wait_ge(s["xs"], it * E + n + 1)
                            rhs = xs[sl][:]
                            a, b = w.expT[:, n, :], w.expT[:, 2 * E + n, :]
                        else:
                            rhs = k.xnT[:, bass.ds(it * BLK, BLK)]
                            a, b = w.shT[:, n - E, :], w.shT[:, 2 + n - E, :]
                        nc.tensor.matmul(p_h[sl][:], a, rhs, start=True, stop=True).then_inc(s["h"], 1)
                        if n >= 2:
                            pe.wait_ge(s["x3s"], it * E + n + 1)
                        else:
                            pe.wait_ge(s["sm"], it * 2 + 1)
                        nc.tensor.matmul(p_3[sl][:], b, rhs, start=True, stop=True).then_inc(s["x3"], 1)

                    up(0)
                    for e in range(E):
                        up(e + 1)
                        pe.wait_ge(s["hs"], it * N + e + 3)
                        pe.wait_ge(s["pr"], it * E + e + 1)
                        nc.tensor.matmul(p_2[e % 2][:], w.expT[:, E + e, :], hh[e % 2][:], start=True, stop=True).then_inc(s["x2"], 1)
                    up(N - 1)
                    for c in range(2):
                        pe.wait_ge(s["sm"], it * 2 + c + 2)
                        last = nc.tensor.matmul(p_z[:], w.shT[:, 4 + c, :], xm[c][:], start=(c == 0), stop=(c == 1))
                    last.then_inc(s["z"], 1)
                    pe.wait_ge(s["acc"], it * (E + 1) + E + 3)
                    pe.wait_ge(s["x"], it + 1)
                    for u in range(U):
                        last = nc.tensor.transpose(p_t[:, u * P:(u + 1) * P], acc[:, u * P:(u + 1) * P], k.const("ident"))
                    last.then_inc(s["tr"], 1)


class Weights0:
    def __init__(self, k, ctx):
        self.expT = k.sb(ctx, "expT", [P, 3 * E, P])
        self.shT = k.sb(ctx, "shT", [P, 6, P])
        self.outT = k.sb(ctx, "outT", [P, P])
        self.proj = k.sb(ctx, "proj0", [P, 392])
        self.bias = k.sb(ctx, "bias0", [P, 3 * E])
        self.map_bias = k.sb(ctx, "map_bias", [P, 2, HD])
        self.logits = k.sb(ctx, "logits0", [P, NT, E])

class Weights1:
    def __init__(self, k, ctx):
        self.proj = k.sb(ctx, "proj1", [P, 3 * D])
        self.route = k.sb(ctx, "route1", [P, E + 1])
        self.bias = k.sb(ctx, "bias1", [P, 3 * D])
        self.hd = k.sb(ctx, "hd1", [P, 2, HD])
        self.rhb = k.sb(ctx, "rhb", [P, 1])
        self.outw = k.sb(ctx, "outw1", [P, D])
        self.outb = k.sb(ctx, "outb1", [P, D])
        self.lg = k.sb(ctx, "lg1", [P, NT, E + 1])


def phase_weights1(k, w):
    nc, io = k.nc, k.io
    with ExitStack() as ctx:
        vec = k.sb(ctx, "w1_vec", [P, 4])
        rep = k.sb(ctx, "w1_rep", [P, 2, P])
        raw = k.sb(ctx, "w1_raw", [P, 3 * D])
        p_b = k.ps(ctx, "ps_w1", [P, 512])
        s = {n: k.sem("w1_" + n) for n in ("in", "rep", "mm", "done")}
        names = ("qn_w", "qn_b", "kvn_w", "kvn_b")
        col = lambda v: v.rearrange("(p a) -> p a", a=1)
        with nc.Block("weights1") as block:
            @block.sync
            def _(sp):
                for i, n in enumerate(names):
                    sp.dma_start(vec[:, i:i + 1], col(io["L1_attn_" + n])).then_inc(s["in"], 16)
                sp.dma_start(raw[:, 0:D], io["L1_attn_q_w"]).then_inc(s["in"], 16)
                sp.dma_start(raw[:, D:3 * D], io["L1_attn_kv_w"]).then_inc(s["in"], 16)
                sp.dma_start(w.route[:, 0:E], io["L1_ffn_Wr"]).then_inc(s["in"], 16)
                sp.dma_start(w.route[:, E:E + 1], io["L1_attn_rh_w"]).then_inc(s["in"], 16)
                sp.dma_start(w.bias[:, 0:D], rows_of(io["L1_attn_q_b"], P)).then_inc(s["in"], 16)
                sp.dma_start(w.bias[:, D:3 * D], rows_of(io["L1_attn_kv_b"], P)).then_inc(s["in"], 16)
                sp.dma_start(w.hd[:, 0, :], rows_of(io["L1_attn_ln_w"], P)).then_inc(s["in"], 16)
                sp.dma_start(w.hd[:, 1, :], rows_of(io["L1_attn_ln_b"], P)).then_inc(s["in"], 16)
                sp.dma_start(w.rhb[:], rows_of(io["L1_attn_rh_b"], P)).then_inc(s["in"], 16)
                sp.dma_start(w.outw[:], io["L1_attn_out_w"]).then_inc(s["in"], 16)
                sp.dma_start(w.outb[:], rows_of(io["L1_attn_out_b"], P)).then_inc(s["in"], 16)

            @block.vector
            def _(dve):
                dve.wait_ge(s["in"], 16 * 15)
                for i in range(2):
                    last = nc.vector.tensor_copy(rep[:, i, :], vec[:, 2 * i + 1:2 * i + 2].broadcast_to([P, P]))
                last.then_inc(s["rep"], 1)
                nc.vector.tensor_scalar(w.proj[:, 0:D], raw[:, 0:D], vec[:, 0:1], None, ALU.mult)
                nc.vector.tensor_scalar(w.proj[:, D:3 * D], raw[:, D:3 * D], vec[:, 2:3], None, ALU.mult)
                dve.wait_ge(s["mm"], 1)
                nc.vector.tensor_tensor(w.bias[:], w.bias[:], p_b[:, 0:3 * D], ALU.add).then_inc(s["done"], 1)

            @block.tensor
            def _(pe):
                pe.wait_ge(s["rep"], 1)
                nc.tensor.matmul(p_b[:, 0:D], rep[:, 0, :], raw[:, 0:D], start=True, stop=True)
                nc.tensor.matmul(p_b[:, D:3 * D], rep[:, 1, :], raw[:, D:3 * D], start=True, stop=True).then_inc(s["mm"], 1)


def phase_project1(k, w):
    nc = k.nc
    with ExitStack() as ctx:
        st = [k.sb(ctx, f"p1_st{i}", [P, U, 6]) for i in range(2)]
        mv = [k.sb(ctx, f"p1_mv{i}", [P, U, 2]) for i in range(2)]
        sd = [k.sb(ctx, f"p1_sd{i}", [P, U]) for i in range(2)]
        rs = [k.sb(ctx, f"p1_rs{i}", [P, U]) for i in range(2)]
        pause = k.sb(ctx, "p1_pause", [P, 2])
        xn = [k.sb(ctx, f"p1_xn{i}", [P, U, D]) for i in range(2)]
        xt = [k.sb(ctx, f"p1_xt{i}", [P, BLK]) for i in range(2)]
        ps_t = [k.ps(ctx, f"ps_p1t{i}", [P, 512]) for i in range(2)]
        ps_q = k.ps(ctx, "ps_p1q", [P, U, 512])
        s = {n: k.sem("p1_" + n) for n in ("chain", "stats", "std", "normed", "turned", "xt", "proj", "kept")}
        with nc.Block("project1") as block:

            @block.vector
            def _(dve):
                step = Steps(dve, s["chain"])
                with dve.Fori(0, NB) as it:
                    step.loop(it, 4 + 1)
                    for r in range(2):
                        src = [k.x[:, bass.ds(it * U + u, 1), :].rearrange("p a d -> p (a d)") if r == 0 else xn[0][:, u, :]
                               for u in range(U)]
                        for u in range(U):
                            last = nc.vector.bn_stats(st[r][:, u, :], src[u])
                        step(last)
                        nc.vector.memset(pause[:, r:r + 1], 0.0)
                        for u in range(U):
                            last = nc.vector.bn_aggr(mv[r][:, u, :], st[r][:, u, :])
                        last.then_inc(s["stats"], 1)
                        dve.wait_ge(s["std"], it * 2 + r + 1)
                        step(nc.vector.reciprocal(rs[r][:], sd[r][:]))
                        dve.wait_ge(s["turned"], it * 2 + r + 1)
                        for u in range(U):
                            last = nc.vector.tensor_scalar(xn[r][:, u, :], src[u], mv[r][:, u, 0:1], rs[r][:, u:u + 1],
                                                           ALU.subtract, ALU.mult)
                        last.then_inc(s["normed"], 1)
                        if r == 0:
                            dve.wait_ge(s["normed"], it * 2 + 1)
                    dve.wait_ge(s["proj"], it + 1)
                    for u in range(U):
                        nc.vector.tensor_tensor(w.qk[:, bass.ds(it * U + u, 1), :].rearrange("p a c -> p (a c)"),
                                                ps_q[:, u, 0:2 * D], w.bias[:, 0:2 * D], ALU.add)
                        nc.vector.tensor_tensor(w.v1[:, bass.ds(it * U + u, 1), :, 0:HD].rearrange("p a h e -> p (a h) e"),
                                                ps_q[:, u, 2 * D:3 * D].rearrange("p (h e) -> p h e", e=HD),
                                                w.bias[:, 2 * D:3 * D].rearrange("p (h e) -> p h e", e=HD), ALU.add)
                    nc.vector.tensor_copy(w.lg[:, bass.ds(it * U, U), :], ps_q[:, :, 3 * D:3 * D + E + 1]).then_inc(s["kept"], 1)
                    step(nc.vector.tensor_copy(k.xnT[:, bass.ds(it * BLK, BLK)], xt[0][:]))

            @block.scalar
            def _(act):
                with act.Fori(0, NB) as it:
                    for r in range(2):
                        act.wait_ge(s["stats"], it * 2 + r + 1)
                        nc.scalar.activation(sd[r][:], mv[r][:, :, 1], ACT.Sqrt, bias=k.eps[:]).then_inc(s["std"], 1)
                    for r in range(2):
                        act.wait_ge(s["turned"], it * 2 + r + 3)
                        nc.scalar.activation(xt[r][:], ps_t[r][:], ACT.Copy).then_inc(s["xt"], 1)

            @block.tensor
            def _(pe):
                pe.sem_inc(s["turned"], 2)
                with pe.Fori(0, NB) as it:
                    for r in range(2):
                        pe.wait_ge(s["normed"], it * 2 + r + 1)
                        for u in range(U):
                            last = nc.tensor.transpose(ps_t[r][:, u * P:(u + 1) * P], xn[r][:, u, :], k.const("ident"))
                        last.then_inc(s["turned"], 1)
                    pe.wait_ge(s["xt"], it * 2 + 2)
                    pe.wait_ge(s["kept"], it + 1)
                    for u in range(U):
                        nc.tensor.matmul(ps_q[:, u, 0:3 * D], xt[1][:, u * P:(u + 1) * P], w.proj[:], start=True, stop=True)
                        last = nc.tensor.matmul(ps_q[:, u, 3 * D:3 * D + E + 1], xt[0][:, u * P:(u + 1) * P], w.route[:],
                                                start=True, stop=True)
                    last.then_inc(s["proj"], 1)

            @block.gpsimd
            def _(pool):
                pool.sem_inc(s["kept"], 1)


def phase_rotary(k, w):
    nc = k.nc
    G8 = 2 * H
    with ExitStack() as ctx:
        fr = k.sb(ctx, "ro_fr", [P, 2, NT, 4])
        rad = k.sb(ctx, "ro_rad", [P, NT])
        var = k.sb(ctx, "ro_var", [P, NT, G8])
        rv = k.sb(ctx, "ro_rv", [P, NT, G8])
        t1 = k.sb(ctx, "ro_t1", [P, U, 256])
        t2 = k.sb(ctx, "ro_t2", [P, U, 256])
        rot = k.sb(ctx, "ro_rot", [P, U, 256])
        sm = k.sb(ctx, "ro_sm", [P, U * G8])
        s = {n: k.sem("ro_" + n) for n in ("chain", "fr", "t2", "c", "sq", "var", "sd")}
        with nc.Block("rotary") as block:
            @block.vector
            def _(dve):
                step = Steps(dve, s["chain"])
                step(nc.vector.tensor_scalar(rad[:], w.lg[:, :, E], w.rhb[:], 0.01, ALU.add, ALU.mult))
                step(nc.vector.tensor_scalar(rad[:], rad[:], 0.5, 2.0, ALU.max, ALU.min))
                for i, n in enumerate(("cos", "sin")):
                    tab = k.const(n).rearrange("p (t f) -> p t f", f=4).unsqueeze(1).broadcast_to([P, BATCH, TB, 4])
                    r4 = rad[:].rearrange("p (b t) -> p b t", b=BATCH).unsqueeze(3).broadcast_to([P, BATCH, TB, 4])
                    step(nc.vector.tensor_tensor(fr[:, i].rearrange("p (b t) f -> p b t f", b=BATCH), tab, r4, ALU.mult))
                dve.sem_inc(s["fr"], 1)
                with dve.Fori(0, NB) as it:
                    step.loop(it, 6)
                    pairs = lambda a: a.rearrange("p (g f c) -> p g f c", f=4, c=2)
                    for u in range(U):
                        f = fr[:, 0, bass.ds(it * U + u, 1), :].unsqueeze(3).broadcast_to([P, G8, 4, 2])
                        src = pairs(w.qk[:, bass.ds(it * U + u, 1), :].rearrange("p a c -> p (a c)"))
                        last = nc.vector.tensor_tensor(pairs(t1[:, u, :]), src, f, ALU.mult)
                    step(last)
                    dve.wait_ge(s["t2"], it + 1)
                    one = lambda a, c: a[:].rearrange("p u (x c) -> p (u x) c", c=2)[:, :, c]
                    nc.vector.tensor_tensor(one(rot, 0), one(t1, 0), one(t2, 1), ALU.subtract)
                    step(nc.vector.tensor_tensor(one(rot, 1), one(t2, 0), one(t1, 1), ALU.add))
                    rg = rot[:].rearrange("p u (g e) -> p (u g) e", e=HD)
                    step(nc.vector.tensor_reduce(sm[:], rg, axis=AX, op=ALU.add))
                    step(nc.vector.tensor_scalar(sm[:], sm[:], 1.0 / HD, None, ALU.mult))
                    nc.vector.tensor_tensor(w.qk[:, bass.ds(it * U, U), :].rearrange("p a (g e) -> p (a g) e", e=HD), rg,
                                            sm[:].unsqueeze(2).broadcast_to([P, U * G8, HD]), ALU.subtract).then_inc(s["c"], 1)
                    dve.wait_ge(s["sq"], it + 1)
                    step(nc.vector.tensor_reduce(var[:, bass.ds(it * U, U), :].rearrange("p a g -> p (a g)"),
                                                 t1[:].rearrange("p u (g e) -> p (u g) e", e=HD), axis=AX, op=ALU.add))
                    step(nc.vector.memset(sm[:, 0:1], 0.0))
                step.end(NB)
                dve.sem_inc(s["var"], 1)
                dve.wait_ge(s["sd"], 1)
                step(nc.vector.reciprocal(rv[:], var[:]))

            @block.gpsimd
            def _(pool):
                pool.wait_ge(s["fr"], 1)
                with pool.Fori(0, NB) as it:
                    pool.wait_ge(s["c"], it + 1)
                    pairs = lambda a: a.rearrange("p (g f c) -> p g f c", f=4, c=2)
                    for u in range(U):
                        f = fr[:, 1, bass.ds(it * U + u, 1), :].unsqueeze(3).broadcast_to([P, G8, 4, 2])
                        src = pairs(w.qk[:, bass.ds(it * U + u, 1), :].rearrange("p a c -> p (a c)"))
                        last = nc.gpsimd.tensor_tensor(pairs(t2[:, u, :]), src, f, ALU.mult)
                    last.then_inc(s["t2"], 1)

            @block.scalar
            def _(act):
                act.sem_inc(s["c"], 1)
                with act.Fori(0, NB) as it:
                    act.wait_ge(s["c"], it + 2)
                    nc.scalar.activation(t1[:], w.qk[:, bass.ds(it * U, U), :], ACT.Square).then_inc(s["sq"], 1)
                act.wait_ge(s["var"], 1)
                nc.scalar.activation(var[:], var[:], ACT.Sqrt, scale=1.0 / HD, bias=k.eps[:]).then_inc(s["sd"], 1)

        nb = k.sb(ctx, "ro_nb", [P, U, 256])
        sq = k.sb(ctx, "ro_sqn", [P, U, 256])
        part = [[k.sb(ctx, f"ro_part{i}{j}", [P, BLK], BF16) for j in range(PARTS)] for i in range(2)]
        rest = [k.sb(ctx, f"ro_rest{i}", [P, BLK]) for i in range(2)]
        n2 = k.sb(ctx, "ro_n2", [P, NT, G8])
        mx = k.sb(ctx, "ro_mx", [P, 2])
        mall = k.sb(ctx, "ro_mall", [P, 2])
        p_t = [k.ps(ctx, f"ps_ro{i}", [P, 512]) for i in range(2)]
        s = {n: k.sem("rp_" + n) for n in ("chain", "n", "sq", "tr", "p1", "r1", "p2", "p3", "out0", "out1", "n2", "nrm", "mx", "all")}
        with nc.Block("parts") as block:
            @block.vector
            def _(dve):
                step = Steps(dve, s["chain"])
                with dve.Fori(0, NB) as it:
                    step.loop(it, 3)
                    wide = lambda a: a.rearrange("p u (g e) -> p (u g) e", e=HD)
                    row = lambda i: w.hd[:, i, :].unsqueeze(1).broadcast_to([P, U * G8, HD])
                    dve.wait_ge(s["tr"], it + 1)
                    dve.wait_ge(s["sq"], it + 1)
                    step(nc.vector.tensor_tensor(wide(nb[:]), wide(w.qk[:, bass.ds(it * U, U), :]),
                                                 rv[:, bass.ds(it * U, U), :].rearrange("p a g -> p (a g)").unsqueeze(2).broadcast_to([P, U * G8, HD]),
                                                 ALU.mult))
                    step(nc.vector.tensor_tensor(wide(nb[:]), wide(nb[:]), row(0), ALU.mult))
                    nc.vector.tensor_tensor(wide(nb[:]), wide(nb[:]), row(1), ALU.add).then_inc(s["n"], 1)
                    dve.wait_ge(s["sq"], it + 2)
                    step(nc.vector.tensor_reduce(n2[:, bass.ds(it * U, U), :].rearrange("p a g -> p (a g)"), wide(sq[:]), axis=AX, op=ALU.add))
                    for i in range(2):
                        dve.wait_ge(s["p1"], it * 2 + i + 1)
                        nc.vector.tensor_tensor(rest[i][:], p_t[i][:], part[i][0][:], ALU.subtract).then_inc(s["r1"], 1)
                        dve.wait_ge(s["p2"], it * 2 + i + 1)
                        nc.vector.tensor_tensor(part[i][2][:], rest[i][:], part[i][1][:], ALU.subtract).then_inc(s["p3"], 1)
                step.end(NB)
                dve.sem_inc(s["n2"], 1)
                dve.wait_ge(s["nrm"], 1)
                for i in range(2):
                    last = nc.vector.tensor_reduce(mx[:, i:i + 1], n2[:, :, i * H:(i + 1) * H], axis=mybir.AxisListType.XY, op=ALU.max)
                last.then_inc(s["mx"], 1)
                dve.wait_ge(s["all"], 1)
                step(nc.vector.tensor_scalar(k.rowmax[:], n2[:, :, 0:H], mall[:, 1:2], None, ALU.mult))
                step(nc.vector.tensor_tensor(mx[:, 0:1], mall[:, 0:1], mall[:, 1:2], ALU.mult))
                step(nc.vector.tensor_scalar(mx[:, 1:2], mx[:, 0:1], MAX_GAP / (2 * HD ** -0.5), None, ALU.is_gt))
                step(nc.vector.tensor_copy(k.flag[:], mx[:, 1:2]))

            @block.gpsimd
            def _(pool):
                pool.sem_inc(s["sq"], 1)
                pool.wait_ge(s["mx"], 1)
                nc.gpsimd.partition_all_reduce(mall[:], mx[:], P, bass.bass_isa.ReduceOp.max).then_inc(s["all"], 1)

            @block.scalar
            def _(act):
                with act.Fori(0, NB) as it:
                    act.wait_ge(s["n"], it + 1)
                    nc.scalar.activation(sq[:], nb[:], ACT.Square).then_inc(s["sq"], 1)
                    for i in range(2):
                        act.wait_ge(s["tr"], it + 2)
                        act.wait_ge(s["out" + str(i)], (it + 1) * 16 * PARTS)
                        nc.scalar.activation(part[i][0][:], p_t[i][:], ACT.Copy).then_inc(s["p1"], 1)
                        act.wait_ge(s["r1"], it * 2 + i + 1)
                        nc.scalar.activation(part[i][1][:], rest[i][:], ACT.Copy).then_inc(s["p2"], 1)
                act.wait_ge(s["n2"], 1)
                nc.scalar.activation(n2[:], n2[:], ACT.Sqrt).then_inc(s["nrm"], 1)

            @block.tensor
            def _(pe):
                pe.sem_inc(s["tr"], 1)
                pe.sem_inc(s["p3"], 2)
                with pe.Fori(0, NB) as it:
                    pe.wait_ge(s["n"], it + 1)
                    pe.wait_ge(s["p3"], it * 2 + 2)
                    for i in range(2):
                        for u in range(U):
                            last = nc.tensor.transpose(p_t[i][:, u * P:(u + 1) * P], nb[:, u, i * P:(i + 1) * P], k.const("ident"))
                    last.then_inc(s["tr"], 1)

            @block.sync
            def _(sp):
                for i in range(2):
                    sp.sem_inc(s["out" + str(i)], 16 * PARTS)
                with sp.Fori(0, NB) as it:
                    for i in range(2):
                        sp.wait_ge(s["p3"], it * 2 + i + 3)
                        for j in range(PARTS):
                            dst = k.parts[i, j, :, bass.ds(it * BLK, BLK)]
                            sp.dma_start(dst, part[i][j][:]).then_inc(s["out" + str(i)], 16)
                for i in range(2):
                    sp.wait_ge(s["out" + str(i)], (NB + 1) * 16 * PARTS)


def split_rows(k, side, head, cols):
    src = k.parts[side, :, head, cols]
    return src.unsqueeze(1 - side).broadcast_to([PARTS, PARTS, HD, SEQ])


def load_split(nc, sp, k, dst, side, b, g, hh, sem):
    head = bass.ds(g * (G * HD) + hh * HD, HD)
    src = split_rows(k, side, head, bass.ds(b * SEQ, SEQ))
    for i in range(PARTS):
        sp.dma_start(dst[i * PARTS * HD:(i + 1) * PARTS * HD, hh, :], src[i]).then_inc(sem, 16)


def phase_maxima(k):
    nc = k.nc
    with ExitStack() as ctx:
        qs = k.sb(ctx, "mx_qs", [SR, G, SEQ], BF16)
        ks = k.sb(ctx, "mx_ks", [SR, G, SEQ], BF16)
        top = k.sb(ctx, "mx_top", [P, TB, G])
        p_s = [k.ps(ctx, f"ps_mx{i}", [P, 2, 512]) for i in range(4)]
        s = {n: k.sem("mx_" + n) for n in ("in", "mm", "red", "kept")}
        UN = G * TB

        def taken(eng):
            return eng.If(eng.value_load(k.flag[0:1, 0:1], min_val=0, max_val=1) != 0)

        with nc.Block("maxima") as block:
            @block.sync
            def _(sp):
                with taken(sp):
                    with sp.Fori(0, BATCH) as b:
                        with sp.Fori(0, NG) as g:
                            sp.wait_ge(s["kept"], b * NG + g + 1)
                            for hh in range(G):
                                load_split(nc, sp, k, qs, 0, b, g, hh, s["in"])
                                load_split(nc, sp, k, ks, 1, b, g, hh, s["in"])

            @block.tensor
            def _(pe):
                with taken(pe):
                    with pe.Fori(0, BATCH * NG) as it:
                        pe.wait_ge(s["in"], (it + 1) * (2 * G * PARTS * 16))
                        for n in range(UN):
                            hh, t = n // TB, n % TB
                            pe.wait_ge(s["red"], it * UN + n + 1)
                            for half in range(2):
                                last = nc.tensor.matmul(p_s[n % 4][:, half, :], qs[:, hh, t * P:(t + 1) * P],
                                                        ks[:, hh, half * 512:half * 512 + 512], start=True, stop=True)
                            last.then_inc(s["mm"], 1)

            @block.vector
            def _(dve):
                with taken(dve):
                    dve.sem_inc(s["kept"], 1)
                    dve.sem_inc(s["red"], 4)
                    with dve.Fori(0, BATCH) as b:
                        with dve.Fori(0, NG) as g:
                            for n in range(UN):
                                hh, t = n // TB, n % TB
                                dve.wait_ge(s["mm"], (b * NG + g) * UN + n + 1)
                                nc.vector.tensor_reduce(top[:, t, hh:hh + 1], p_s[n % 4][:].rearrange("p a c -> p (a c)"),
                                                        axis=AX, op=ALU.max).then_inc(s["red"], 1)
                            dve.wait_ge(s["red"], (b * NG + g + 1) * UN + 4)
                            nc.vector.tensor_copy(k.rowmax[:, bass.ds(b * TB, TB), bass.ds(g * G, G)], top[:]).then_inc(s["kept"], 1)
                            dve.wait_ge(s["kept"], b * NG + g + 2)


def phase_rows(k, ks_ones):
    nc = k.nc
    with ExitStack() as ctx:
        mT = k.sb(ctx, "rw_mT", [P, 4, P], BF16)
        ones = k.sb(ctx, "rw_ones", [1, G * SEQ], BF16)
        p_m = k.ps(ctx, "ps_rw", [P, 512])
        s = {n: k.sem("rw_" + n) for n in ("ones", "tr", "cp", "out")}
        with nc.Block("rows") as block:
            @block.vector
            def _(dve):
                nc.vector.memset(ones[:], 1.0).then_inc(s["ones"], 1)

            @block.tensor
            def _(pe):
                for i in range(4):
                    last = nc.tensor.transpose(p_m[:, i * P:(i + 1) * P],
                                               k.rowmax[:, i * TB:(i + 1) * TB, :].rearrange("p t h -> p (t h)"), k.const("ident"))
                last.then_inc(s["tr"], 1)

            @block.scalar
            def _(act):
                act.wait_ge(s["tr"], 1)
                nc.scalar.activation(mT[:].rearrange("p a t -> p (a t)"), p_m[:], ACT.Copy, scale=-1.0).then_inc(s["cp"], 1)

            @block.sync
            def _(sp):
                sp.wait_ge(s["cp"], 1)
                for i in range(4):
                    for t in range(TB):
                        sp.dma_start(k.rows[:, (i * TB + t) * P:(i * TB + t + 1) * P], mT[t * H:(t + 1) * H, i, :]).then_inc(s["out"], 16)
                sp.wait_ge(s["ones"], 1)
                for ks in ks_ones:
                    sp.dma_start(ks[SR:SR + 1, :, :].rearrange("p g t -> p (g t)"), ones[:]).then_inc(s["out"], 16)
                sp.wait_ge(s["out"], 16 * (4 * TB + len(ks_ones)))


def phase_attention(k, w, ab):
    nc = k.nc
    QH, KB = 2, TB
    RUNS = 2 * QH
    UN = RUNS * KB * 2
    slot_of = [n % 3 for n in range(UN - 1)] + [1]
    NP = 4
    CREDIT = UN // 2
    with ExitStack() as ctx:
        qs = [k.sb(ctx, f"at_qs{i}", [SR + 1, G, SEQ], BF16) for i in range(2)]
        ks = [k.sb(ctx, f"at_ks{i}", [SR + 1, G, SEQ], BF16) for i in range(2)]
        phase_rows(k, ks)
        vs = [k.sb(ctx, f"at_vs{i}", [P, TB, G, HD + 1]) for i in range(2)]
        pp = [k.sb(ctx, f"at_pp{i}", [P, 2, 512]) for i in range(NP)]
        oT = k.sb(ctx, "at_oT", [P, 512])
        den = k.sb(ctx, "at_den", [P, 16])
        p_s = [k.ps(ctx, f"ps_at{i}", [P, 2, 512]) for i in range(3)]
        p_o = k.ps(ctx, "ps_ato", [P, 512])
        p_t = k.ps(ctx, "ps_att", [P, 512])
        s = {n: k.sem("at_" + n) for n in ("in0", "in1", "v", "qk", "exp", "pv", "ev", "tr", "den", "y", "zero")}
        with nc.Block("attention") as block:
            @block.sync
            def _(sp):
                with sp.Fori(0, BATCH) as b:
                    with sp.Fori(0, NG // 2) as gp:
                        for i in range(2):
                            sp.wait_ge(s["pv"], (b * (NG // 2) + gp) * (UN // 2) + (UN // 4) * (i + 1) - UN // 2 + CREDIT)
                            for hh in range(G):
                                load_split(nc, sp, k, qs[i], 0, b, gp * 2 + i, hh, s[f"in{i}"])
                                load_split(nc, sp, k, ks[i], 1, b, gp * 2 + i, hh, s[f"in{i}"])
                            sp.dma_start(qs[i][SR:SR + 1, :, :],
                                         k.rows[bass.ds(gp * (2 * G) + i * G, G), bass.ds(b * SEQ, SEQ)].unsqueeze(0)).then_inc(s[f"in{i}"], 16)

            @block.gpsimd
            def _(pool):
                with pool.Fori(0, BATCH) as b:
                    with pool.Fori(0, NG // 2) as gp:
                        for i in range(2):
                            pool.wait_ge(s["pv"], (b * (NG // 2) + gp) * (UN // 2) + (UN // 4) * (i + 1) - UN // 2 + CREDIT)
                            nc.gpsimd.tensor_copy(vs[i][:], w.v1[:, bass.ds(b * TB, TB), bass.ds(gp * (2 * G) + i * G, G), :]).then_inc(s["v"], 1)

            @block.tensor
            def _(pe):
                pe.wait_ge(s["zero"], 1)
                with pe.Fori(0, BATCH * NG // 2) as it:
                    def scores(n):
                        r, kb, pair = n // (KB * 2), n // 2 % KB, n % 2
                        i, qh, sl = r // QH, r % QH, slot_of[n]
                        if n % (UN // 2) == 0:
                            pe.wait_ge(s[f"in{i}"], (it + 1) * (16 * (2 * G * PARTS + 1)))
                        before = max([m for m in range(n) if slot_of[m] == sl], default=None)
                        if before is None:
                            before = max(m for m in range(UN) if slot_of[m] == sl) - UN
                        pe.wait_ge(s["exp"], it * UN + before + 1 + UN)
                        for a in range(2):
                            hh = pair * 2 + a
                            last = nc.tensor.matmul(p_s[sl][:, a, :], ks[i][:, hh, kb * P:(kb + 1) * P],
                                                    qs[i][:, hh, qh * 512:qh * 512 + 512], start=True, stop=True)
                        last.then_inc(s["qk"], 1)

                    for n in range(2):
                        scores(n)
                    for m in range(UN // 2):
                        if 2 * m + 2 < UN:
                            scores(2 * m + 2)
                        r, kb = m // KB, m % KB
                        i = r // QH
                        if kb == 0:
                            pe.wait_ge(s["ev"], it * RUNS + r + 1)
                            if r % QH == 0:
                                pe.wait_ge(s["v"], it * 2 + i + 1)
                        pe.wait_ge(s["exp"], it * UN + 2 * m + 2 + UN)
                        for hh in range(G):
                            last = nc.tensor.matmul(p_o[32 * hh:32 * hh + HD + 1, :], vs[i][:, kb, hh, :],
                                                    pp[(2 * m + hh // 2) % NP][:, hh % 2, :], start=(kb == 0), stop=(kb == KB - 1),
                                                    tile_position=(0, 32 * hh), skip_group_check=True)
                        last.then_inc(s["pv"], 1)
                        if 2 * m + 3 < UN:
                            scores(2 * m + 3)
                        if kb == KB - 1:
                            pe.wait_ge(s["ev"], it * RUNS + r + 2)
                            pe.wait_ge(s["y"], it * RUNS + r + 1)
                            for u in range(U):
                                last = nc.tensor.transpose(p_t[:, u * P:(u + 1) * P], oT[:, u * P:(u + 1) * P], k.const("ident"))
                            last.then_inc(s["tr"], 1)

            @block.scalar
            def _(act):
                act.sem_inc(s["exp"], UN)
                act.sem_inc(s["pv"], CREDIT)
                act.sem_inc(s["tr"], 1)
                with act.Fori(0, BATCH * NG // 2) as it:
                    for n in range(UN):
                        act.wait_ge(s["qk"], it * UN + n + 1)
                        act.wait_ge(s["pv"], it * (UN // 2) + n // 2 - 1 + CREDIT)
                        nc.scalar.activation(pp[n % NP][:], p_s[slot_of[n]][:], ACT.Exp, scale=HD ** -0.5).then_inc(s["exp"], 1)

            @block.vector
            def _(dve):
                nc.vector.memset(p_o[:], 0.0).then_inc(s["zero"], 1)
                dve.sem_inc(s["ev"], 1)
                dve.sem_inc(s["y"], 1)
                with dve.Fori(0, BATCH * NG // 2) as it:
                    for r in range(RUNS):
                        i, qh = r // QH, r % QH
                        dve.wait_ge(s["pv"], it * (UN // 2) + (r + 1) * KB + CREDIT)
                        dve.wait_ge(s["tr"], it * RUNS + r + 1)
                        nc.vector.tensor_copy(oT[:], p_o[:]).then_inc(s["ev"], 1)
                        dve.wait_ge(s["tr"], it * RUNS + r + 2)
                        o = p_t[:].rearrange("p (x c) -> p x c", c=32)
                        nc.vector.reciprocal(den[:], o[:, :, HD]).then_inc(s["den"], 1)
                        dve.wait_ge(s["den"], it * RUNS + r + 1)
                        nc.vector.tensor_tensor(ab[:, bass.ds((it * 2 + i) * TB + qh * U, U), :].rearrange("p t (h e) -> p (t h) e", e=HD),
                                                o[:, :, 0:HD], den[:].unsqueeze(2).broadcast_to([P, 16, HD]), ALU.mult).then_inc(s["y"], 1)
                        dve.wait_ge(s["y"], it * RUNS + r + 2)

def phase_out1(k, w, ab):
    nc = k.nc
    with ExitStack() as ctx:
        a = [k.sb(ctx, f"o1_a{i}", [P, U, D]) for i in range(2)]
        aT = k.sb(ctx, "o1_aT", [P, 512])
        p_a = k.ps(ctx, "ps_o1a", [P, 512])
        p_r = k.ps(ctx, "ps_o1r", [P, 512])
        s = {n: k.sem("o1_" + n) for n in ("a", "tr", "aT", "mm", "x")}
        with nc.Block("out1") as block:
            @block.gpsimd
            def _(pool):
                pool.sem_inc(s["tr"], 2)
                pool.sem_inc(s["aT"], 1)
                pool.sem_inc(s["x"], 1)
                with pool.Fori(0, BATCH) as b:
                    for i in range(2):
                        pool.wait_ge(s["tr"], b * 2 + i + 1)
                        for u in range(U):
                            last = nc.gpsimd.tensor_copy(a[i][:, u, :].rearrange("p (g c) -> p g c", g=NG),
                                                         ab[:].rearrange("p (bg t) c -> p bg t c", t=TB)[:, bass.ds(b * NG, NG), i * U + u, :])
                        last.then_inc(s["a"], 1)

            @block.tensor
            def _(pe):
                with pe.Fori(0, BATCH) as b:
                    for i in range(2):
                        pe.wait_ge(s["a"], b * 2 + i + 1)
                        pe.wait_ge(s["aT"], b * 2 + i + 1)
                        for u in range(U):
                            last = nc.tensor.transpose(p_a[:, u * P:(u + 1) * P], a[i][:, u, :], k.const("ident"))
                        last.then_inc(s["tr"], 1)
                        pe.wait_ge(s["aT"], b * 2 + i + 2)
                        pe.wait_ge(s["x"], b * 2 + i + 1)
                        for u in range(U):
                            last = nc.tensor.matmul(p_r[:, u * P:(u + 1) * P], aT[:, u * P:(u + 1) * P], w.outw[:], start=True, stop=True)
                        last.then_inc(s["mm"], 1)

            @block.scalar
            def _(act):
                with act.Fori(0, BATCH) as b:
                    for i in range(2):
                        act.wait_ge(s["tr"], b * 2 + i + 3)
                        act.wait_ge(s["x"], b * 2 + i + 1)
                        nc.scalar.activation(aT[:], p_a[:], ACT.Copy).then_inc(s["aT"], 1)

            @block.vector
            def _(dve):
                chain = k.sem("o1_chain")
                with dve.Fori(0, BATCH) as b:
                    for i in range(2):
                        x = k.x[:, bass.ds(b * TB + i * U, U), :]
                        nc.vector.tensor_tensor(x, x, w.outb[:].unsqueeze(1).broadcast_to([P, U, D]), ALU.add).then_inc(chain, 1)
                        dve.wait_ge(chain, b * 2 + i + 1)
                        dve.wait_ge(s["mm"], b * 2 + i + 1)
                        nc.vector.tensor_tensor(x, x, p_r[:].rearrange("p (u d) -> p u d", u=U), ALU.add).then_inc(s["x"], 1)


def phase_choose1(k, w, gate, s):
    nc = k.nc
    with ExitStack() as ctx:
        sc = k.sb(ctx, "c1_sc", [P, NT, E])
        sp2 = k.sb(ctx, "c1_sp", [P, 2, NT // 2, E])
        r1 = k.sb(ctx, "c1_r1", [P, NT])
        sT = k.sb(ctx, "c1_sT", [P, 2 * P])
        junk = k.sb(ctx, "c1_junk", [P, 2 * P])
        gtm = k.sb(ctx, "c1_gt", [P, 2 * P])
        eqm = k.sb(ctx, "c1_eq", [P, 2 * P])
        one = k.sb(ctx, "c1_one", [P, 2 * P])
        cur, cand, bit, ok = (k.sb(ctx, "c1_" + n, [P, 1], I32) for n in ("cur", "cand", "bit", "ok"))
        cnt = k.sb(ctx, "c1_cnt", [P, 2])
        off = k.sb(ctx, "c1_off", [P, 3])
        p_s = k.ps(ctx, "ps_c1s", [P, 512])
        p_c = k.ps(ctx, "ps_c1c", [P, 512])
        NBITS = 30
        with nc.Block("choose1") as block:
            @block.vector
            def _(dve):
                step = Steps(dve, s["chain"])
                wide = lambda a: a[:].unsqueeze(2).broadcast_to([P, NT, E])
                lg = w.lg[:, :, 0:E]
                nc.vector.memset(one[:], 1.0)
                nc.vector.memset(cur[:], 0)
                nc.vector.memset(bit[:], 1 << (NBITS - 1))
                step(nc.vector.tensor_reduce(r1[:], lg, axis=AX, op=ALU.max))
                nc.vector.tensor_tensor(sc[:], lg, wide(r1), ALU.subtract).then_inc(s["lg"], 1)
                dve.wait_ge(s["ex"], 1)
                step(nc.vector.tensor_reduce(r1[:], sc[:], axis=AX, op=ALU.add))
                step(nc.vector.reciprocal(r1[:], r1[:]))
                split = lambda x: x.rearrange("p (i a) e -> p i a e", a=2)
                nc.vector.tensor_tensor(sp2[:].rearrange("p a i e -> p i a e"), split(sc[:]), split(wide(r1)), ALU.mult).then_inc(s["sc"], 1)
                dve.wait_ge(s["sT"], 1)
                with dve.Fori(0, NBITS) as it:
                    step.loop(it, 4)
                    step(nc.vector.tensor_tensor(cand[:], cur[:], bit[:], ALU.bitwise_or))
                    nc.vector.tensor_scalar(junk[:], sT[:], cand[:].bitcast(F32), None, ALU.is_ge, ALU.add,
                                            accum_out=cnt[:, 0:1]).then_inc(s["cnt"], 1)
                    dve.wait_ge(s["tot"], it + 1)
                    step(nc.vector.tensor_scalar(ok[:], p_c[:, 0:1], float(CAP), None, ALU.is_ge))
                    step.mark(nc.vector.tensor_scalar(bit[:], bit[:], 1, None, ALU.logical_shift_right))
                    step(nc.vector.copy_predicated(cur[:], ok[:], cand[:]))
                step.end(NBITS)
                thr = cur[:].bitcast(F32)
                nc.vector.tensor_scalar(gtm[:], sT[:], thr, None, ALU.is_gt, ALU.add, accum_out=cnt[:, 0:1])
                nc.vector.tensor_scalar(eqm[:], sT[:], thr, None, ALU.is_equal, ALU.add, accum_out=cnt[:, 1:2]).then_inc(s["cnt"], 1)
                dve.wait_ge(s["cnt"], NBITS + 1)
                step(nc.vector.tensor_tensor_scan(junk[:], one[:], eqm[:], 0.0, ALU.mult, ALU.add))
                dve.wait_ge(s["tot"], NBITS + 1)
                step(nc.vector.tensor_copy(off[:], p_c[:, 0:3]))
                step(nc.vector.tensor_tensor(off[:, 0:1], off[:, 0:1], off[:, 2:3], ALU.add))
                step(nc.vector.tensor_scalar(junk[:], junk[:], off[:, 0:1], float(CAP), ALU.add, ALU.is_le))
                step(nc.vector.tensor_tensor(eqm[:], eqm[:], junk[:], ALU.mult))
                step(nc.vector.tensor_tensor(gtm[:], gtm[:], eqm[:], ALU.add))
                nc.vector.tensor_tensor(gate[:], sT[:], gtm[:], ALU.mult).then_inc(s["gate"], 1)

            @block.scalar
            def _(act):
                act.wait_ge(s["lg"], 1)
                nc.scalar.activation(sc[:], sc[:], ACT.Exp).then_inc(s["ex"], 1)
                act.wait_ge(s["tr"], 1)
                nc.scalar.activation(sT[:], p_s[:, 0:256], ACT.Copy).then_inc(s["sT"], 1)

            @block.tensor
            def _(pe):
                pe.wait_ge(s["sc"], 1)
                for half in range(2):
                    src = sp2[:, half].rearrange("p i e -> p (i e)")
                    last = nc.tensor.transpose(p_s[:, half * P:(half + 1) * P], src, k.const("ident"))
                last.then_inc(s["tr"], 1)
                with pe.Fori(0, NBITS) as it:
                    pe.wait_ge(s["cnt"], it + 1)
                    nc.tensor.matmul(p_c[:, 0:1], k.const("same_e"), cnt[:, 0:1], start=True, stop=True).then_inc(s["tot"], 1)
                pe.wait_ge(s["cnt"], NBITS + 1)
                nc.tensor.matmul(p_c[:, 0:2], k.const("same_e"), cnt[:], start=True, stop=True)
                nc.tensor.matmul(p_c[:, 2:3], k.const("before_e"), cnt[:, 1:2], start=True, stop=True).then_inc(s["tot"], 1)


def phase_ffn1(k, w):
    nc, io = k.nc, k.io
    with ExitStack() as ctx:
        gate = k.sb(ctx, "gate1", [P, 2 * P])
        w1 = k.sb(ctx, "w1_1", [P, E, HID1])
        w2 = k.sb(ctx, "w2_1", [P, E, CH1, D])
        b1n = k.sb(ctx, "b1_nat", [E * CH1, P])
        b2n = k.sb(ctx, "b2_nat", [E, P])
        b1 = k.sb(ctx, "b1_1", [P, E * CH1])
        b2 = k.sb(ctx, "b2_1", [P, E])
        s = {n: k.sem("c1_" + n) for n in ("chain", "lg", "ex", "sc", "tr", "sT", "cnt", "tot", "gate")}
        phase_choose1(k, w, gate, s)
        s = {n: k.sem("g1_" + n) for n in ("w", "out", "tr", "b")}
        with ExitStack() as cb:
            p_b = k.ps(cb, "ps_b1", [P, 512])
            with nc.Block("biases1") as block:
                @block.sync
                def _(sp):
                    sp.dma_start(b1n[:], io["L1_ffn_b1"].rearrange("e (c p) -> (e c) p", p=P)).then_inc(s["w"], 16)
                    sp.dma_start(b2n[:], io["L1_ffn_b2"]).then_inc(s["w"], 16)
                    sp.dma_start(w1[:], io["L1_ffn_W1"].rearrange("e d h -> d e h")).then_inc(s["w"], 16)
                    for e in range(E):
                        sp.dma_start(w2[:, e], io["L1_ffn_W2"][e].rearrange("(c p) d -> p c d", p=P)).then_inc(s["w"], 16)
                    for i in range(16):
                        sp.dma_start(k.gates[:, i * 2 * P:(i + 1) * 2 * P], gate[8 * i:8 * i + 8, :]).then_inc(s["out"], 16)
                    sp.wait_ge(s["out"], 16 * 16)
                    sp.wait_ge(s["w"], 16 * (3 + E))

                @block.tensor
                def _(pe):
                    pe.wait_ge(s["w"], 16 * (3 + E))
                    nc.tensor.transpose(p_b[:, 0:E * CH1], b1n[:], k.const("ident")[0:E * CH1, 0:E * CH1])
                    nc.tensor.transpose(p_b[:, 64:64 + E], b2n[:], k.const("ident")[0:E, 0:E]).then_inc(s["tr"], 1)

                @block.vector
                def _(dve):
                    dve.wait_ge(s["tr"], 1)
                    nc.vector.tensor_copy(b1[:], p_b[:, 0:E * CH1])
                    nc.vector.tensor_copy(b2[:], p_b[:, 64:64 + E]).then_inc(s["b"], 1)

        NGB = 4
        gb = [k.sb(ctx, f"g1_gb{i}", [P, BLK]) for i in range(NGB)]
        hs = [k.sb(ctx, f"g1_hs{i}", [P, BLK]) for i in range(CH1)]
        pr = [k.sb(ctx, f"g1_pr{i}", [P, BLK]) for i in range(2)]
        acc = k.sb(ctx, "g1_acc", [P, BLK])
        p_h = [k.ps(ctx, f"ps_g1h{i}", [P, 512]) for i in range(CH1)]
        p_y = [k.ps(ctx, f"ps_g1y{i}", [P, 512]) for i in range(2)]
        p_t = k.ps(ctx, "ps_g1t", [P, 512])
        s = {n: k.sem("g1b_" + n) for n in ("h", "hs", "y", "pr", "acc", "tr", "x")}
        gbs = [k.sem(f"g1b_gate{i}") for i in range(NGB)]
        with nc.Block("experts1") as block:
            @block.sync
            def _(sp):
                sp.sem_inc(s["hs"], CH1)
                sp.sem_inc(s["pr"], NGB)
                sp.sem_inc(s["acc"], 2)
                sp.sem_inc(s["x"], 1)
                sp.sem_inc(s["tr"], 1)
                with sp.Fori(0, NB) as it:
                    for e in range(E):
                        sp.wait_ge(s["pr"], it * E + e + 1)
                        sp.dma_start(gb[e % NGB][:], k.gates[e:e + 1, bass.ds(it * BLK, BLK)].broadcast_to([P, BLK])).then_inc(gbs[e % NGB], 16)

            @block.tensor
            def _(pe):
                pe.sem_inc(s["y"], 1)
                with pe.Fori(0, NB) as it:
                    def up(e, c):
                        pe.wait_ge(s["hs"], (it * E + e) * CH1 + c + 1)
                        nc.tensor.matmul(p_h[c][:], w1[:, e, c * P:(c + 1) * P], k.xnT[:, bass.ds(it * BLK, BLK)],
                                         start=True, stop=True).then_inc(s["h"], 1)
                    for c in range(CH1):
                        up(0, c)
                    for e in range(E):
                        pe.wait_ge(s["pr"], it * E + e + NGB - 1)
                        for c in range(CH1):
                            pe.wait_ge(s["hs"], (it * E + e) * CH1 + c + 1 + CH1)
                            last = nc.tensor.matmul(p_y[e % 2][:], w2[:, e, c, :], hs[c][:], start=(c == 0), stop=(c == CH1 - 1))
                            if c == CH1 - 1:
                                last.then_inc(s["y"], 1)
                            if e + 1 < E:
                                up(e + 1, c)
                    pe.wait_ge(s["acc"], it * E + E + 2)
                    pe.wait_ge(s["x"], it + 1)
                    for u in range(U):
                        last = nc.tensor.transpose(p_t[:, u * P:(u + 1) * P], acc[:, u * P:(u + 1) * P], k.const("ident"))
                    last.then_inc(s["tr"], 1)

            @block.scalar
            def _(act):
                with act.Fori(0, NB) as it:
                    for e in range(E):
                        act.wait_ge(s["y"], it * E + e + 1)
                        for c in range(CH1):
                            act.wait_ge(s["h"], (it * E + e) * CH1 + c + 1)
                            nc.scalar.activation(hs[c][:], p_h[c][:], ACT.Gelu, bias=b1[:, e * CH1 + c:e * CH1 + c + 1]).then_inc(s["hs"], 1)

            @block.vector
            def _(dve):
                with dve.Fori(0, NB) as it:
                    for e in range(E):
                        dve.wait_ge(gbs[e % NGB], it * (16 * (E // NGB)) + 16 * (e // NGB + 1))
                        dve.wait_ge(s["y"], it * E + e + 2)
                        dve.wait_ge(s["acc"], it * E + max(e + 1, 2))
                        nc.vector.scalar_tensor_tensor(out=pr[e % 2][:], in0=p_y[e % 2][:], scalar=b2[:, e:e + 1], in1=gb[e % NGB][:],
                                                       op0=ALU.add, op1=ALU.mult).then_inc(s["pr"], 1)
                    dve.wait_ge(s["tr"], it + 2)
                    xv = k.x[:, bass.ds(it * U, U), :].rearrange("p a d -> p (a d)")
                    nc.vector.tensor_tensor(xv, xv, p_t[:], ALU.add).then_inc(s["x"], 1)

            @block.gpsimd
            def _(pool):
                with pool.Fori(0, NB) as it:
                    pool.wait_ge(s["tr"], it + 1)
                    pool.wait_ge(s["pr"], it * E + 2 + NGB)
                    nc.gpsimd.tensor_tensor(acc[:], pr[0][:], pr[1][:], ALU.add).then_inc(s["acc"], 2)
                    for e in range(2, E):
                        pool.wait_ge(s["pr"], it * E + e + 1 + NGB)
                        pool.wait_ge(s["acc"], it * E + e + 2)
                        nc.gpsimd.tensor_tensor(acc[:], acc[:], pr[e % 2][:], ALU.add).then_inc(s["acc"], 1)


MAX_GAP = 60.0


def build_layer1(k, stop, dbg):
    nc = k.nc
    k.parts = nc.dram_tensor("parts", [2, PARTS, P, TOK], BF16, kind="Internal").ap()
    k.rows = nc.dram_tensor("neg_rowmax", [H, TOK], BF16, kind="Internal").ap()
    with ExitStack() as l1:
        w = Weights1(k, l1)
        w.v1 = k.sb(l1, "v1b", [P, NT, H, HD + 1])
        k.rowmax = k.sb(l1, "rowmax", [P, NT, H])
        k.flag = k.sb(l1, "flag", [P, 1], I32)
        with ExitStack() as lr:
            w.qk = k.sb(lr, "qk1", [P, NT, 2 * D])
            with nc.Block("ones1") as block:
                @block.vector
                def _(dve):
                    nc.vector.memset(w.v1[:, :, :, HD:HD + 1], 1.0)
            phase_weights1(k, w)
            phase_project1(k, w)
            if dbg: dbg(nc, k, w, 4)
            if stop > 4:
                phase_rotary(k, w)
            if dbg: dbg(nc, k, w, 5)
        if stop > 5:
            with ExitStack() as la:
                ab = k.sb(la, "heads_out", [P, BATCH * NG * TB, G * HD])
                phase_maxima(k)
                phase_attention(k, w, ab)
                phase_out1(k, w, ab)
        if stop > 6:
            phase_ffn1(k, w)



def build(nc, io, out, stop=99, dbg=None):
    with ExitStack() as ctx:
        k = Kernel(nc, ctx, io)
        k.gates = nc.dram_tensor("gates", [E, TOK], F32, kind="Internal").ap()
        k.x_loaded = [k.sem(f"x_loaded{b}") for b in range(NB)]
        with ExitStack() as l0:
            w = Weights0(k, l0)
            with ExitStack() as la:
                w.v1 = k.sb(la, "v1", [P, NT, H, HD + 1])
                w.qk = k.sb(la, "qk0", [P, NT, 256])
                phase_weights0(k, w)
                phase_project0(k, w)
                if dbg: dbg(nc, k, w, 1)
                if stop > 1:
                    phase_linear_attention(k, w)
            if dbg: dbg(nc, k, w, 2)
            if stop > 2:
                phase_ffn0(k, w)
        if dbg: dbg(nc, k, w, 3)
        if stop > 3:
            build_layer1(k, stop, dbg)
        k.store(out)


def store(k, out):
    nc = k.nc
    with ExitStack() as ctx:
        stored = k.sem("stored")
        block = ctx.enter_context(nc.Block("store"))
        od = out.rearrange("b (t p) d -> p (b t) d", p=P)

        @block.sync
        def _(sp):
            for b in range(NB):
                sp.dma_start(od[:, U * b:U * b + U, :], k.x[:, U * b:U * b + U, :]).then_inc(stored, 16)
            sp.wait_ge(stored, 16 * NB)

Kernel.store = store


INPUTS = ['L0_attn_x', 'L0_attn_w_qkv', 'L0_attn_wq_map', 'L0_attn_bq_map', 'L0_attn_wk_map', 'L0_attn_bk_map',
          'L0_attn_w_out', 'L0_ffn_gate_w', 'L0_ffn_w1', 'L0_ffn_b1', 'L0_ffn_w2', 'L0_ffn_b2', 'L0_ffn_w3', 'L0_ffn_b3',
          'L0_ffn_sw1', 'L0_ffn_sw2', 'L0_ffn_sw3', 'L1_attn_qn_w', 'L1_attn_qn_b', 'L1_attn_q_w', 'L1_attn_q_b',
          'L1_attn_kvn_w', 'L1_attn_kvn_b', 'L1_attn_kv_w', 'L1_attn_kv_b', 'L1_attn_out_w', 'L1_attn_out_b',
          'L1_attn_ln_w', 'L1_attn_ln_b', 'L1_attn_rh_w', 'L1_attn_rh_b', 'L1_ffn_Wr', 'L1_ffn_W1', 'L1_ffn_b1',
          'L1_ffn_W2', 'L1_ffn_b2']


def kernel(**inputs):
    import concourse.bacc as bacc
    from concourse.bass_utils import run_bass_kernel_spmd

    nc = bacc.Bacc("TRN2", target_bir_lowering=False, num_devices=1)
    given = {n: np.ascontiguousarray(inputs[n]) for n in INPUTS}
    given["consts"] = constants()
    io = {n: nc.dram_tensor(f"in_{n}", a.shape, mybir.dt.from_np(a.dtype), kind="ExternalInput").ap() for n, a in given.items()}
    out = nc.dram_tensor("out", (BATCH, SEQ, D), F32, kind="ExternalOutput").ap()
    build(nc, io, out)
    r = run_bass_kernel_spmd(nc, [{f"in_{n}": a for n, a in given.items()}], core_ids=[0])
    return r.results[0]["out"]
```

```python
from contextlib import ExitStack

import numpy as np

import concourse.bass as bass
from concourse import mybir

ALU = mybir.AluOpType
ACT = mybir.ActivationFunctionType
F32 = mybir.dt.float32
BF16 = mybir.dt.bfloat16
I32 = mybir.dt.int32
AX = mybir.AxisListType.X

P = 128
D = 128
BATCH, SEQ = 4, 1024
TOK = BATCH * SEQ
NT = TOK // P
U = 4
BLK = U * P
NB = TOK // BLK
TB = SEQ // P
H, HD = 16, 8
E = 8
HID0 = 128
ISH = 256
HID1 = 512
CH1 = HID1 // P
CAP = TOK * 2 // E
EPS = 1e-5
G = 4
NG = H // G
PARTS = 3
SR = PARTS * PARTS * HD

CONST = {}
_w = 0
for _name, _n in (("ident", P), ("causal", P), ("blk8", P), ("rep8", P), ("same_e", P), ("before_e", P),
                  ("kvmask", 72), ("of_head", P // 16), ("tri", E * E), ("keep", NT), ("cos", TB * 4), ("sin", TB * 4)):
    CONST[_name] = (_w, _w + _n)
    _w += _n
NCONST = _w


def constants():
    c = np.zeros((P, NCONST), np.float32)
    p = np.arange(P)

    def put(name, a):
        lo, hi = CONST[name]
        c[: a.shape[0], lo:hi] = a

    put("ident", np.eye(P))
    put("causal", p[:, None] <= p[None, :])
    put("blk8", p[:, None] // HD == p[None, :] // HD)
    put("rep8", np.arange(HD)[:, None] == p[None, :] % HD)
    put("same_e", p[:, None] % E == p[None, :] % E)
    put("before_e", (p[:, None] % E == p[None, :] % E) & (p[:, None] // E < p[None, :] // E))
    put("kvmask", p[:, None] // 16 == np.arange(72)[None, :] // 9)
    put("of_head", p[:, None] // 16 == np.arange(P // 16)[None, :])
    e = np.arange(E)
    put("tri", np.broadcast_to((e[None, :] < e[:, None]).reshape(1, -1), (P, E * E)))
    put("keep", np.broadcast_to((np.arange(1, NT + 1) % TB != 0)[None, :], (P, NT)))
    d2 = HD // 2
    mel_max = 2595.0 * np.log10(1.0 + 4000.0 / 200.0)
    lin = np.linspace(0.0, mel_max, d2, dtype=np.float32)
    scale = np.power(np.float32(10.0), lin / np.float32(2595.0)).astype(np.float32) - np.float32(1.0)
    fb = (np.float32(200.0) * scale / np.float32(1000.0)).astype(np.float32)
    fr = np.arange(SEQ, dtype=np.float32)[:, None] * fb[None, :]
    lay = lambda a: a.reshape(TB, P, d2).transpose(1, 0, 2).reshape(P, TB * d2)
    put("cos", lay(np.cos(fr)))
    put("sin", lay(np.sin(fr)))
    return c


class Steps:

    def __init__(self, eng, sem):
        self.eng, self.sem, self.base, self.n = eng, sem, 0, 0

    def __call__(self, ins):
        self.mark(ins)
        self.eng.wait_ge(self.sem, self.base + self.n)

    def mark(self, ins):
        self.n += 1
        ins.then_inc(self.sem, 1)

    def loop(self, it, per):
        self.start, self.per = self.base + self.n, per
        self.base, self.n = it * per + self.start, 0

    def end(self, count):
        assert self.n == self.per, (self.n, self.per)
        self.base, self.n = self.start + count * self.per, 0


def tiles_of(big, it, n=U):
    return big[:, bass.ds(it * n, n)]


class Kernel:

    def __init__(self, nc, ctx, io):
        self.nc, self.ctx, self.io = nc, ctx, io
        self.sems = []
        self.x = self.sb(ctx, "x_res", [P, NT, D])
        self.xnT = self.sb(ctx, "xnT", [P, TOK])
        self.cst = self.sb(ctx, "cst", [P, NCONST])
        self.eps = self.sb(ctx, "eps", [P, 1])
        self.mean_var = self.sb(ctx, "mean_var", [P, NT, 2])

    def sb(self, ctx, name, shape, dt=F32):
        return ctx.enter_context(self.nc.sbuf_tensor(name, shape, dt))

    def ps(self, ctx, name, shape, dt=F32):
        return ctx.enter_context(self.nc.psum_tensor(name, shape, dt))

    def sem(self, name):
        self.sems.append(self.nc.alloc_semaphore(name=name))
        return self.sems[-1]

    def clear_sems(self):
        self.nc.clear_and_free_semaphores(self.sems)
        self.sems = []
        self.nc.all_engine_barrier()

    def const(self, name, rows=P):
        lo, hi = CONST[name]
        return self.cst[0:rows, lo:hi]


def rows_of(vec, n):
    return vec.partition_broadcast(n)


def phase_weights0(k, w):
    nc, io = k.nc, k.io
    with ExitStack() as ctx:
        wqkv = k.sb(ctx, "wqkv_nat", [P, 3, D])
        maps = k.sb(ctx, "maps_nat", [HD, 2, HD])
        wexp = k.sb(ctx, "wexp_nat", [P, 3 * E, D])
        wsh = k.sb(ctx, "wsh_nat", [P, 6, D])
        wo = k.sb(ctx, "wo_nat", [P, D])
        small = k.sb(ctx, "small_nat", [32, D])
        bd = k.sb(ctx, "bd", [P, 2, D])
        pst = k.ps(ctx, "ps_w0", [P, 8, 512])
        loaded, tr_done, copied, bd_done = (k.sem(n) for n in ("w0_loaded", "w0_tr", "w0_copied", "w0_bd"))
        xl = k.x_loaded
        block = ctx.enter_context(nc.Block("weights0"))

        groups = [([wexp[:, 4 * j + i, :] for i in range(4)], w.expT[:, 4 * j:4 * j + 4, :]) for j in range(6)]
        groups.append(([wsh[:, i, :] for i in range(4)], w.shT[:, 0:4, :]))
        groups.append(([wsh[:, 4, :], wsh[:, 5, :], wo[:], wqkv[:, 2, :]], None))

        @block.sync
        def _(sp):
            sp.dma_start(k.cst[:], io["consts"]).then_inc(loaded, 16)
            sp.dma_start(wqkv[:], io["L0_attn_w_qkv"].rearrange("(t p) d -> p t d", p=P)).then_inc(loaded, 16)
            for i, n in enumerate(("L0_attn_wq_map", "L0_attn_wk_map")):
                with nc.allow_non_contiguous_dma("eight by eight"):
                    sp.dma_start(maps[:, i, :], io[n].rearrange("e d -> d e")).then_inc(loaded, 16)
            for i, n in enumerate(("L0_attn_bq_map", "L0_attn_bk_map")):
                sp.dma_start(w.map_bias[:, i, :], rows_of(io[n], P)).then_inc(loaded, 16)
            for i, n in enumerate(("L0_ffn_w1", "L0_ffn_w2", "L0_ffn_w3")):
                sp.dma_start(wexp[:, i * E:(i + 1) * E, :], io[n].rearrange("e h d -> h e d")).then_inc(loaded, 16)
            for i, n in enumerate(("L0_ffn_sw1", "L0_ffn_sw2")):
                sp.dma_start(wsh[:, 2 * i:2 * i + 2, :], io[n].rearrange("(c p) d -> p c d", p=P)).then_inc(loaded, 16)
            sp.dma_start(wsh[:, 4:6, :], io["L0_ffn_sw3"].rearrange("d (c p) -> d c p", p=P)).then_inc(loaded, 16)
            sp.dma_start(wo[:], io["L0_attn_w_out"]).then_inc(loaded, 16)
            for i, n in enumerate(("L0_ffn_b1", "L0_ffn_b2", "L0_ffn_b3", "L0_ffn_gate_w")):
                sp.dma_start(small[i * E:(i + 1) * E, :], io[n]).then_inc(loaded, 16)

        @block.scalar
        def _(act):
            xd = io["L0_attn_x"].rearrange("b (t p) d -> p (b t) d", p=P)
            for b in range(NB):
                act.dma_start(k.x[:, U * b:U * b + U, :], xd[:, U * b:U * b + U, :]).then_inc(xl[b], 16)

        n_loads = 17

        @block.tensor
        def _(pe):
            pe.wait_ge(loaded, 16 * n_loads)
            ident = k.const("ident")
            for g, (srcs, _) in enumerate(groups):
                for i, s in enumerate(srcs):
                    last = nc.tensor.transpose(pst[:, g, i * P:(i + 1) * P], s, ident)
                last.then_inc(tr_done, 1)
            pe.wait_ge(copied, 1)
            nc.tensor.transpose(pst[:, 0, 0:32], small[:], ident[0:32, 0:32])
            for i in range(2):
                last = nc.tensor.matmul(pst[:, 0, 64 + 8 * i:72 + 8 * i], k.const("rep8", HD), maps[:, i, :],
                                        start=True, stop=True)
            last.then_inc(tr_done, 1)
            pe.wait_ge(bd_done, 1)
            for i in range(2):
                last = nc.tensor.matmul(pst[:, 1, i * P:(i + 1) * P], wqkv[:, i, :], bd[:, i, :], start=True, stop=True)
            last.then_inc(tr_done, 1)

        @block.vector
        def _(dve):
            nc.vector.memset(k.eps[:], EPS)
            nc.vector.memset(w.v1[:, :, :, HD:HD + 1], 1.0)
            for g, (_, dst) in enumerate(groups):
                dve.wait_ge(tr_done, g + 1)
                if dst is not None:
                    nc.vector.tensor_copy(dst.rearrange("p a b -> p (a b)"), pst[:, g, :]).then_inc(copied, 1)
                else:
                    nc.vector.tensor_copy(w.shT[:, 4:6, :].rearrange("p a b -> p (a b)"), pst[:, g, 0:256])
                    nc.vector.tensor_copy(w.outT[:], pst[:, g, 256:384])
                    nc.vector.tensor_copy(w.proj[:, 256:384], pst[:, g, 384:512])
            dve.wait_ge(tr_done, len(groups) + 1)
            nc.vector.tensor_copy(w.bias[:], pst[:, 0, 0:24])
            nc.vector.tensor_copy(w.proj[:, 384:392], pst[:, 0, 24:32])
            for i in range(2):
                blk = k.const("blk8").rearrange("p (h e) -> p h e", e=HD)
                rep = pst[:, 0, 64 + 8 * i:72 + 8 * i].unsqueeze(1).broadcast_to([P, H, HD])
                ins = nc.vector.tensor_tensor(bd[:, i, :].rearrange("p (h e) -> p h e", e=HD), rep, blk, ALU.mult)
            ins.then_inc(bd_done, 1)
            dve.wait_ge(tr_done, len(groups) + 2)
            nc.vector.tensor_copy(w.proj[:, 0:256], pst[:, 1, 0:256])


def steps(eng, count, body, after=0):
    for t in range(2):
        body(t, t % 2, lambda n, t=t: t + n >= 0)
    with eng.Fori(0, (count - 4) // 2) as it:
        for u in range(2):
            body(it * 2 + (2 + u), u, lambda n: True)
    for t in range(count - 2, count + after):
        body(t, t % 2, lambda n, t=t: t + n < count)


def row_statistics(k, dve, step, st, mv):
    nc = k.nc
    with dve.Fori(0, NB) as it:
        step.loop(it, 3)
        for u in range(U):
            nc.vector.bn_stats(st[:, u, :], k.x[:, bass.ds(it * U + u, 1), :].rearrange("p a d -> p (a d)"))
        step(nc.vector.memset(mv[:, U, 0:1], 0.0))
        nc.vector.memset(mv[:, U, 1:2], 0.0)
        for u in range(U):
            last = nc.vector.bn_aggr(mv[:, u, :], st[:, u, :])
        step(last)
        step(nc.vector.tensor_copy(k.mean_var[:, bass.ds(it * U, U), :], mv[:, 0:U, :]))
    step.end(NB)


def phase_project(k, w, layer):
    nc = k.nc
    W = 2
    NU = NT // W
    NL = (E, E + 1)[layer]
    with ExitStack() as ctx:
        n = f"p{layer}_"
        st = k.sb(ctx, n + "st", [P, U, 6])
        mv = k.sb(ctx, n + "mv", [P, U + 1, 2])
        sd = k.sb(ctx, n + "sd", [P, NT])
        rs = k.sb(ctx, n + "rs", [P, NT])
        rs2 = k.sb(ctx, n + "rs2", [P, NT])
        xn = [k.sb(ctx, f"{n}xn{i}", [P, W, D]) for i in range(2)]
        xt = [k.sb(ctx, f"{n}xt{i}", [P, W * P]) for i in range(2)]
        ps_t = [k.ps(ctx, f"ps_{n}t{i}", [P, 512]) for i in range(2)]
        ps_q = [k.ps(ctx, f"ps_{n}q{i}", [P, W, 512]) for i in range(2)]
        s = {m: k.sem(n + m) for m in ("chain", "var", "sd", "var2", "sd2", "normed", "turned", "xt", "proj", "qkv", "kept")}
        with nc.Block(f"project{layer}") as block:

            @block.vector
            def _(dve):
                step = Steps(dve, s["chain"])
                if layer == 0:
                    for b in range(NB):
                        dve.wait_ge(k.x_loaded[b], 16)
                row_statistics(k, dve, step, st, mv)
                dve.sem_inc(s["var"], 1)
                dve.wait_ge(s["sd"], 1)
                step(nc.vector.reciprocal(rs[:], sd[:]))
                if layer == 1:
                    step(nc.vector.tensor_tensor(rs2[:], k.mean_var[:, :, 1], rs[:], ALU.mult))
                    nc.vector.tensor_tensor(rs2[:], rs2[:], rs[:], ALU.mult).then_inc(s["var2"], 1)
                    dve.wait_ge(s["sd2"], 1)
                    step(nc.vector.reciprocal(rs2[:], rs2[:]))

                def norm(t, u):
                    dve.wait_ge(s["turned"], t + 1)
                    for i in range(W):
                        last = nc.vector.tensor_scalar(xn[u][:, i, :], k.x[:, bass.ds(t * W + i, 1), :].rearrange("p a d -> p (a d)"),
                                                       k.mean_var[:, bass.ds(t * W + i, 1), 0], rs[:, bass.ds(t * W + i, 1)],
                                                       ALU.subtract, ALU.mult)
                    last.then_inc(s["normed"], 1)

                def body(t, u, has):
                    if has(2):
                        norm(t + 2, u)
                    dve.wait_ge(s["proj"], t + 3)
                    if layer == 0:
                        for i in range(2):
                            last = nc.vector.tensor_tensor(
                                w.qk[:, bass.ds(t * W, W), i * P:(i + 1) * P].rearrange("p a (h e) -> p a h e", e=HD),
                                ps_q[u][:, :, i * P:(i + 1) * P].rearrange("p a (h e) -> p a h e", e=HD),
                                w.map_bias[:, i, :].unsqueeze(1).unsqueeze(1).broadcast_to([P, W, H, HD]), ALU.add)
                    else:
                        for i in range(W):
                            tok = rs2[:, bass.ds(t * W + i, 1)]
                            nc.vector.scalar_tensor_tensor(
                                out=w.qk[:, bass.ds(t * W + i, 1), :].rearrange("p a c -> p (a c)"), in0=ps_q[u][:, i, 0:2 * D],
                                scalar=tok, in1=w.bias[:, 0:2 * D], op0=ALU.mult, op1=ALU.add)
                            heads = lambda a: a.rearrange("p (h e) -> p h e", e=HD)
                            last = nc.vector.scalar_tensor_tensor(
                                out=w.v1[:, bass.ds(t * W + i, 1), :, 0:HD].rearrange("p a h e -> p (a h) e"),
                                in0=heads(ps_q[u][:, i, 2 * D:3 * D]), scalar=tok, in1=heads(w.bias[:, 2 * D:3 * D]),
                                op0=ALU.mult, op1=ALU.add)
                    last.then_inc(s["qkv"], 1)

                norm(0, 0)
                norm(1, 1)
                steps(dve, NU, body)

            @block.scalar
            def _(act):
                act.wait_ge(s["var"], 1)
                nc.scalar.activation(sd[:], k.mean_var[:, :, 1], ACT.Sqrt, bias=k.eps[:]).then_inc(s["sd"], 1)
                if layer == 1:
                    act.wait_ge(s["var2"], 1)
                    nc.scalar.activation(rs2[:], rs2[:], ACT.Sqrt, bias=k.eps[:]).then_inc(s["sd2"], 1)

                def keep_xt(t, u):
                    act.wait_ge(s["turned"], t + 3)
                    act.wait_ge(s["proj"], t + 1)
                    nc.scalar.activation(xt[u][:], ps_t[u][:, 0:W * P], ACT.Copy)
                    nc.scalar.activation(k.xnT[:, bass.ds(t * (W * P), W * P)], ps_t[u][:, 0:W * P], ACT.Copy).then_inc(s["xt"], 1)

                def body(t, u, has):
                    if has(1):
                        keep_xt(t + 1, 1 - u)
                    act.wait_ge(s["qkv"], t + 1)
                    if layer == 0:
                        nc.scalar.activation(w.v1[:, bass.ds(t * W, W), :, 0:HD],
                                             ps_q[u][:, :, 2 * D:3 * D].rearrange("p a (h e) -> p a h e", e=HD), ACT.Copy)
                    nc.scalar.activation(w.logits[:, bass.ds(t * W, W), :], ps_q[u][:, :, 3 * D:3 * D + NL], ACT.Copy).then_inc(s["kept"], 1)

                keep_xt(0, 0)
                steps(act, NU, body)

            @block.tensor
            def _(pe):
                def turn(t, u):
                    pe.wait_ge(s["normed"], t + 1)
                    pe.wait_ge(s["xt"], t + 1)
                    for i in range(W):
                        last = nc.tensor.transpose(ps_t[u][:, i * P:(i + 1) * P], xn[u][:, i, :], k.const("ident"))
                    last.then_inc(s["turned"], 1)

                def body(t, u, has):
                    if has(1):
                        turn(t + 1, 1 - u)
                    pe.wait_ge(s["xt"], t + 3)
                    pe.wait_ge(s["kept"], t + 1)
                    for i in range(W):
                        last = nc.tensor.matmul(ps_q[u][:, i, 0:3 * D + NL], xt[u][:, i * P:(i + 1) * P], w.proj[:], start=True, stop=True)
                    last.then_inc(s["proj"], 1)

                turn(0, 0)
                steps(pe, NU, body)

            @block.gpsimd
            def _(pool):
                for m in ("turned", "xt", "proj", "kept"):
                    pool.sem_inc(s[m], 2)


def phase_linear_attention(k, w):
    nc = k.nc
    with ExitStack() as ctx:
        S2 = range(2)
        mm = [k.sb(ctx, f"la_mm{s}", [P, 2, 32]) for s in S2]
        dd = [k.sb(ctx, f"la_dd{s}", [P, 32, 2, HD]) for s in S2]
        ee = [k.sb(ctx, f"la_ee{s}", [P, 64, HD]) for s in S2]
        sm = [k.sb(ctx, f"la_sm{s}", [P, 2, 64]) for s in S2]
        ff = [k.sb(ctx, f"la_ff{s}", [P, 64, HD]) for s in S2]
        vs = [k.sb(ctx, f"la_vs{s}", [P, H, HD + 1]) for s in S2]
        qT = [k.sb(ctx, f"la_qT{s}", [P, 256]) for s in S2]
        kT = [k.sb(ctx, f"la_kT{s}", [P, 8, 256]) for s in S2]
        am = [k.sb(ctx, f"la_am{s}", [P, 4, 4, P]) for s in S2]
        run = [k.sb(ctx, f"la_run{s}", [P, NG, G, 32]) for s in S2]
        add = k.sb(ctx, "la_add", [P, 2, 72])
        oT = [k.sb(ctx, f"la_oT{s}", [P, 512]) for s in S2]
        den = [k.sb(ctx, f"la_den{s}", [P, 2, H]) for s in S2]
        y = [k.sb(ctx, f"la_y{s}", [P, D]) for s in S2]
        yT = [k.sb(ctx, f"la_yT{s}", [P, D]) for s in S2]
        p_ft = k.ps(ctx, "ps_ft", [P, 512])
        p_a = k.ps(ctx, "ps_a", [P, 3, 512])
        p_o = k.ps(ctx, "ps_o", [P, 512])
        p_ds = k.ps(ctx, "ps_ds", [P, 512])
        p_y = k.ps(ctx, "ps_y", [P, 512])
        p_r = k.ps(ctx, "ps_r", [P, 512])
        bank_of = [0, 1, 2, 0, 1, 2, 0, 2]
        names = ("mm", "dd", "ee", "ff", "vs", "ft", "ds", "kt", "a", "am", "o", "ot", "otT", "run", "y", "yt", "yts", "pr", "x",
                 "sum", "rs", "add", "den", "rden")
        s = {n: k.sem("la_" + n) for n in names}
        block = ctx.enter_context(nc.Block("linear_attention"))

        def tile(big, t):
            return big[:, bass.ds(t, 1)]

        @block.vector
        def _(dve):
            for u in S2:
                last = nc.vector.memset(run[u][:], 0.0)
            last.then_inc(s["run"], 1)
            dve.wait_ge(s["run"], 1)

            def link(name, ins, t):
                ins.then_inc(s[name], 1)
                dve.wait_ge(s[name], t + 1)

            def maxima(t, u):
                src = tile(w.qk, t).rearrange("p a (g e) -> p (a g) e", e=HD)
                dve.wait_ge(s["dd"], t + 1)
                nc.vector.tensor_reduce(mm[u][:, 0, :], src, axis=AX, op=ALU.max)
                nc.vector.tensor_reduce(mm[u][:, 1, :], src, axis=AX, op=ALU.min).then_inc(s["mm"], 1)

            def features(t, u):
                dve.wait_ge(s["ee"], t + 1)
                link("sum", nc.vector.tensor_reduce(sm[u][:, 0, :], ee[u][:], axis=AX, op=ALU.add), t)
                link("rs", nc.vector.reciprocal(sm[u][:, 1, :], sm[u][:, 0, :]), t)
                nc.vector.tensor_tensor(ff[u][:], ee[u][:], sm[u][:, 1, :].unsqueeze(2).broadcast_to([P, 64, HD]),
                                        ALU.mult).then_inc(s["ff"], 1)

            def mask(t, u, b):
                dve.wait_ge(s["a"], t * 4 + b + 1)
                nc.vector.tensor_tensor(am[u][:, b], p_a[:, bank_of[4 * u + b], :].rearrange("p (a t) -> p a t", a=4),
                                        k.const("causal").unsqueeze(1).broadcast_to([P, 4, P]), ALU.mult).then_inc(s["am"], 1)

            def running(t, u):
                dve.wait_ge(s["ds"], t + 1)
                keep = k.cst[:, bass.ds(t + CONST["keep"][0], 1)]
                link("add", nc.vector.scalar_tensor_tensor(
                    out=add[:], in0=p_ds[:, 0:144].rearrange("p (a c) -> p a c", a=2), scalar=keep,
                    in1=k.const("kvmask").unsqueeze(1).broadcast_to([P, 2, 72]), op0=ALU.mult, op1=ALU.mult), t)
                dve.wait_ge(s["o"], t + 2)
                heads = lambda a: a[:].rearrange("p g j c -> p (g j) c")[:, :, 0:HD + 1]
                nc.vector.scalar_tensor_tensor(out=heads(run[1 - u]), in0=heads(run[u]), scalar=keep,
                                               in1=add[:].rearrange("p a (j c) -> p (a j) c", c=HD + 1),
                                               op0=ALU.mult, op1=ALU.add).then_inc(s["run"], 1)

            def divide(t, u):
                dve.wait_ge(s["otT"], t + 1)
                o = p_y[:].rearrange("p (h c) -> p h c", c=32)
                link("den", nc.vector.tensor_scalar(den[u][:, 0, :], o[:, :, HD], 1e-6, None, ALU.max), t)
                link("rden", nc.vector.reciprocal(den[u][:, 1, :], den[u][:, 0, :]), t)
                nc.vector.tensor_tensor(y[u][:].rearrange("p (h c) -> p h c", c=HD), o[:, :, 0:HD],
                                        den[u][:, 1, :].unsqueeze(2).broadcast_to([P, H, HD]), ALU.mult).then_inc(s["y"], 1)

            def residual(t):
                dve.wait_ge(s["pr"], t + 1)
                xt = tile(k.x, t).rearrange("p a d -> p (a d)")
                nc.vector.tensor_tensor(xt, xt, p_r[:, 0:P], ALU.add).then_inc(s["x"], 1)

            def body(t, u, has):
                if has(0):
                    mask(t, u, 0)
                    mask(t, u, 1)
                if has(1):
                    features(t + 1, 1 - u)
                if has(0):
                    mask(t, u, 2)
                    mask(t, u, 3)
                if has(-2):
                    residual(t - 2)
                if has(-1):
                    divide(t - 1, 1 - u)
                if has(0):
                    running(t, u)
                if has(2):
                    maxima(t + 2, u)

            maxima(0, 0)
            features(0, 0)
            maxima(1, 1)
            steps(dve, NT, body, 2)

        @block.gpsimd
        def _(pool):
            pool.sem_inc(s["dd"], 2)

            def body(t, u):
                src = tile(w.qk, t).rearrange("p a (g e) -> p (a g) e", e=HD)
                pool.wait_ge(s["mm"], t + 1)
                nc.gpsimd.tensor_tensor(dd[u][:, :, 0, :], src, mm[u][:, 0, :].unsqueeze(2).broadcast_to([P, 32, HD]), ALU.subtract)
                nc.gpsimd.tensor_tensor(dd[u][:, :, 1, :], mm[u][:, 1, :].unsqueeze(2).broadcast_to([P, 32, HD]), src,
                                        ALU.subtract).then_inc(s["dd"], 1)
                pool.wait_ge(s["o"], t + 1)
                nc.gpsimd.tensor_copy(vs[u][:], tile(w.v1, t).rearrange("p a h c -> p (a h) c")).then_inc(s["vs"], 1)

            with pool.Fori(0, NT // 2) as it:
                for u in S2:
                    body(it * 2 + u, u)

        @block.scalar
        def _(act):
            def exps(t, u):
                act.wait_ge(s["dd"], t + 3)
                act.wait_ge(s["ff"], t + 1)
                nc.scalar.activation(ee[u][:], dd[u][:].rearrange("p g a e -> p (g a) e"), ACT.Exp).then_inc(s["ee"], 1)

            def turned(t, u):
                act.wait_ge(s["ft"], t + 1)
                nc.scalar.activation(qT[u][:], p_ft[:, 0:256], ACT.Copy)
                for i in range(8):
                    last = nc.scalar.activation(kT[u][:, i, :], p_ft[:, 256:512], ACT.Copy, scale=k.const("of_head")[:, i:i + 1])
                last.then_inc(s["kt"], 1)

            def body(t, u, has):
                if has(1):
                    turned(t + 1, 1 - u)
                if has(0):
                    act.wait_ge(s["o"], t + 3)
                    nc.scalar.activation(oT[u][:], p_o[:], ACT.Copy).then_inc(s["ot"], 1)
                if has(2):
                    exps(t + 2, u)
                if has(-1):
                    act.wait_ge(s["yt"], t)
                    nc.scalar.activation(yT[1 - u][:], p_r[:, P:2 * P], ACT.Copy).then_inc(s["yts"], 1)

            exps(0, 0)
            turned(0, 0)
            exps(1, 1)
            steps(act, NT, body, 2)

        @block.tensor
        def _(pe):
            pe.sem_inc(s["o"], 2)
            ident = k.const("ident")

            def turn_features(t, u):
                pe.wait_ge(s["ff"], t + 3)
                pe.wait_ge(s["kt"], t + 1)
                for i in range(4):
                    last = nc.tensor.transpose(p_ft[:, i * P:(i + 1) * P],
                                               ff[u][:, 16 * i:16 * i + 16, :].rearrange("p g e -> p (g e)"), ident)
                last.then_inc(s["ft"], 1)

            def share(t, u):
                pe.wait_ge(s["vs"], t + 1)
                pe.wait_ge(s["run"], t + 1)
                for i in range(2):
                    last = nc.tensor.matmul(p_ds[:, 72 * i:72 * i + 72],
                                            ff[u][:, 32 + 16 * i:48 + 16 * i, :].rearrange("p g e -> p (g e)"),
                                            vs[u][:, 8 * i:8 * i + 8, :].rearrange("p h c -> p (h c)"), start=True, stop=True)
                last.then_inc(s["ds"], 1)

            def products(t, u):
                pe.wait_ge(s["kt"], t + 2)
                for b in range(4):
                    bank = bank_of[4 * u + b]
                    back = next(n for n in range(1, 9) if bank_of[4 * u + b - n] == bank)
                    pe.wait_ge(s["am"], t * 4 + (b - back + 5))
                    for half in range(2):
                        for par in range(2):
                            i = half * 2 + par
                            last = nc.tensor.matmul(p_a[:, bank, i * P:(i + 1) * P],
                                                    kT[u][:, 2 * b + par, half * P:half * P + P],
                                                    qT[u][:, half * P:half * P + P], start=True, stop=True)
                    last.then_inc(s["a"], 1)

            def before(t, u):
                pe.wait_ge(s["run"], t + 1)
                pe.wait_ge(s["ot"], t + 1)
                for g in range(NG):
                    nc.tensor.matmul(p_o[:, g * P:(g + 1) * P], run[u][:, g].rearrange("p j c -> p (j c)"),
                                     qT[u][:, (g // 2) * P:(g // 2) * P + P], start=(g == 0), stop=False, skip_group_check=True)

            def inside(t, u):
                pe.wait_ge(s["am"], t * 4 + 8)
                for g in range(NG):
                    for j in range(G):
                        h = g * G + j
                        last = nc.tensor.matmul(p_o[32 * j:32 * j + HD + 1, g * P:(g + 1) * P], vs[u][:, h, :],
                                                am[u][:, (h % 8) // 2, (h // 8) * 2 + h % 2, :], start=False,
                                                stop=(g == NG - 1), skip_group_check=True, tile_position=(0, 32 * j))
                last.then_inc(s["o"], 1)

            def body(t, u, has):
                if has(0):
                    products(t, u)
                if has(-2):
                    pe.wait_ge(s["yts"], t - 1)
                    nc.tensor.matmul(p_r[:, 0:P], yT[u][:], w.outT[:], start=True, stop=True).then_inc(s["pr"], 1)
                if has(1):
                    turn_features(t + 1, 1 - u)
                if has(0):
                    before(t, u)
                if has(-1):
                    pe.wait_ge(s["ot"], t + 1)
                    pe.wait_ge(s["y"], t)
                    for g in range(NG):
                        last = nc.tensor.transpose(p_y[:, g * P:(g + 1) * P], oT[1 - u][:, g * P:(g + 1) * P], ident)
                    last.then_inc(s["otT"], 1)
                if has(0):
                    inside(t, u)
                if has(1):
                    share(t + 1, 1 - u)
                if has(-1):
                    pe.wait_ge(s["y"], t + 1)
                    pe.wait_ge(s["x"], t)
                    nc.tensor.transpose(p_r[:, P:2 * P], y[1 - u][:], ident).then_inc(s["yt"], 1)

            turn_features(0, 0)
            share(0, 0)
            steps(pe, NT, body, 2)

        @block.sync
        def _(sp):
            for n, c in (("ff", 2), ("kt", 1), ("x", 1), ("am", 4), ("ot", 1), ("y", 1)):
                sp.sem_inc(s[n], c)


def phase_ffn0(k, w):
    nc, io = k.nc, k.io
    with ExitStack() as ctx:
        sc = k.sb(ctx, "f0_sc", [P, NT, E])
        r1 = k.sb(ctx, "f0_r1", [P, NT])
        gt = k.sb(ctx, "f0_gt", [P, NT, E, E])
        eq = k.sb(ctx, "f0_eq", [P, NT, E, E])
        rank = k.sb(ctx, "f0_rank", [P, NT, E])
        gT = k.sb(ctx, "f0_gT", [P, 2, P])
        p_g = k.ps(ctx, "ps_f0g", [P, 512])
        s = {n: k.sem("f0_" + n) for n in ("chain", "lg", "ex", "g", "gt", "gts", "gd")}
        with nc.Block("route0") as block:
            @block.vector
            def _(dve):
                step = Steps(dve, s["chain"])
                lg = w.logits
                wide = lambda a: a[:].unsqueeze(2).broadcast_to([P, NT, E])
                step(nc.vector.tensor_reduce(r1[:], lg[:], axis=AX, op=ALU.max))
                nc.vector.tensor_tensor(lg[:], lg[:], wide(r1), ALU.subtract).then_inc(s["lg"], 1)
                dve.wait_ge(s["ex"], 1)
                step(nc.vector.tensor_reduce(r1[:], sc[:], axis=AX, op=ALU.add))
                step(nc.vector.reciprocal(r1[:], r1[:]))
                step(nc.vector.tensor_tensor(sc[:], sc[:], wide(r1), ALU.mult))
                of_j = sc[:].unsqueeze(2).broadcast_to([P, NT, E, E])
                of_e = sc[:].unsqueeze(3).broadcast_to([P, NT, E, E])
                nc.vector.tensor_tensor(gt[:], of_j, of_e, ALU.is_gt)
                step(nc.vector.tensor_tensor(eq[:], of_j, of_e, ALU.is_equal))
                flat = lambda a: a[:].rearrange("p t e j -> p t (e j)")
                step(nc.vector.tensor_tensor(flat(eq), flat(eq), k.const("tri").unsqueeze(1).broadcast_to([P, NT, E * E]), ALU.mult))
                step(nc.vector.tensor_tensor(flat(gt), flat(gt), flat(eq), ALU.add))
                step(nc.vector.tensor_reduce(rank[:], gt[:], axis=AX, op=ALU.add))
                step(nc.vector.tensor_scalar(rank[:], rank[:], 2.0, None, ALU.is_lt))
                step(nc.vector.tensor_tensor(sc[:], sc[:], rank[:], ALU.mult))
                step(nc.vector.tensor_scalar(rank[:], rank[:], -1.0, None, ALU.add))
                nc.vector.tensor_tensor(sc[:], sc[:], rank[:], ALU.add).then_inc(s["g"], 1)

            @block.scalar
            def _(act):
                act.wait_ge(s["lg"], 1)
                nc.scalar.activation(sc[:], w.logits[:], ACT.Exp).then_inc(s["ex"], 1)
                act.wait_ge(s["gt"], 1)
                nc.scalar.activation(gT[:].rearrange("p a t -> p (a t)"), p_g[:, 0:256], ACT.Copy).then_inc(s["gts"], 1)

            @block.tensor
            def _(pe):
                pe.wait_ge(s["g"], 1)
                for i in range(2):
                    last = nc.tensor.transpose(p_g[:, i * P:(i + 1) * P],
                                               sc[:, 16 * i:16 * i + 16, :].rearrange("p t e -> p (t e)"), k.const("ident"))
                last.then_inc(s["gt"], 1)

            @block.sync
            def _(sp):
                sp.wait_ge(s["gts"], 1)
                for i in range(2):
                    for j in range(16):
                        sp.dma_start(k.gates[:, (16 * i + j) * P:(16 * i + j + 1) * P], gT[8 * j:8 * j + 8, i, :]).then_inc(s["gd"], 16)
                sp.wait_ge(s["gd"], 16 * 32)

    with ExitStack() as ctx:
        R = range(2)
        NGB = 4
        gb = [k.sb(ctx, f"f0_gb{i}", [P, BLK]) for i in range(NGB)]
        xs = [k.sb(ctx, f"f0_xs{i}", [P, BLK]) for i in R]
        hh = [k.sb(ctx, f"f0_hh{i}", [P, BLK]) for i in R]
        x3 = [k.sb(ctx, f"f0_x3{i}", [P, BLK]) for i in R]
        xm = [k.sb(ctx, f"f0_xm{i}", [P, BLK]) for i in R]
        pr = [k.sb(ctx, f"f0_pr{i}", [P, BLK]) for i in R]
        acc = k.sb(ctx, "f0_acc", [P, BLK])
        p_h = [k.ps(ctx, f"ps_f0h{i}", [P, 512]) for i in R]
        p_3 = [k.ps(ctx, f"ps_f03{i}", [P, 512]) for i in R]
        p_2 = [k.ps(ctx, f"ps_f02{i}", [P, 512]) for i in R]
        p_z = k.ps(ctx, "ps_f0z", [P, 512])
        p_t = k.ps(ctx, "ps_f0t", [P, 512])
        names = ("gb", "xs", "h", "hs", "x3", "x3s", "sm", "x2", "pr", "acc", "z", "zc", "tr", "x", "chain")
        s = {n: k.sem("f0b_" + n) for n in names}
        gbs = [k.sem(f"f0b_gate{i}") for i in range(NGB)]
        N = E + 2
        with nc.Block("experts0") as block:

            @block.sync
            def _(sp):
                for n, c in (("sm", 1), ("x3s", 2), ("hs", 2), ("pr", 2), ("acc", 2), ("x", 1), ("x2", 2), ("tr", 1)):
                    sp.sem_inc(s[n], c)
                sp.sem_inc(s["gb"], NGB)
                with sp.Fori(0, NB) as it:
                    for e in range(E):
                        sp.wait_ge(s["gb"], it * E + e + 1)
                        sp.dma_start(gb[e % NGB][:], k.gates[e:e + 1, bass.ds(it * BLK, BLK)].broadcast_to([P, BLK])).then_inc(gbs[e % NGB], 16)

            @block.vector
            def _(dve):
                def scale(it, e):
                    dve.wait_ge(gbs[e % NGB], it * (16 * (E // NGB)) + 16 * (e // NGB + 1))
                    dve.wait_ge(s["x3"], it * N + e + 1)
                    nc.vector.scalar_tensor_tensor(out=xs[e % 2][:], in0=gb[e % NGB][:], scalar=0.0,
                                                   in1=k.xnT[:, bass.ds(it * BLK, BLK)], op0=ALU.max, op1=ALU.mult).then_inc(s["xs"], 1)

                with dve.Fori(0, NB) as it:
                    scale(it, 0)
                    for e in range(E):
                        if e + 1 < E:
                            scale(it, e + 1)
                        dve.wait_ge(s["x3s"], it * E + e + 3)
                        dve.wait_ge(s["pr"], it * E + e + 1)
                        nc.vector.scalar_tensor_tensor(out=xm[e % 2][:], in0=gb[e % NGB][:], scalar=0.0, in1=x3[e % 2][:],
                                                       op0=ALU.is_ge, op1=ALU.mult).then_inc(s["gb"], 1)
                        dve.wait_ge(s["gb"], it * E + e + NGB + 1)
                        dve.wait_ge(s["x2"], it * E + e + 3)
                        dve.wait_ge(s["acc"], it * (E + 1) + max(e + 1, 2))
                        nc.vector.scalar_tensor_tensor(out=pr[e % 2][:], in0=p_2[e % 2][:], scalar=w.bias[:, E + e:E + e + 1],
                                                       in1=xm[e % 2][:], op0=ALU.add, op1=ALU.mult).then_inc(s["pr"], 1)
                    for c in range(2):
                        dve.wait_ge(s["hs"], it * N + E + c + 3)
                        dve.wait_ge(s["x3"], it * N + E + c + 3)
                        dve.wait_ge(s["pr"], it * E + E + c + 1)
                        nc.vector.tensor_tensor(xm[c][:], hh[c][:], p_3[c][:], ALU.mult).then_inc(s["sm"], 1)
                    dve.wait_ge(s["tr"], it + 2)
                    xv = k.x[:, bass.ds(it * U, U), :].rearrange("p a d -> p (a d)")
                    nc.vector.tensor_tensor(xv, xv, p_t[:], ALU.add).then_inc(s["x"], 1)

            @block.gpsimd
            def _(pool):
                with pool.Fori(0, NB) as it:
                    pool.wait_ge(s["tr"], it + 1)
                    pool.wait_ge(s["pr"], it * E + 4)
                    nc.gpsimd.tensor_tensor(acc[:], pr[0][:], pr[1][:], ALU.add).then_inc(s["acc"], 2)
                    for e in range(2, E):
                        pool.wait_ge(s["pr"], it * E + e + 3)
                        pool.wait_ge(s["acc"], it * (E + 1) + e + 2)
                        nc.gpsimd.tensor_tensor(acc[:], acc[:], pr[e % 2][:], ALU.add).then_inc(s["acc"], 1)
                    pool.wait_ge(s["zc"], it + 1)
                    pool.wait_ge(s["acc"], it * (E + 1) + E + 2)
                    nc.gpsimd.tensor_tensor(acc[:], acc[:], pr[0][:], ALU.add).then_inc(s["acc"], 1)

            @block.scalar
            def _(act):
                with act.Fori(0, NB) as it:
                    for n in range(N):
                        sl = n % 2
                        act.wait_ge(s["h"], it * N + n + 1)
                        if n >= 2:
                            act.wait_ge(s["x2"], it * E + n + 1)
                        else:
                            act.wait_ge(s["sm"], it * 2 + 1)
                        if n < E:
                            nc.scalar.activation(hh[sl][:], p_h[sl][:], ACT.Silu, bias=w.bias[:, n:n + 1]).then_inc(s["hs"], 1)
                            act.wait_ge(s["x3"], it * N + n + 3)
                            act.wait_ge(s["gb"], it * E + n + 3)
                            nc.scalar.activation(x3[sl][:], p_3[sl][:], ACT.Identity, bias=w.bias[:, 2 * E + n:2 * E + n + 1]).then_inc(s["x3s"], 1)
                        else:
                            nc.scalar.activation(hh[sl][:], p_h[sl][:], ACT.Silu).then_inc(s["hs"], 1)
                    act.wait_ge(s["z"], it + 1)
                    act.wait_ge(s["acc"], it * (E + 1) + E + 1)
                    nc.scalar.activation(pr[0][:], p_z[:], ACT.Copy).then_inc(s["zc"], 1)

            @block.tensor
            def _(pe):
                pe.sem_inc(s["x3"], 2)
                with pe.Fori(0, NB) as it:
                    def up(n):
                        sl = n % 2
                        pe.wait_ge(s["hs"], it * N + n + 1)
                        if n < E:
                            pe.wait_ge(s["xs"], it * E + n + 1)
                            rhs = xs[sl][:]
                            a, b = w.expT[:, n, :], w.expT[:, 2 * E + n, :]
                        else:
                            rhs = k.xnT[:, bass.ds(it * BLK, BLK)]
                            a, b = w.shT[:, n - E, :], w.shT[:, 2 + n - E, :]
                        nc.tensor.matmul(p_h[sl][:], a, rhs, start=True, stop=True).then_inc(s["h"], 1)
                        if n >= 2:
                            pe.wait_ge(s["x3s"], it * E + n + 1)
                        else:
                            pe.wait_ge(s["sm"], it * 2 + 1)
                        nc.tensor.matmul(p_3[sl][:], b, rhs, start=True, stop=True).then_inc(s["x3"], 1)

                    up(0)
                    for e in range(E):
                        up(e + 1)
                        pe.wait_ge(s["hs"], it * N + e + 3)
                        pe.wait_ge(s["pr"], it * E + e + 1)
                        nc.tensor.matmul(p_2[e % 2][:], w.expT[:, E + e, :], hh[e % 2][:], start=True, stop=True).then_inc(s["x2"], 1)
                    up(N - 1)
                    for c in range(2):
                        pe.wait_ge(s["sm"], it * 2 + c + 2)
                        last = nc.tensor.matmul(p_z[:], w.shT[:, 4 + c, :], xm[c][:], start=(c == 0), stop=(c == 1))
                    last.then_inc(s["z"], 1)
                    pe.wait_ge(s["acc"], it * (E + 1) + E + 3)
                    pe.wait_ge(s["x"], it + 1)
                    for u in range(U):
                        last = nc.tensor.transpose(p_t[:, u * P:(u + 1) * P], acc[:, u * P:(u + 1) * P], k.const("ident"))
                    last.then_inc(s["tr"], 1)


class Weights0:
    def __init__(self, k, ctx):
        self.expT = k.sb(ctx, "expT", [P, 3 * E, P])
        self.shT = k.sb(ctx, "shT", [P, 6, P])
        self.outT = k.sb(ctx, "outT", [P, P])
        self.proj = k.sb(ctx, "proj0", [P, 392])
        self.bias = k.sb(ctx, "bias0", [P, 3 * E])
        self.map_bias = k.sb(ctx, "map_bias", [P, 2, HD])
        self.logits = k.sb(ctx, "logits0", [P, NT, E])

class Weights1:
    def __init__(self, k, ctx):
        self.proj = k.sb(ctx, "proj1", [P, 3 * D + E + 1])
        self.bias = k.sb(ctx, "bias1", [P, 3 * D])
        self.hd = k.sb(ctx, "hd1", [P, 2, HD])
        self.rhb = k.sb(ctx, "rhb", [P, 1])
        self.outw = k.sb(ctx, "outw1", [P, D])
        self.outb = k.sb(ctx, "outb1", [P, D])
        self.logits = k.sb(ctx, "lg1", [P, NT, E + 1])


def phase_weights1(k, w):
    nc, io = k.nc, k.io
    with ExitStack() as ctx:
        vec = k.sb(ctx, "w1_vec", [P, 4])
        rep = k.sb(ctx, "w1_rep", [P, 2, P])
        raw = k.sb(ctx, "w1_raw", [P, 3 * D])
        p_b = k.ps(ctx, "ps_w1", [P, 512])
        s = {n: k.sem("w1_" + n) for n in ("in", "rep", "mm", "done")}
        names = ("qn_w", "qn_b", "kvn_w", "kvn_b")
        col = lambda v: v.rearrange("(p a) -> p a", a=1)
        with nc.Block("weights1") as block:
            @block.sync
            def _(sp):
                for i, n in enumerate(names):
                    sp.dma_start(vec[:, i:i + 1], col(io["L1_attn_" + n])).then_inc(s["in"], 16)
                sp.dma_start(raw[:, 0:D], io["L1_attn_q_w"]).then_inc(s["in"], 16)
                sp.dma_start(raw[:, D:3 * D], io["L1_attn_kv_w"]).then_inc(s["in"], 16)
                sp.dma_start(w.proj[:, 3 * D:3 * D + E], io["L1_ffn_Wr"]).then_inc(s["in"], 16)
                sp.dma_start(w.proj[:, 3 * D + E:3 * D + E + 1], io["L1_attn_rh_w"]).then_inc(s["in"], 16)
                sp.dma_start(w.bias[:, 0:D], rows_of(io["L1_attn_q_b"], P)).then_inc(s["in"], 16)
                sp.dma_start(w.bias[:, D:3 * D], rows_of(io["L1_attn_kv_b"], P)).then_inc(s["in"], 16)
                sp.dma_start(w.hd[:, 0, :], rows_of(io["L1_attn_ln_w"], P)).then_inc(s["in"], 16)
                sp.dma_start(w.hd[:, 1, :], rows_of(io["L1_attn_ln_b"], P)).then_inc(s["in"], 16)
                sp.dma_start(w.rhb[:], rows_of(io["L1_attn_rh_b"], P)).then_inc(s["in"], 16)
                sp.dma_start(w.outw[:], io["L1_attn_out_w"]).then_inc(s["in"], 16)
                sp.dma_start(w.outb[:], rows_of(io["L1_attn_out_b"], P)).then_inc(s["in"], 16)

            @block.vector
            def _(dve):
                dve.wait_ge(s["in"], 16 * 15)
                for i in range(2):
                    last = nc.vector.tensor_copy(rep[:, i, :], vec[:, 2 * i + 1:2 * i + 2].broadcast_to([P, P]))
                last.then_inc(s["rep"], 1)
                nc.vector.tensor_scalar(w.proj[:, 0:D], raw[:, 0:D], vec[:, 0:1], None, ALU.mult)
                nc.vector.tensor_scalar(w.proj[:, D:3 * D], raw[:, D:3 * D], vec[:, 2:3], None, ALU.mult)
                dve.wait_ge(s["mm"], 1)
                nc.vector.tensor_tensor(w.bias[:], w.bias[:], p_b[:, 0:3 * D], ALU.add).then_inc(s["done"], 1)

            @block.tensor
            def _(pe):
                pe.wait_ge(s["rep"], 1)
                nc.tensor.matmul(p_b[:, 0:D], rep[:, 0, :], raw[:, 0:D], start=True, stop=True)
                nc.tensor.matmul(p_b[:, D:3 * D], rep[:, 1, :], raw[:, D:3 * D], start=True, stop=True).then_inc(s["mm"], 1)


def phase_rotary(k, w):
    nc = k.nc
    G8 = 2 * H
    with ExitStack() as ctx:
        fr = k.sb(ctx, "ro_fr", [P, 2, NT, 4])
        rad = k.sb(ctx, "ro_rad", [P, NT])
        var = k.sb(ctx, "ro_var", [P, NT, G8])
        rv = k.sb(ctx, "ro_rv", [P, NT, G8])
        t1 = k.sb(ctx, "ro_t1", [P, U, 256])
        t2 = k.sb(ctx, "ro_t2", [P, U, 256])
        rot = k.sb(ctx, "ro_rot", [P, U, 256])
        sm = k.sb(ctx, "ro_sm", [P, U * G8])
        s = {n: k.sem("ro_" + n) for n in ("chain", "fr", "t2", "c", "sq", "var", "sd")}
        with nc.Block("rotary") as block:
            @block.vector
            def _(dve):
                step = Steps(dve, s["chain"])
                step(nc.vector.tensor_scalar(rad[:], w.logits[:, :, E], w.rhb[:], 0.01, ALU.add, ALU.mult))
                step(nc.vector.tensor_scalar(rad[:], rad[:], 0.5, 2.0, ALU.max, ALU.min))
                for i, n in enumerate(("cos", "sin")):
                    tab = k.const(n).rearrange("p (t f) -> p t f", f=4).unsqueeze(1).broadcast_to([P, BATCH, TB, 4])
                    r4 = rad[:].rearrange("p (b t) -> p b t", b=BATCH).unsqueeze(3).broadcast_to([P, BATCH, TB, 4])
                    step(nc.vector.tensor_tensor(fr[:, i].rearrange("p (b t) f -> p b t f", b=BATCH), tab, r4, ALU.mult))
                dve.sem_inc(s["fr"], 1)
                with dve.Fori(0, NB) as it:
                    step.loop(it, 6)
                    pairs = lambda a: a.rearrange("p (g f c) -> p g f c", f=4, c=2)
                    for u in range(U):
                        f = fr[:, 0, bass.ds(it * U + u, 1), :].unsqueeze(3).broadcast_to([P, G8, 4, 2])
                        src = pairs(w.qk[:, bass.ds(it * U + u, 1), :].rearrange("p a c -> p (a c)"))
                        last = nc.vector.tensor_tensor(pairs(t1[:, u, :]), src, f, ALU.mult)
                    step(last)
                    dve.wait_ge(s["t2"], it + 1)
                    one = lambda a, c: a[:].rearrange("p u (x c) -> p (u x) c", c=2)[:, :, c]
                    nc.vector.tensor_tensor(one(rot, 0), one(t1, 0), one(t2, 1), ALU.subtract)
                    step(nc.vector.tensor_tensor(one(rot, 1), one(t2, 0), one(t1, 1), ALU.add))
                    rg = rot[:].rearrange("p u (g e) -> p (u g) e", e=HD)
                    step(nc.vector.tensor_reduce(sm[:], rg, axis=AX, op=ALU.add))
                    step(nc.vector.tensor_scalar(sm[:], sm[:], 1.0 / HD, None, ALU.mult))
                    nc.vector.tensor_tensor(w.qk[:, bass.ds(it * U, U), :].rearrange("p a (g e) -> p (a g) e", e=HD), rg,
                                            sm[:].unsqueeze(2).broadcast_to([P, U * G8, HD]), ALU.subtract).then_inc(s["c"], 1)
                    dve.wait_ge(s["sq"], it + 1)
                    step(nc.vector.tensor_reduce(var[:, bass.ds(it * U, U), :].rearrange("p a g -> p (a g)"),
                                                 t1[:].rearrange("p u (g e) -> p (u g) e", e=HD), axis=AX, op=ALU.add))
                    step(nc.vector.memset(sm[:, 0:1], 0.0))
                step.end(NB)
                dve.sem_inc(s["var"], 1)
                dve.wait_ge(s["sd"], 1)
                step(nc.vector.reciprocal(rv[:], var[:]))

            @block.gpsimd
            def _(pool):
                pool.wait_ge(s["fr"], 1)
                with pool.Fori(0, NB) as it:
                    pool.wait_ge(s["c"], it + 1)
                    pairs = lambda a: a.rearrange("p (g f c) -> p g f c", f=4, c=2)
                    for u in range(U):
                        f = fr[:, 1, bass.ds(it * U + u, 1), :].unsqueeze(3).broadcast_to([P, G8, 4, 2])
                        src = pairs(w.qk[:, bass.ds(it * U + u, 1), :].rearrange("p a c -> p (a c)"))
                        last = nc.gpsimd.tensor_tensor(pairs(t2[:, u, :]), src, f, ALU.mult)
                    last.then_inc(s["t2"], 1)

            @block.scalar
            def _(act):
                act.sem_inc(s["c"], 1)
                with act.Fori(0, NB) as it:
                    act.wait_ge(s["c"], it + 2)
                    nc.scalar.activation(t1[:], w.qk[:, bass.ds(it * U, U), :], ACT.Square).then_inc(s["sq"], 1)
                act.wait_ge(s["var"], 1)
                nc.scalar.activation(var[:], var[:], ACT.Sqrt, scale=1.0 / HD, bias=k.eps[:]).then_inc(s["sd"], 1)

        nb = k.sb(ctx, "ro_nb", [P, U, 256])
        sq = k.sb(ctx, "ro_sqn", [P, U, 256])
        part = [[k.sb(ctx, f"ro_part{i}{j}", [P, BLK], BF16) for j in range(PARTS)] for i in range(2)]
        rest = [k.sb(ctx, f"ro_rest{i}", [P, BLK]) for i in range(2)]
        n2 = k.sb(ctx, "ro_n2", [P, NT, G8])
        mx = k.sb(ctx, "ro_mx", [P, 2])
        mall = k.sb(ctx, "ro_mall", [P, 2])
        p_t = [k.ps(ctx, f"ps_ro{i}", [P, 512]) for i in range(2)]
        s = {n: k.sem("rp_" + n) for n in ("chain", "n", "sq", "tr", "p1", "r1", "p2", "p3", "out0", "out1", "n2", "nrm", "mx", "all")}
        with nc.Block("parts") as block:
            @block.vector
            def _(dve):
                step = Steps(dve, s["chain"])
                with dve.Fori(0, NB) as it:
                    step.loop(it, 3)
                    wide = lambda a: a.rearrange("p u (g e) -> p (u g) e", e=HD)
                    row = lambda i: w.hd[:, i, :].unsqueeze(1).broadcast_to([P, U * G8, HD])
                    dve.wait_ge(s["tr"], it + 1)
                    dve.wait_ge(s["sq"], it + 1)
                    step(nc.vector.tensor_tensor(wide(nb[:]), wide(w.qk[:, bass.ds(it * U, U), :]),
                                                 rv[:, bass.ds(it * U, U), :].rearrange("p a g -> p (a g)").unsqueeze(2).broadcast_to([P, U * G8, HD]),
                                                 ALU.mult))
                    step(nc.vector.tensor_tensor(wide(nb[:]), wide(nb[:]), row(0), ALU.mult))
                    nc.vector.tensor_tensor(wide(nb[:]), wide(nb[:]), row(1), ALU.add).then_inc(s["n"], 1)
                    dve.wait_ge(s["sq"], it + 2)
                    step(nc.vector.tensor_reduce(n2[:, bass.ds(it * U, U), :].rearrange("p a g -> p (a g)"), wide(sq[:]), axis=AX, op=ALU.add))
                    for i in range(2):
                        dve.wait_ge(s["p1"], it * 2 + i + 1)
                        nc.vector.tensor_tensor(rest[i][:], p_t[i][:], part[i][0][:], ALU.subtract).then_inc(s["r1"], 1)
                        dve.wait_ge(s["p2"], it * 2 + i + 1)
                        nc.vector.tensor_tensor(part[i][2][:], rest[i][:], part[i][1][:], ALU.subtract).then_inc(s["p3"], 1)
                step.end(NB)
                dve.sem_inc(s["n2"], 1)
                dve.wait_ge(s["nrm"], 1)
                for i in range(2):
                    last = nc.vector.tensor_reduce(mx[:, i:i + 1], n2[:, :, i * H:(i + 1) * H], axis=mybir.AxisListType.XY, op=ALU.max)
                last.then_inc(s["mx"], 1)
                dve.wait_ge(s["all"], 1)
                step(nc.vector.tensor_scalar(k.rowmax[:], n2[:, :, 0:H], mall[:, 1:2], None, ALU.mult))
                step(nc.vector.tensor_tensor(mx[:, 0:1], mall[:, 0:1], mall[:, 1:2], ALU.mult))
                step(nc.vector.tensor_scalar(mx[:, 1:2], mx[:, 0:1], MAX_GAP / (2 * HD ** -0.5), None, ALU.is_gt))
                step(nc.vector.tensor_copy(k.flag[:], mx[:, 1:2]))

            @block.gpsimd
            def _(pool):
                pool.sem_inc(s["sq"], 1)
                pool.wait_ge(s["mx"], 1)
                nc.gpsimd.partition_all_reduce(mall[:], mx[:], P, bass.bass_isa.ReduceOp.max).then_inc(s["all"], 1)

            @block.scalar
            def _(act):
                with act.Fori(0, NB) as it:
                    act.wait_ge(s["n"], it + 1)
                    nc.scalar.activation(sq[:], nb[:], ACT.Square).then_inc(s["sq"], 1)
                    for i in range(2):
                        act.wait_ge(s["tr"], it + 2)
                        act.wait_ge(s["out" + str(i)], (it + 1) * 16 * PARTS)
                        nc.scalar.activation(part[i][0][:], p_t[i][:], ACT.Copy).then_inc(s["p1"], 1)
                        act.wait_ge(s["r1"], it * 2 + i + 1)
                        nc.scalar.activation(part[i][1][:], rest[i][:], ACT.Copy).then_inc(s["p2"], 1)
                act.wait_ge(s["n2"], 1)
                nc.scalar.activation(n2[:], n2[:], ACT.Sqrt).then_inc(s["nrm"], 1)

            @block.tensor
            def _(pe):
                pe.sem_inc(s["tr"], 1)
                pe.sem_inc(s["p3"], 2)
                with pe.Fori(0, NB) as it:
                    pe.wait_ge(s["n"], it + 1)
                    pe.wait_ge(s["p3"], it * 2 + 2)
                    for i in range(2):
                        for u in range(U):
                            last = nc.tensor.transpose(p_t[i][:, u * P:(u + 1) * P], nb[:, u, i * P:(i + 1) * P], k.const("ident"))
                    last.then_inc(s["tr"], 1)

            @block.sync
            def _(sp):
                for i in range(2):
                    sp.sem_inc(s["out" + str(i)], 16 * PARTS)
                with sp.Fori(0, NB) as it:
                    for i in range(2):
                        sp.wait_ge(s["p3"], it * 2 + i + 3)
                        for j in range(PARTS):
                            dst = k.parts[i, j, :, bass.ds(it * BLK, BLK)]
                            sp.dma_start(dst, part[i][j][:]).then_inc(s["out" + str(i)], 16)
                for i in range(2):
                    sp.wait_ge(s["out" + str(i)], (NB + 1) * 16 * PARTS)


def load_split(nc, sp, k, dst, side, b, g, sem):
    src = k.parts[side, :, bass.ds(g * (G * HD), G * HD), bass.ds(b * SEQ, SEQ)]
    for i in range(PARTS):
        for j in range(PARTS):
            row = (i * PARTS + j) * HD
            sp.dma_start(dst[row:row + HD, :, :], src[(i, j)[side]].rearrange("(g d) t -> d g t", d=HD)).then_inc(sem, 16)


def phase_maxima(k):
    nc = k.nc
    with ExitStack() as ctx:
        qs = k.sb(ctx, "mx_qs", [SR, G, SEQ], BF16)
        ks = k.sb(ctx, "mx_ks", [SR, G, SEQ], BF16)
        top = k.sb(ctx, "mx_top", [P, TB, G])
        p_s = [k.ps(ctx, f"ps_mx{i}", [P, 2, 512]) for i in range(4)]
        s = {n: k.sem("mx_" + n) for n in ("in", "mm", "red", "kept")}
        UN = G * TB

        def taken(eng):
            return eng.If(eng.value_load(k.flag[0:1, 0:1], min_val=0, max_val=1) != 0)

        with nc.Block("maxima") as block:
            @block.sync
            def _(sp):
                with taken(sp):
                    with sp.Fori(0, BATCH) as b:
                        with sp.Fori(0, NG) as g:
                            sp.wait_ge(s["kept"], b * NG + g + 1)
                            load_split(nc, sp, k, qs, 0, b, g, s["in"])
                            load_split(nc, sp, k, ks, 1, b, g, s["in"])

            @block.tensor
            def _(pe):
                with taken(pe):
                    with pe.Fori(0, BATCH * NG) as it:
                        pe.wait_ge(s["in"], (it + 1) * (2 * PARTS * PARTS * 16))
                        for n in range(UN):
                            hh, t = n // TB, n % TB
                            pe.wait_ge(s["red"], it * UN + n + 1)
                            for half in range(2):
                                last = nc.tensor.matmul(p_s[n % 4][:, half, :], qs[:, hh, t * P:(t + 1) * P],
                                                        ks[:, hh, half * 512:half * 512 + 512], start=True, stop=True)
                            last.then_inc(s["mm"], 1)

            @block.vector
            def _(dve):
                with taken(dve):
                    dve.sem_inc(s["kept"], 1)
                    dve.sem_inc(s["red"], 4)
                    with dve.Fori(0, BATCH) as b:
                        with dve.Fori(0, NG) as g:
                            for n in range(UN):
                                hh, t = n // TB, n % TB
                                dve.wait_ge(s["mm"], (b * NG + g) * UN + n + 1)
                                nc.vector.tensor_reduce(top[:, t, hh:hh + 1], p_s[n % 4][:].rearrange("p a c -> p (a c)"),
                                                        axis=AX, op=ALU.max).then_inc(s["red"], 1)
                            dve.wait_ge(s["red"], (b * NG + g + 1) * UN + 4)
                            nc.vector.tensor_copy(k.rowmax[:, bass.ds(b * TB, TB), bass.ds(g * G, G)], top[:]).then_inc(s["kept"], 1)
                            dve.wait_ge(s["kept"], b * NG + g + 2)


def phase_rows(k, ks_ones):
    nc = k.nc
    with ExitStack() as ctx:
        mT = k.sb(ctx, "rw_mT", [P, 4, P], BF16)
        ones = k.sb(ctx, "rw_ones", [1, G * SEQ], BF16)
        p_m = k.ps(ctx, "ps_rw", [P, 512])
        s = {n: k.sem("rw_" + n) for n in ("ones", "tr", "cp", "out")}
        with nc.Block("rows") as block:
            @block.vector
            def _(dve):
                nc.vector.memset(ones[:], 1.0).then_inc(s["ones"], 1)

            @block.tensor
            def _(pe):
                for i in range(4):
                    last = nc.tensor.transpose(p_m[:, i * P:(i + 1) * P],
                                               k.rowmax[:, i * TB:(i + 1) * TB, :].rearrange("p t h -> p (t h)"), k.const("ident"))
                last.then_inc(s["tr"], 1)

            @block.scalar
            def _(act):
                act.wait_ge(s["tr"], 1)
                nc.scalar.activation(mT[:].rearrange("p a t -> p (a t)"), p_m[:], ACT.Copy, scale=-1.0).then_inc(s["cp"], 1)

            @block.sync
            def _(sp):
                sp.wait_ge(s["cp"], 1)
                sp.dma_start(k.rows, mT[:]).then_inc(s["out"], 16)
                sp.wait_ge(s["ones"], 1)
                for ks in ks_ones:
                    sp.dma_start(ks[SR:SR + 1, :, :].rearrange("p g t -> p (g t)"), ones[:]).then_inc(s["out"], 16)
                sp.wait_ge(s["out"], 16 * (1 + len(ks_ones)))


def phase_attention(k, w, ab):
    nc = k.nc
    QH, KB = 2, TB
    RUNS = 2 * QH
    UN = RUNS * KB * 2
    slot_of = [n % 3 for n in range(UN - 1)] + [1]
    NP = 4
    CREDIT = UN // 2
    with ExitStack() as ctx:
        qs = [k.sb(ctx, f"at_qs{i}", [SR + 1, G, SEQ], BF16) for i in range(2)]
        ks = [k.sb(ctx, f"at_ks{i}", [SR + 1, G, SEQ], BF16) for i in range(2)]
        phase_rows(k, ks)
        vs = [k.sb(ctx, f"at_vs{i}", [P, TB, G, HD + 1]) for i in range(2)]
        pp = [k.sb(ctx, f"at_pp{i}", [P, 2, 512]) for i in range(NP)]
        oT = [k.sb(ctx, f"at_oT{i}", [P, 512]) for i in range(2)]
        den = k.sb(ctx, "at_den", [P, 16])
        p_s = [k.ps(ctx, f"ps_at{i}", [P, 2, 512]) for i in range(3)]
        p_o = [k.ps(ctx, f"ps_ato{i}", [P, 512]) for i in range(2)]
        s = {n: k.sem("at_" + n) for n in ("in0", "in1", "v", "qk", "exp", "pv", "ev", "tr", "den", "y", "zero")}
        with nc.Block("attention") as block:
            @block.sync
            def _(sp):
                with sp.Fori(0, BATCH) as b:
                    with sp.Fori(0, NG // 2) as gp:
                        for i in range(2):
                            sp.wait_ge(s["pv"], (b * (NG // 2) + gp) * (UN // 2) + (UN // 4) * (i + 1) - UN // 2 + CREDIT)
                            load_split(nc, sp, k, qs[i], 0, b, gp * 2 + i, s[f"in{i}"])
                            load_split(nc, sp, k, ks[i], 1, b, gp * 2 + i, s[f"in{i}"])
                            heads = k.rows.rearrange("(t h) b c -> h b t c", h=H)[bass.ds(gp * (2 * G) + i * G, G), bass.ds(b, 1)]
                            sp.dma_start(qs[i][SR:SR + 1, :, :].rearrange("p g (t c) -> p g t c", c=P),
                                         heads.rearrange("g b t c -> b g t c")).then_inc(s[f"in{i}"], 16)

            @block.gpsimd
            def _(pool):
                with pool.Fori(0, BATCH) as b:
                    with pool.Fori(0, NG // 2) as gp:
                        for i in range(2):
                            pool.wait_ge(s["pv"], (b * (NG // 2) + gp) * (UN // 2) + (UN // 4) * (i + 1) - UN // 2 + CREDIT)
                            nc.gpsimd.tensor_copy(vs[i][:], w.v1[:, bass.ds(b * TB, TB), bass.ds(gp * (2 * G) + i * G, G), :]).then_inc(s["v"], 1)

            @block.tensor
            def _(pe):
                pe.wait_ge(s["zero"], 1)

                def scores(it, n):
                    r, kb, pair = n // (KB * 2), n // 2 % KB, n % 2
                    i, qh, sl = r // QH, r % QH, slot_of[n]
                    if n % (UN // 2) == 0:
                        pe.wait_ge(s[f"in{i}"], (it + 1) * (16 * (2 * PARTS * PARTS + 1)))
                    before = max([m for m in range(n) if slot_of[m] == sl], default=None)
                    if before is None:
                        before = max(m for m in range(UN) if slot_of[m] == sl) - UN
                    pe.wait_ge(s["exp"], it * UN + before + 1 + UN)
                    for a in range(2):
                        hh = pair * 2 + a
                        last = nc.tensor.matmul(p_s[sl][:, a, :], ks[i][:, hh, kb * P:(kb + 1) * P],
                                                qs[i][:, hh, qh * 512:qh * 512 + 512], start=True, stop=True)
                    last.then_inc(s["qk"], 1)

                def turn(it, r):
                    pe.wait_ge(s["ev"], it * RUNS + r + 3)
                    for u in range(U):
                        last = nc.tensor.transpose(p_o[r % 2][:, u * P:(u + 1) * P], oT[r % 2][:, u * P:(u + 1) * P], k.const("ident"))
                    last.then_inc(s["tr"], 1)

                def body(it, more):
                    for m in range(UN // 2):
                        for n in (2 * m + 2, 2 * m + 3):
                            if n < UN:
                                scores(it, n)
                            elif more:
                                scores(it + 1, n - UN)
                        r, kb = m // KB, m % KB
                        i = r // QH
                        if kb == 0:
                            pe.wait_ge(s["y"], it * RUNS + r + 1)
                            if r % QH == 0:
                                pe.wait_ge(s["v"], it * 2 + i + 1)
                        pe.wait_ge(s["exp"], it * UN + 2 * m + 2 + UN)
                        for hh in range(G):
                            last = nc.tensor.matmul(p_o[r % 2][32 * hh:32 * hh + HD + 1, :], vs[i][:, kb, hh, :],
                                                    pp[(2 * m + hh // 2) % NP][:, hh % 2, :], start=(kb == 0), stop=(kb == KB - 1),
                                                    tile_position=(0, 32 * hh), skip_group_check=True)
                        last.then_inc(s["pv"], 1)
                        if kb == 0 and r > 0:
                            turn(it, r - 1)
                    turn(it, RUNS - 1)

                BODIES = BATCH * NG // 2
                for n in range(2):
                    scores(0, n)
                with pe.Fori(0, BODIES - 1) as it:
                    body(it, True)
                body(BODIES - 1, False)

            @block.scalar
            def _(act):
                act.sem_inc(s["exp"], UN)
                act.sem_inc(s["pv"], CREDIT)
                act.sem_inc(s["tr"], 2)
                with act.Fori(0, BATCH * NG // 2) as it:
                    for n in range(UN):
                        act.wait_ge(s["qk"], it * UN + n + 1)
                        act.wait_ge(s["pv"], it * (UN // 2) + n // 2 - 1 + CREDIT)
                        nc.scalar.activation(pp[n % NP][:], p_s[slot_of[n]][:], ACT.Exp, scale=HD ** -0.5).then_inc(s["exp"], 1)

            @block.vector
            def _(dve):
                nc.vector.memset(p_o[0][:], 0.0)
                nc.vector.memset(p_o[1][:], 0.0).then_inc(s["zero"], 1)
                dve.sem_inc(s["ev"], 2)
                dve.sem_inc(s["y"], 2)
                with dve.Fori(0, BATCH * NG // 2) as it:
                    for r in range(RUNS):
                        i, qh = r // QH, r % QH
                        dve.wait_ge(s["pv"], it * (UN // 2) + (r + 1) * KB + CREDIT)
                        dve.wait_ge(s["tr"], it * RUNS + r + 1)
                        nc.vector.tensor_copy(oT[r % 2][:], p_o[r % 2][:]).then_inc(s["ev"], 1)
                        dve.wait_ge(s["tr"], it * RUNS + r + 3)
                        o = p_o[r % 2][:].rearrange("p (x c) -> p x c", c=32)
                        nc.vector.reciprocal(den[:], o[:, :, HD]).then_inc(s["den"], 1)
                        dve.wait_ge(s["den"], it * RUNS + r + 1)
                        nc.vector.tensor_tensor(ab[:, bass.ds((it * 2 + i) * TB + qh * U, U), :].rearrange("p t (h e) -> p (t h) e", e=HD),
                                                o[:, :, 0:HD], den[:].unsqueeze(2).broadcast_to([P, 16, HD]), ALU.mult).then_inc(s["y"], 1)
                        dve.wait_ge(s["y"], it * RUNS + r + 3)


def phase_out1(k, w, ab):
    nc = k.nc
    with ExitStack() as ctx:
        a = [k.sb(ctx, f"o1_a{i}", [P, U, D]) for i in range(2)]
        aT = k.sb(ctx, "o1_aT", [P, 512])
        p_a = k.ps(ctx, "ps_o1a", [P, 512])
        p_r = k.ps(ctx, "ps_o1r", [P, 512])
        s = {n: k.sem("o1_" + n) for n in ("a", "tr", "aT", "mm", "x")}
        with nc.Block("out1") as block:
            @block.gpsimd
            def _(pool):
                pool.sem_inc(s["tr"], 2)
                pool.sem_inc(s["aT"], 1)
                pool.sem_inc(s["x"], 1)
                with pool.Fori(0, BATCH) as b:
                    for i in range(2):
                        pool.wait_ge(s["tr"], b * 2 + i + 1)
                        for u in range(U):
                            last = nc.gpsimd.tensor_copy(a[i][:, u, :].rearrange("p (g c) -> p g c", g=NG),
                                                         ab[:].rearrange("p (bg t) c -> p bg t c", t=TB)[:, bass.ds(b * NG, NG), i * U + u, :])
                        last.then_inc(s["a"], 1)

            @block.tensor
            def _(pe):
                with pe.Fori(0, BATCH) as b:
                    for i in range(2):
                        pe.wait_ge(s["a"], b * 2 + i + 1)
                        pe.wait_ge(s["aT"], b * 2 + i + 1)
                        for u in range(U):
                            last = nc.tensor.transpose(p_a[:, u * P:(u + 1) * P], a[i][:, u, :], k.const("ident"))
                        last.then_inc(s["tr"], 1)
                        pe.wait_ge(s["aT"], b * 2 + i + 2)
                        pe.wait_ge(s["x"], b * 2 + i + 1)
                        for u in range(U):
                            last = nc.tensor.matmul(p_r[:, u * P:(u + 1) * P], aT[:, u * P:(u + 1) * P], w.outw[:], start=True, stop=True)
                        last.then_inc(s["mm"], 1)

            @block.scalar
            def _(act):
                with act.Fori(0, BATCH) as b:
                    for i in range(2):
                        act.wait_ge(s["tr"], b * 2 + i + 3)
                        act.wait_ge(s["x"], b * 2 + i + 1)
                        nc.scalar.activation(aT[:], p_a[:], ACT.Copy).then_inc(s["aT"], 1)

            @block.vector
            def _(dve):
                chain = k.sem("o1_chain")
                with dve.Fori(0, BATCH) as b:
                    for i in range(2):
                        x = k.x[:, bass.ds(b * TB + i * U, U), :]
                        nc.vector.tensor_tensor(x, x, w.outb[:].unsqueeze(1).broadcast_to([P, U, D]), ALU.add).then_inc(chain, 1)
                        dve.wait_ge(chain, b * 2 + i + 1)
                        dve.wait_ge(s["mm"], b * 2 + i + 1)
                        nc.vector.tensor_tensor(x, x, p_r[:].rearrange("p (u d) -> p u d", u=U), ALU.add).then_inc(s["x"], 1)


def phase_choose1(k, w, gate, s):
    nc = k.nc
    with ExitStack() as ctx:
        sc = k.sb(ctx, "c1_sc", [P, NT, E])
        sp2 = k.sb(ctx, "c1_sp", [P, 2, NT // 2, E])
        r1 = k.sb(ctx, "c1_r1", [P, NT])
        sT = k.sb(ctx, "c1_sT", [P, 2 * P])
        junk = k.sb(ctx, "c1_junk", [P, 2 * P])
        gtm = k.sb(ctx, "c1_gt", [P, 2 * P])
        eqm = k.sb(ctx, "c1_eq", [P, 2 * P])
        one = k.sb(ctx, "c1_one", [P, 2 * P])
        cur, cand, bit, ok = (k.sb(ctx, "c1_" + n, [P, 1], I32) for n in ("cur", "cand", "bit", "ok"))
        cnt = k.sb(ctx, "c1_cnt", [P, 2])
        off = k.sb(ctx, "c1_off", [P, 3])
        p_s = k.ps(ctx, "ps_c1s", [P, 512])
        p_c = k.ps(ctx, "ps_c1c", [P, 512])
        NBITS = 30
        with nc.Block("choose1") as block:
            @block.vector
            def _(dve):
                step = Steps(dve, s["chain"])
                wide = lambda a: a[:].unsqueeze(2).broadcast_to([P, NT, E])
                lg = w.logits[:, :, 0:E]
                nc.vector.memset(one[:], 1.0)
                nc.vector.memset(cur[:], 0)
                nc.vector.memset(bit[:], 1 << (NBITS - 1))
                step(nc.vector.tensor_reduce(r1[:], lg, axis=AX, op=ALU.max))
                nc.vector.tensor_tensor(sc[:], lg, wide(r1), ALU.subtract).then_inc(s["lg"], 1)
                dve.wait_ge(s["ex"], 1)
                step(nc.vector.tensor_reduce(r1[:], sc[:], axis=AX, op=ALU.add))
                step(nc.vector.reciprocal(r1[:], r1[:]))
                split = lambda x: x.rearrange("p (i a) e -> p i a e", a=2)
                nc.vector.tensor_tensor(sp2[:].rearrange("p a i e -> p i a e"), split(sc[:]), split(wide(r1)), ALU.mult).then_inc(s["sc"], 1)
                dve.wait_ge(s["sT"], 1)
                with dve.Fori(0, NBITS) as it:
                    step.loop(it, 4)
                    step(nc.vector.tensor_tensor(cand[:], cur[:], bit[:], ALU.bitwise_or))
                    nc.vector.tensor_scalar(junk[:], sT[:], cand[:].bitcast(F32), None, ALU.is_ge, ALU.add,
                                            accum_out=cnt[:, 0:1]).then_inc(s["cnt"], 1)
                    dve.wait_ge(s["tot"], it + 1)
                    step(nc.vector.tensor_scalar(ok[:], p_c[:, 0:1], float(CAP), None, ALU.is_ge))
                    step.mark(nc.vector.tensor_scalar(bit[:], bit[:], 1, None, ALU.logical_shift_right))
                    step(nc.vector.copy_predicated(cur[:], ok[:], cand[:]))
                step.end(NBITS)
                thr = cur[:].bitcast(F32)
                nc.vector.tensor_scalar(gtm[:], sT[:], thr, None, ALU.is_gt, ALU.add, accum_out=cnt[:, 0:1])
                nc.vector.tensor_scalar(eqm[:], sT[:], thr, None, ALU.is_equal, ALU.add, accum_out=cnt[:, 1:2]).then_inc(s["cnt"], 1)
                dve.wait_ge(s["cnt"], NBITS + 1)
                step(nc.vector.tensor_tensor_scan(junk[:], one[:], eqm[:], 0.0, ALU.mult, ALU.add))
                dve.wait_ge(s["tot"], NBITS + 1)
                step(nc.vector.tensor_copy(off[:], p_c[:, 0:3]))
                step(nc.vector.tensor_tensor(off[:, 0:1], off[:, 0:1], off[:, 2:3], ALU.add))
                step(nc.vector.tensor_scalar(junk[:], junk[:], off[:, 0:1], float(CAP), ALU.add, ALU.is_le))
                step(nc.vector.tensor_tensor(eqm[:], eqm[:], junk[:], ALU.mult))
                step(nc.vector.tensor_tensor(gtm[:], gtm[:], eqm[:], ALU.add))
                nc.vector.tensor_tensor(gate[:], sT[:], gtm[:], ALU.mult).then_inc(s["gate"], 1)

            @block.scalar
            def _(act):
                act.wait_ge(s["lg"], 1)
                nc.scalar.activation(sc[:], sc[:], ACT.Exp).then_inc(s["ex"], 1)
                act.wait_ge(s["tr"], 1)
                nc.scalar.activation(sT[:], p_s[:, 0:256], ACT.Copy).then_inc(s["sT"], 1)

            @block.tensor
            def _(pe):
                pe.wait_ge(s["sc"], 1)
                for half in range(2):
                    src = sp2[:, half].rearrange("p i e -> p (i e)")
                    last = nc.tensor.transpose(p_s[:, half * P:(half + 1) * P], src, k.const("ident"))
                last.then_inc(s["tr"], 1)
                with pe.Fori(0, NBITS) as it:
                    pe.wait_ge(s["cnt"], it + 1)
                    nc.tensor.matmul(p_c[:, 0:1], k.const("same_e"), cnt[:, 0:1], start=True, stop=True).then_inc(s["tot"], 1)
                pe.wait_ge(s["cnt"], NBITS + 1)
                nc.tensor.matmul(p_c[:, 0:2], k.const("same_e"), cnt[:], start=True, stop=True)
                nc.tensor.matmul(p_c[:, 2:3], k.const("before_e"), cnt[:, 1:2], start=True, stop=True).then_inc(s["tot"], 1)


def phase_ffn1(k, w):
    nc, io = k.nc, k.io
    with ExitStack() as ctx:
        gate = k.sb(ctx, "gate1", [P, 2 * P])
        w1 = k.sb(ctx, "w1_1", [P, E, HID1])
        w2 = k.sb(ctx, "w2_1", [P, E, CH1, D])
        b1n = k.sb(ctx, "b1_nat", [E * CH1, P])
        b2n = k.sb(ctx, "b2_nat", [E, P])
        b1 = k.sb(ctx, "b1_1", [P, E * CH1])
        b2 = k.sb(ctx, "b2_1", [P, E])
        s = {n: k.sem("c1_" + n) for n in ("chain", "lg", "ex", "sc", "tr", "sT", "cnt", "tot", "gate")}
        phase_choose1(k, w, gate, s)
        s = {n: k.sem("g1_" + n) for n in ("w", "out", "tr", "b")}
        with ExitStack() as cb:
            p_b = k.ps(cb, "ps_b1", [P, 512])
            with nc.Block("biases1") as block:
                @block.sync
                def _(sp):
                    sp.dma_start(b1n[:], io["L1_ffn_b1"].rearrange("e (c p) -> (e c) p", p=P)).then_inc(s["w"], 16)
                    sp.dma_start(b2n[:], io["L1_ffn_b2"]).then_inc(s["w"], 16)
                    sp.dma_start(w1[:], io["L1_ffn_W1"].rearrange("e d h -> d e h")).then_inc(s["w"], 16)
                    for e in range(E):
                        sp.dma_start(w2[:, e], io["L1_ffn_W2"][e].rearrange("(c p) d -> p c d", p=P)).then_inc(s["w"], 16)
                    for i in range(16):
                        sp.dma_start(k.gates[:, i * 2 * P:(i + 1) * 2 * P], gate[8 * i:8 * i + 8, :]).then_inc(s["out"], 16)
                    sp.wait_ge(s["out"], 16 * 16)
                    sp.wait_ge(s["w"], 16 * (3 + E))

                @block.tensor
                def _(pe):
                    pe.wait_ge(s["w"], 16 * (3 + E))
                    nc.tensor.transpose(p_b[:, 0:E * CH1], b1n[:], k.const("ident")[0:E * CH1, 0:E * CH1])
                    nc.tensor.transpose(p_b[:, 64:64 + E], b2n[:], k.const("ident")[0:E, 0:E]).then_inc(s["tr"], 1)

                @block.vector
                def _(dve):
                    dve.wait_ge(s["tr"], 1)
                    nc.vector.tensor_copy(b1[:], p_b[:, 0:E * CH1])
                    nc.vector.tensor_copy(b2[:], p_b[:, 64:64 + E]).then_inc(s["b"], 1)

        NGB = 4
        gb = [k.sb(ctx, f"g1_gb{i}", [P, BLK]) for i in range(NGB)]
        hs = [k.sb(ctx, f"g1_hs{i}", [P, BLK]) for i in range(CH1)]
        pr = [k.sb(ctx, f"g1_pr{i}", [P, BLK]) for i in range(2)]
        acc = k.sb(ctx, "g1_acc", [P, BLK])
        p_h = [k.ps(ctx, f"ps_g1h{i}", [P, 512]) for i in range(CH1)]
        p_y = [k.ps(ctx, f"ps_g1y{i}", [P, 512]) for i in range(2)]
        p_t = k.ps(ctx, "ps_g1t", [P, 512])
        s = {n: k.sem("g1b_" + n) for n in ("h", "hs", "y", "pr", "acc", "tr", "x")}
        gbs = [k.sem(f"g1b_gate{i}") for i in range(NGB)]
        with nc.Block("experts1") as block:
            @block.sync
            def _(sp):
                sp.sem_inc(s["hs"], CH1)
                sp.sem_inc(s["pr"], NGB)
                sp.sem_inc(s["acc"], 2)
                sp.sem_inc(s["x"], 1)
                sp.sem_inc(s["tr"], 1)
                with sp.Fori(0, NB) as it:
                    for e in range(E):
                        sp.wait_ge(s["pr"], it * E + e + 1)
                        sp.dma_start(gb[e % NGB][:], k.gates[e:e + 1, bass.ds(it * BLK, BLK)].broadcast_to([P, BLK])).then_inc(gbs[e % NGB], 16)

            @block.tensor
            def _(pe):
                pe.sem_inc(s["y"], 1)
                with pe.Fori(0, NB) as it:
                    def up(e, c):
                        pe.wait_ge(s["hs"], (it * E + e) * CH1 + c + 1)
                        nc.tensor.matmul(p_h[c][:], w1[:, e, c * P:(c + 1) * P], k.xnT[:, bass.ds(it * BLK, BLK)],
                                         start=True, stop=True).then_inc(s["h"], 1)
                    for c in range(CH1):
                        up(0, c)
                    for e in range(E):
                        pe.wait_ge(s["pr"], it * E + e + NGB - 1)
                        for c in range(CH1):
                            pe.wait_ge(s["hs"], (it * E + e) * CH1 + c + 1 + CH1)
                            last = nc.tensor.matmul(p_y[e % 2][:], w2[:, e, c, :], hs[c][:], start=(c == 0), stop=(c == CH1 - 1))
                            if c == CH1 - 1:
                                last.then_inc(s["y"], 1)
                            if e + 1 < E:
                                up(e + 1, c)
                    pe.wait_ge(s["acc"], it * E + E + 2)
                    pe.wait_ge(s["x"], it + 1)
                    for u in range(U):
                        last = nc.tensor.transpose(p_t[:, u * P:(u + 1) * P], acc[:, u * P:(u + 1) * P], k.const("ident"))
                    last.then_inc(s["tr"], 1)

            @block.scalar
            def _(act):
                with act.Fori(0, NB) as it:
                    for e in range(E):
                        act.wait_ge(s["y"], it * E + e + 1)
                        for c in range(CH1):
                            act.wait_ge(s["h"], (it * E + e) * CH1 + c + 1)
                            nc.scalar.activation(hs[c][:], p_h[c][:], ACT.Gelu, bias=b1[:, e * CH1 + c:e * CH1 + c + 1]).then_inc(s["hs"], 1)

            @block.vector
            def _(dve):
                with dve.Fori(0, NB) as it:
                    for e in range(E):
                        dve.wait_ge(gbs[e % NGB], it * (16 * (E // NGB)) + 16 * (e // NGB + 1))
                        dve.wait_ge(s["y"], it * E + e + 2)
                        dve.wait_ge(s["acc"], it * E + max(e + 1, 2))
                        nc.vector.scalar_tensor_tensor(out=pr[e % 2][:], in0=p_y[e % 2][:], scalar=b2[:, e:e + 1], in1=gb[e % NGB][:],
                                                       op0=ALU.add, op1=ALU.mult).then_inc(s["pr"], 1)
                    dve.wait_ge(s["tr"], it + 2)
                    xv = k.x[:, bass.ds(it * U, U), :].rearrange("p a d -> p (a d)")
                    nc.vector.tensor_tensor(xv, xv, p_t[:], ALU.add).then_inc(s["x"], 1)

            @block.gpsimd
            def _(pool):
                with pool.Fori(0, NB) as it:
                    pool.wait_ge(s["tr"], it + 1)
                    pool.wait_ge(s["pr"], it * E + 2 + NGB)
                    nc.gpsimd.tensor_tensor(acc[:], pr[0][:], pr[1][:], ALU.add).then_inc(s["acc"], 2)
                    for e in range(2, E):
                        pool.wait_ge(s["pr"], it * E + e + 1 + NGB)
                        pool.wait_ge(s["acc"], it * E + e + 2)
                        nc.gpsimd.tensor_tensor(acc[:], acc[:], pr[e % 2][:], ALU.add).then_inc(s["acc"], 1)


MAX_GAP = 60.0


def build_layer1(k, stop, dbg):
    nc = k.nc
    k.parts = nc.dram_tensor("parts", [2, PARTS, P, TOK], BF16, kind="Internal").ap()
    k.rows = nc.dram_tensor("neg_rowmax", [P, BATCH, P], BF16, kind="Internal").ap()
    with ExitStack() as l1:
        w = Weights1(k, l1)
        w.v1 = k.sb(l1, "v1b", [P, NT, H, HD + 1])
        k.rowmax = k.sb(l1, "rowmax", [P, NT, H])
        k.flag = k.sb(l1, "flag", [P, 1], I32)
        with ExitStack() as lr:
            w.qk = k.sb(lr, "qk1", [P, NT, 2 * D])
            with nc.Block("ones1") as block:
                @block.vector
                def _(dve):
                    nc.vector.memset(w.v1[:, :, :, HD:HD + 1], 1.0)
            phase_weights1(k, w)
            phase_project(k, w, 1)
            if dbg: dbg(nc, k, w, 4)
            if stop > 4:
                phase_rotary(k, w)
            if dbg: dbg(nc, k, w, 5)
        if stop > 5:
            with ExitStack() as la:
                ab = k.sb(la, "heads_out", [P, BATCH * NG * TB, G * HD])
                phase_maxima(k)
                phase_attention(k, w, ab)
                phase_out1(k, w, ab)
        if stop > 6:
            phase_ffn1(k, w)



def build(nc, io, out, stop=99, dbg=None):
    with ExitStack() as ctx:
        k = Kernel(nc, ctx, io)
        k.gates = nc.dram_tensor("gates", [E, TOK], F32, kind="Internal").ap()
        k.x_loaded = [k.sem(f"x_loaded{b}") for b in range(NB)]
        with ExitStack() as l0:
            w = Weights0(k, l0)
            with ExitStack() as la:
                w.v1 = k.sb(la, "v1", [P, NT, H, HD + 1])
                w.qk = k.sb(la, "qk0", [P, NT, 256])
                phase_weights0(k, w)
                phase_project(k, w, 0)
                if dbg: dbg(nc, k, w, 1)
                if stop > 1:
                    phase_linear_attention(k, w)
            if dbg: dbg(nc, k, w, 2)
            if stop > 2:
                phase_ffn0(k, w)
        k.clear_sems()
        if dbg: dbg(nc, k, w, 3)
        if stop > 3:
            build_layer1(k, stop, dbg)
        k.store(out)
        k.clear_sems()


def store(k, out):
    nc = k.nc
    with ExitStack() as ctx:
        stored = k.sem("stored")
        block = ctx.enter_context(nc.Block("store"))
        od = out.rearrange("b (t p) d -> p (b t) d", p=P)

        @block.sync
        def _(sp):
            for b in range(NB):
                sp.dma_start(od[:, U * b:U * b + U, :], k.x[:, U * b:U * b + U, :]).then_inc(stored, 16)
            sp.wait_ge(stored, 16 * NB)

Kernel.store = store


INPUTS = ['L0_attn_x', 'L0_attn_w_qkv', 'L0_attn_wq_map', 'L0_attn_bq_map', 'L0_attn_wk_map', 'L0_attn_bk_map',
          'L0_attn_w_out', 'L0_ffn_gate_w', 'L0_ffn_w1', 'L0_ffn_b1', 'L0_ffn_w2', 'L0_ffn_b2', 'L0_ffn_w3', 'L0_ffn_b3',
          'L0_ffn_sw1', 'L0_ffn_sw2', 'L0_ffn_sw3', 'L1_attn_qn_w', 'L1_attn_qn_b', 'L1_attn_q_w', 'L1_attn_q_b',
          'L1_attn_kvn_w', 'L1_attn_kvn_b', 'L1_attn_kv_w', 'L1_attn_kv_b', 'L1_attn_out_w', 'L1_attn_out_b',
          'L1_attn_ln_w', 'L1_attn_ln_b', 'L1_attn_rh_w', 'L1_attn_rh_b', 'L1_ffn_Wr', 'L1_ffn_W1', 'L1_ffn_b1',
          'L1_ffn_W2', 'L1_ffn_b2']


def kernel(**inputs):
    import concourse.bacc as bacc
    from concourse.bass_utils import run_bass_kernel_spmd

    nc = bacc.Bacc("TRN2", target_bir_lowering=False, num_devices=1)
    given = {n: np.ascontiguousarray(inputs[n]) for n in INPUTS}
    given["consts"] = constants()
    io = {n: nc.dram_tensor(f"in_{n}", a.shape, mybir.dt.from_np(a.dtype), kind="ExternalInput").ap() for n, a in given.items()}
    out = nc.dram_tensor("out", (BATCH, SEQ, D), F32, kind="ExternalOutput").ap()
    build(nc, io, out)
    r = run_bass_kernel_spmd(nc, [{f"in_{n}": a for n, a in given.items()}], core_ids=[0])
    return r.results[0]["out"]
```
